# Optimizing a Trainium2 kernel written in Bass

```python
import numpy as np
import jax
import jax.numpy as jnp

def _softmax(x, axis=-1):
    return jax.nn.softmax(x, axis=axis)

def _gelu(x):
    return jax.nn.gelu(x, approximate=True)

def _silu(x):
    return jax.nn.silu(x)

def _sigmoid(x):
    return jax.nn.sigmoid(x)

def _layernorm(x, axis=-1, eps=1e-05):
    m = jnp.mean(x, axis=axis, keepdims=True)
    v = jnp.var(x, axis=axis, keepdims=True)
    return (x - m) / jnp.sqrt(v + eps)

def _scatter_add(tgt, idx, src, axis=0):
    return tgt.at[idx].add(src)

def _segment_sum(src, seg, n):
    return jax.ops.segment_sum(src, seg, n)
kernel_name = 'mk_flamingo_gated_d2_seqx_r8_0d108c'

def setup_inputs(seed: int=0):
    np.random.seed(seed)
    _w = jnp.asarray

    def _rec_inputs():
        import jax
        import jax.numpy as jnp
        _rk = jax.random.key(seed)
        x = -0.0002928 + 1 * jax.random.normal(jax.random.fold_in(_rk, 1), (8, 128, 128), jnp.float32)
        _lenS = 128 - jax.random.randint(jax.random.fold_in(_rk, 7), (8,), 0, max(1, 128 // 4) + 1, jnp.int32)
        _lenS2 = 77 - jax.random.randint(jax.random.fold_in(_rk, 8), (8,), 0, max(1, 77 // 4) + 1, jnp.int32)
        _ctx_512P = jax.random.normal(jax.random.fold_in(_rk, 11), (8, 16, 64), jnp.float32)
        _ctx_512c = jax.random.dirichlet(jax.random.fold_in(_rk, 511), 0.3 * jnp.ones((16,), jnp.float32), (8, 77))
        _ctx_512t = jnp.einsum('bsk,bkd->bsd', _ctx_512c, _ctx_512P)
        _ctx_512t = _ctx_512t * jax.lax.rsqrt(jnp.mean(jnp.square(_ctx_512t)) + 1e-12) * 0.953939
        ctx_512 = -1.52775e-05 + 0.999936 * (_ctx_512t + 0.3 * jax.random.normal(jax.random.fold_in(_rk, 611), (8, 77, 64), jnp.float32))
        _g = jax.random.normal(jax.random.fold_in(_rk, 9001), (2, 2), jnp.float32)
        _g = jnp.sign(_g) * jnp.maximum(jnp.abs(_g), 1.0) + (_g == 0) * 1.0
        g_xattn = _g[0]
        g_ffn = _g[1]
        return (x, ctx_512, g_xattn, g_ffn)
    x, ctx_512, g_xattn, g_ffn = _rec_inputs()

    def _L0_xattn_setup():
        import jax, jax.numpy as jnp
        import numpy as np
        NUM_HEADS = 16
        HEAD_DIM = 64
        Q_DIM = 128
        KV_DIM = 64
        INNER = NUM_HEADS * HEAD_DIM
        key = jax.random.key(seed)
        ks = jax.random.split(key, 7)
        B, N, M = (32, 128, 256)
        q = jax.random.normal(ks[0], (B, N, Q_DIM), dtype=jnp.float32)
        kv = jax.random.normal(ks[1], (B, M, KV_DIM), dtype=jnp.float32)
        Wq = jax.random.normal(ks[2], (Q_DIM, INNER), dtype=jnp.float32) / np.sqrt(Q_DIM)
        Wk = jax.random.normal(ks[3], (KV_DIM, INNER), dtype=jnp.float32) / np.sqrt(KV_DIM)
        Wv = jax.random.normal(ks[4], (KV_DIM, INNER), dtype=jnp.float32) / np.sqrt(KV_DIM)
        Wo = jax.random.normal(ks[5], (INNER, Q_DIM), dtype=jnp.float32) / np.sqrt(INNER)
        bo = jax.random.normal(ks[6], (Q_DIM,), dtype=jnp.float32) * 0.01
        return {'q': q, 'kv': kv, 'Wq': Wq, 'Wk': Wk, 'Wv': Wv, 'Wo': Wo, 'bo': bo}
    _L0_xattn_all = _L0_xattn_setup()
    _L0_xattn_in = {k: v for k, v in _L0_xattn_all.items() if k in ('Wq', 'Wk', 'Wv', 'Wo', 'bo')}
    del _L0_xattn_all

    def _L0_ffn_setup():
        import jax, jax.numpy as jnp
        import numpy as np
        DIM = 128
        DEPTH = 6
        HEADS = 16
        DIM_HEAD = 64
        WINDOW = 32
        INNER = HEADS * DIM_HEAD
        DIM_INNER = int(DIM * 4 * 2 / 3)
        QK_SCALE = 8.0

        def shift_tokens(t):
            a, s = jnp.split(t, 2, -1)
            s = jnp.pad(s, ((0, 0), (1, 0), (0, 0)))[:, :-1]
            return jnp.concatenate([a, s], -1)

        def l2norm(t):
            return t / jnp.maximum(jnp.linalg.norm(t, axis=-1, keepdims=True), 1e-12)

        def rotate_half(x):
            x1, x2 = jnp.split(x, 2, -1)
            return jnp.concatenate([-x2, x1], -1)

        def rotary_tables(n):
            half = jnp.arange(0, DIM_HEAD, 2, dtype=jnp.float32)
            inv_freq = 1.0 / 10000.0 ** (half / DIM_HEAD)
            t = jnp.arange(n, dtype=jnp.float32)
            freqs = t[:, None] * inv_freq[None, :]
            freqs = jnp.concatenate([freqs, freqs], -1)
            base_scale = (half + 0.4 * DIM_HEAD) / (1.4 * DIM_HEAD)
            power = (t - n // 2) / (WINDOW // 2)
            scale = base_scale[None, :] ** power[:, None]
            scale = jnp.concatenate([scale, scale], -1)
            return (freqs, scale)

        def local_attention(q, k, v):
            b, h, n, d = q.shape
            w = WINDOW
            nw = n // w
            bq = q.reshape(b, h, nw, w, d)
            bk = k.reshape(b, h, nw, w, d)
            bv = v.reshape(b, h, nw, w, d)

            def look(t):
                p = jnp.pad(t, ((0, 0), (0, 0), (1, 0), (0, 0), (0, 0)))
                return jnp.concatenate([p[:, :, :nw], p[:, :, 1:]], axis=3)
            bk2, bv2 = (look(bk), look(bv))
            seq = jnp.arange(n).reshape(nw, w)
            seq_p = jnp.pad(seq, ((1, 0), (0, 0)), constant_values=-1)
            jt = jnp.concatenate([seq_p[:nw], seq_p[1:]], axis=1)
            it = seq[:, :, None]
            jb = jt[:, None, :]
            mask = (it < jb) | (it > jb + w) | (jb == -1)
            sim = jnp.einsum('bhwie,bhwje->bhwij', bq, bk2) * QK_SCALE
            sim = jnp.where(mask, -jnp.finfo(sim.dtype).max, sim)
            attn = jax.nn.softmax(sim, -1)
            out = jnp.einsum('bhwij,bhwje->bhwie', attn, bv2)
            return out.reshape(b, h, n, d)

        def attn_layer(x, Wqkv, qs, ksc, Wo):
            b, n, _ = x.shape
            qkv = x @ Wqkv
            q, k, v = jnp.split(qkv, 3, -1)
            sh = lambda t: t.reshape(b, n, HEADS, DIM_HEAD).transpose(0, 2, 1, 3)
            q, k, v = (sh(q), sh(k), sh(v))
            q = l2norm(q) * qs
            k = l2norm(k) * ksc
            freqs, scale = rotary_tables(n)
            cos, sin = (jnp.cos(freqs), jnp.sin(freqs))
            q = q * cos * scale + rotate_half(q) * sin * scale
            inv = 1.0 / scale
            k = k * cos * inv + rotate_half(k) * sin * inv
            out = local_attention(q, k, v)
            out = out.transpose(0, 2, 1, 3).reshape(b, n, INNER)
            return out @ Wo

        def ffn_layer(x, g, bln, W1, b1, W2, b2):
            mu = x.mean(-1, keepdims=True)
            var = ((x - mu) ** 2).mean(-1, keepdims=True)
            xn = (x - mu) / jnp.sqrt(var + 1e-05) * g + bln
            hg = xn @ W1 + b1
            a, gate = jnp.split(hg, 2, -1)
            return a * jax.nn.gelu(gate, approximate=False) @ W2 + b2
        key = jax.random.key(seed)
        ks = jax.random.split(key, 8)
        B, N = (2, 256)
        init = lambda k, shape: jax.random.normal(k, shape, jnp.float32) * 0.02
        return {'x': jax.random.normal(ks[0], (B, N, DIM), jnp.float32), 'Wqkv': init(ks[1], (DEPTH, DIM, 3 * INNER)), 'q_scale': jnp.ones((DEPTH, DIM_HEAD), jnp.float32), 'k_scale': jnp.ones((DEPTH, DIM_HEAD), jnp.float32), 'Wo': init(ks[2], (DEPTH, INNER, DIM)), 'ln_g': jnp.ones((DEPTH, DIM), jnp.float32), 'ln_b': jnp.zeros((DEPTH, DIM), jnp.float32), 'W1': init(ks[3], (DEPTH, DIM, 2 * DIM_INNER)), 'b1': jnp.zeros((DEPTH, 2 * DIM_INNER), jnp.float32), 'W2': init(ks[4], (DEPTH, DIM_INNER, DIM)), 'b2': jnp.zeros((DEPTH, DIM), jnp.float32)}
    _L0_ffn_all = _L0_ffn_setup()
    _L0_ffn_in = {k: v for k, v in _L0_ffn_all.items() if k in ('Wqkv', 'q_scale', 'k_scale', 'Wo', 'ln_g', 'ln_b', 'W1', 'b1', 'W2', 'b2')}
    del _L0_ffn_all

    def _L1_xattn_setup():
        import jax, jax.numpy as jnp
        import numpy as np
        HEADS = 16
        D_MODEL = 128
        IMG_MODEL = 64
        D_K = D_MODEL // HEADS
        key = jax.random.key(seed)
        ks = jax.random.split(key, 12)
        B, LQ, LKV = (8, 256, 128)
        s_dm = 1.0 / np.sqrt(D_MODEL)
        s_im = 1.0 / np.sqrt(IMG_MODEL)
        return {'q': jax.random.normal(ks[0], (B, LQ, D_MODEL), jnp.float32), 'k': jax.random.normal(ks[1], (B, LKV, IMG_MODEL), jnp.float32), 'v': jax.random.normal(ks[2], (B, LKV, IMG_MODEL), jnp.float32), 'Wq': jax.random.normal(ks[3], (D_MODEL, D_MODEL), jnp.float32) * s_dm, 'bq': jnp.zeros((D_MODEL,), jnp.float32), 'Wk': jax.random.normal(ks[4], (IMG_MODEL, D_MODEL), jnp.float32) * s_im, 'bk': jnp.zeros((D_MODEL,), jnp.float32), 'Wv': jax.random.normal(ks[5], (IMG_MODEL, D_MODEL), jnp.float32) * s_im, 'bv': jnp.zeros((D_MODEL,), jnp.float32), 'Wo': jax.random.normal(ks[6], (D_MODEL, D_MODEL), jnp.float32) * s_dm, 'bo': jnp.zeros((D_MODEL,), jnp.float32)}
    _L1_xattn_all = _L1_xattn_setup()
    _L1_xattn_in = {k: v for k, v in _L1_xattn_all.items() if k in ('Wq', 'bq', 'Wk', 'bk', 'Wv', 'bv', 'Wo', 'bo')}
    del _L1_xattn_all

    def _L1_ffn_setup():
        import jax, jax.numpy as jnp
        import numpy as np
        W_SCALE = 0.02
        TOP_K = 2
        key = jax.random.key(seed)
        ks = jax.random.split(key, 5)
        B, S, H, I, E = (2, 128, 128, 512, 8)
        return {'x': jax.random.normal(ks[0], (B, S, H), dtype=jnp.float32), 'gate': jax.random.normal(ks[1], (H, E), dtype=jnp.float32) * W_SCALE, 'experts_w1': jax.random.normal(ks[2], (E, H, I), dtype=jnp.float32) * W_SCALE, 'experts_w2': jax.random.normal(ks[3], (E, I, H), dtype=jnp.float32) * W_SCALE, 'experts_w3': jax.random.normal(ks[4], (E, H, I), dtype=jnp.float32) * W_SCALE}
    _L1_ffn_all = _L1_ffn_setup()
    _L1_ffn_in = {k: v for k, v in _L1_ffn_all.items() if k in ('gate', 'experts_w1', 'experts_w2', 'experts_w3')}
    del _L1_ffn_all
    return {'x': x, 'ctx_512': ctx_512, 'g_xattn': g_xattn, 'g_ffn': g_ffn, 'L0_xattn_Wq': _L0_xattn_in['Wq'], 'L0_xattn_Wk': _L0_xattn_in['Wk'], 'L0_xattn_Wv': _L0_xattn_in['Wv'], 'L0_xattn_Wo': _L0_xattn_in['Wo'], 'L0_xattn_bo': _L0_xattn_in['bo'], 'L0_ffn_Wqkv': _L0_ffn_in['Wqkv'], 'L0_ffn_q_scale': _L0_ffn_in['q_scale'], 'L0_ffn_k_scale': _L0_ffn_in['k_scale'], 'L0_ffn_Wo': _L0_ffn_in['Wo'], 'L0_ffn_ln_g': _L0_ffn_in['ln_g'], 'L0_ffn_ln_b': _L0_ffn_in['ln_b'], 'L0_ffn_W1': _L0_ffn_in['W1'], 'L0_ffn_b1': _L0_ffn_in['b1'], 'L0_ffn_W2': _L0_ffn_in['W2'], 'L0_ffn_b2': _L0_ffn_in['b2'], 'L1_xattn_Wq': _L1_xattn_in['Wq'], 'L1_xattn_bq': _L1_xattn_in['bq'], 'L1_xattn_Wk': _L1_xattn_in['Wk'], 'L1_xattn_bk': _L1_xattn_in['bk'], 'L1_xattn_Wv': _L1_xattn_in['Wv'], 'L1_xattn_bv': _L1_xattn_in['bv'], 'L1_xattn_Wo': _L1_xattn_in['Wo'], 'L1_xattn_bo': _L1_xattn_in['bo'], 'L1_ffn_gate': _L1_ffn_in['gate'], 'L1_ffn_experts_w1': _L1_ffn_in['experts_w1'], 'L1_ffn_experts_w2': _L1_ffn_in['experts_w2'], 'L1_ffn_experts_w3': _L1_ffn_in['experts_w3']}

def reference(x, ctx_512, g_xattn, g_ffn, L0_xattn_Wq, L0_xattn_Wk, L0_xattn_Wv, L0_xattn_Wo, L0_xattn_bo, L0_ffn_Wqkv, L0_ffn_q_scale, L0_ffn_k_scale, L0_ffn_Wo, L0_ffn_ln_g, L0_ffn_ln_b, L0_ffn_W1, L0_ffn_b1, L0_ffn_W2, L0_ffn_b2, L1_xattn_Wq, L1_xattn_bq, L1_xattn_Wk, L1_xattn_bk, L1_xattn_Wv, L1_xattn_bv, L1_xattn_Wo, L1_xattn_bo, L1_ffn_gate, L1_ffn_experts_w1, L1_ffn_experts_w2, L1_ffn_experts_w3):
    import jax
    import jax.numpy as jnp

    def _L0_xattn_ref(q, kv, Wq, Wk, Wv, Wo, bo):
        import jax, jax.numpy as jnp
        import numpy as np
        NUM_HEADS = 16
        HEAD_DIM = 64
        Q_DIM = 128
        KV_DIM = 64
        INNER = NUM_HEADS * HEAD_DIM
        B, N, _ = q.shape
        M = kv.shape[1]
        scale = HEAD_DIM ** (-0.5)
        qh = (q @ Wq).reshape(B, N, NUM_HEADS, HEAD_DIM).transpose(0, 2, 1, 3)
        kh = (kv @ Wk).reshape(B, M, NUM_HEADS, HEAD_DIM).transpose(0, 2, 1, 3)
        vh = (kv @ Wv).reshape(B, M, NUM_HEADS, HEAD_DIM).transpose(0, 2, 1, 3)
        scores = jnp.einsum('bhnd,bhmd->bhnm', qh, kh) * scale
        attn = jax.nn.softmax(scores, axis=-1)
        out = jnp.einsum('bhnm,bhmd->bhnd', attn, vh)
        out = out.transpose(0, 2, 1, 3).reshape(B, N, INNER)
        return out @ Wo + bo

    def _L0_ffn_ref(x, Wqkv, q_scale, k_scale, Wo, ln_g, ln_b, W1, b1, W2, b2):
        import jax, jax.numpy as jnp
        import numpy as np
        DIM = 128
        DEPTH = 6
        HEADS = 16
        DIM_HEAD = 64
        WINDOW = 32
        INNER = HEADS * DIM_HEAD
        DIM_INNER = int(DIM * 4 * 2 / 3)
        QK_SCALE = 8.0

        def shift_tokens(t):
            a, s = jnp.split(t, 2, -1)
            s = jnp.pad(s, ((0, 0), (1, 0), (0, 0)))[:, :-1]
            return jnp.concatenate([a, s], -1)

        def l2norm(t):
            return t / jnp.maximum(jnp.linalg.norm(t, axis=-1, keepdims=True), 1e-12)

        def rotate_half(x):
            x1, x2 = jnp.split(x, 2, -1)
            return jnp.concatenate([-x2, x1], -1)

        def rotary_tables(n):
            half = jnp.arange(0, DIM_HEAD, 2, dtype=jnp.float32)
            inv_freq = 1.0 / 10000.0 ** (half / DIM_HEAD)
            t = jnp.arange(n, dtype=jnp.float32)
            freqs = t[:, None] * inv_freq[None, :]
            freqs = jnp.concatenate([freqs, freqs], -1)
            base_scale = (half + 0.4 * DIM_HEAD) / (1.4 * DIM_HEAD)
            power = (t - n // 2) / (WINDOW // 2)
            scale = base_scale[None, :] ** power[:, None]
            scale = jnp.concatenate([scale, scale], -1)
            return (freqs, scale)

        def local_attention(q, k, v):
            b, h, n, d = q.shape
            w = WINDOW
            nw = n // w
            bq = q.reshape(b, h, nw, w, d)
            bk = k.reshape(b, h, nw, w, d)
            bv = v.reshape(b, h, nw, w, d)

            def look(t):
                p = jnp.pad(t, ((0, 0), (0, 0), (1, 0), (0, 0), (0, 0)))
                return jnp.concatenate([p[:, :, :nw], p[:, :, 1:]], axis=3)
            bk2, bv2 = (look(bk), look(bv))
            seq = jnp.arange(n).reshape(nw, w)
            seq_p = jnp.pad(seq, ((1, 0), (0, 0)), constant_values=-1)
            jt = jnp.concatenate([seq_p[:nw], seq_p[1:]], axis=1)
            it = seq[:, :, None]
            jb = jt[:, None, :]
            mask = (it < jb) | (it > jb + w) | (jb == -1)
            sim = jnp.einsum('bhwie,bhwje->bhwij', bq, bk2) * QK_SCALE
            sim = jnp.where(mask, -jnp.finfo(sim.dtype).max, sim)
            attn = jax.nn.softmax(sim, -1)
            out = jnp.einsum('bhwij,bhwje->bhwie', attn, bv2)
            return out.reshape(b, h, n, d)

        def attn_layer(x, Wqkv, qs, ksc, Wo):
            b, n, _ = x.shape
            qkv = x @ Wqkv
            q, k, v = jnp.split(qkv, 3, -1)
            sh = lambda t: t.reshape(b, n, HEADS, DIM_HEAD).transpose(0, 2, 1, 3)
            q, k, v = (sh(q), sh(k), sh(v))
            q = l2norm(q) * qs
            k = l2norm(k) * ksc
            freqs, scale = rotary_tables(n)
            cos, sin = (jnp.cos(freqs), jnp.sin(freqs))
            q = q * cos * scale + rotate_half(q) * sin * scale
            inv = 1.0 / scale
            k = k * cos * inv + rotate_half(k) * sin * inv
            out = local_attention(q, k, v)
            out = out.transpose(0, 2, 1, 3).reshape(b, n, INNER)
            return out @ Wo

        def ffn_layer(x, g, bln, W1, b1, W2, b2):
            mu = x.mean(-1, keepdims=True)
            var = ((x - mu) ** 2).mean(-1, keepdims=True)
            xn = (x - mu) / jnp.sqrt(var + 1e-05) * g + bln
            hg = xn @ W1 + b1
            a, gate = jnp.split(hg, 2, -1)
            return a * jax.nn.gelu(gate, approximate=False) @ W2 + b2
        for i in range(DEPTH):
            x = attn_layer(shift_tokens(x), Wqkv[i], q_scale[i], k_scale[i], Wo[i]) + x
            x = ffn_layer(shift_tokens(x), ln_g[i], ln_b[i], W1[i], b1[i], W2[i], b2[i]) + x
        return x

    def _L1_xattn_ref(q, k, v, Wq, bq, Wk, bk, Wv, bv, Wo, bo):
        import jax, jax.numpy as jnp
        import numpy as np
        HEADS = 16
        D_MODEL = 128
        IMG_MODEL = 64
        D_K = D_MODEL // HEADS
        B, LQ, _ = q.shape
        LKV = k.shape[1]
        qh = (q @ Wq + bq).reshape(B, LQ, HEADS, D_K).transpose(0, 2, 1, 3)
        kh = (k @ Wk + bk).reshape(B, LKV, HEADS, D_K).transpose(0, 2, 1, 3)
        vh = (v @ Wv + bv).reshape(B, LKV, HEADS, D_K).transpose(0, 2, 1, 3)
        scale = 1.0 / np.sqrt(D_K)
        scores = jnp.einsum('bhqd,bhkd->bhqk', qh, kh) * scale
        attn = jax.nn.softmax(scores, axis=-1)
        out = jnp.einsum('bhqk,bhkd->bhqd', attn, vh)
        concat = out.transpose(0, 2, 1, 3).reshape(B, LQ, D_MODEL)
        return concat @ Wo + bo

    def _L1_ffn_ref(x, gate, experts_w1, experts_w2, experts_w3):
        import jax, jax.numpy as jnp
        import numpy as np
        W_SCALE = 0.02
        TOP_K = 2
        E = experts_w1.shape[0]
        router_logits = jnp.einsum('bsh,he->bse', x, gate)
        routing_weights, selected = jax.lax.top_k(router_logits, TOP_K)
        routing_weights = jax.nn.softmax(routing_weights, axis=-1)
        onehot = jax.nn.one_hot(selected, E, dtype=x.dtype)
        tok_w = jnp.einsum('bsk,bske->bse', routing_weights, onehot)
        g = jnp.einsum('bsh,ehi->ebsi', x, experts_w1)
        u = jnp.einsum('bsh,ehi->ebsi', x, experts_w3)
        hid = jax.nn.silu(g) * u
        eo = jnp.einsum('ebsi,eih->ebsh', hid, experts_w2)
        out = jnp.einsum('ebsh,bse->bsh', eo, tok_w)
        return out
    x = x + jnp.tanh(g_xattn[0]) * _L0_xattn_ref(_layernorm(x, axis=-1), ctx_512, L0_xattn_Wq, L0_xattn_Wk, L0_xattn_Wv, L0_xattn_Wo, L0_xattn_bo)
    x = x + jnp.tanh(g_ffn[0]) * _L0_ffn_ref(_layernorm(x, axis=-1), L0_ffn_Wqkv, L0_ffn_q_scale, L0_ffn_k_scale, L0_ffn_Wo, L0_ffn_ln_g, L0_ffn_ln_b, L0_ffn_W1, L0_ffn_b1, L0_ffn_W2, L0_ffn_b2)
    x = x + jnp.tanh(g_xattn[1]) * _L1_xattn_ref(_layernorm(x, axis=-1), ctx_512, ctx_512, L1_xattn_Wq, L1_xattn_bq, L1_xattn_Wk, L1_xattn_bk, L1_xattn_Wv, L1_xattn_bv, L1_xattn_Wo, L1_xattn_bo)
    x = x + jnp.tanh(g_ffn[1]) * _L1_ffn_ref(_layernorm(x, axis=-1), L1_ffn_gate, L1_ffn_experts_w1, L1_ffn_experts_w2, L1_ffn_experts_w3)
    return x

_drawn_inputs = setup_inputs


def setup_inputs(seed=0):
    import zlib

    import numpy as np

    out = dict(_drawn_inputs(seed))
    spreads = {'g_ffn': (-1.0, 0.6),
     'L0_ffn_q_scale': (1.0, 0.6),
     'L0_ffn_k_scale': (1.0, 0.6),
     'L0_ffn_ln_g': (1.0, 0.6),
     'L0_ffn_ln_b': (0.0, 0.8),
     'L0_ffn_b1': (0.0, 0.36),
     'L0_ffn_b2': (0.0, 0.1),
     'L1_xattn_bq': (0.0, 0.1),
     'L1_xattn_bk': (0.0, 0.8),
     'L1_xattn_bv': (0.0, 0.1),
     'L1_xattn_bo': (0.0, 0.1)}
    factors = {'L0_xattn_bo': 8.0,
     'L1_ffn_gate': 6.546,
     'L1_ffn_experts_w1': 5.647,
     'L1_ffn_experts_w2': 5.728,
     'L1_ffn_experts_w3': 5.609}
    for name, (base, spread) in spreads.items():
        noise = np.random.default_rng([zlib.crc32(name.encode()), seed]).standard_normal(out[name].shape)
        drawn = base * np.exp(spread * noise) if base else spread * noise
        out[name] = jnp.asarray(drawn.astype(out[name].dtype))
    for name, factor in factors.items():
        out[name] = (out[name] * factor).astype(out[name].dtype)
    return out
```

```python
from contextlib import ExitStack

import numpy as np

import concourse.bass as bass
from concourse import mybir

F32 = mybir.dt.float32
BF16 = mybir.dt.bfloat16
U32 = mybir.dt.uint32
ALU = mybir.AluOpType
ACT = mybir.ActivationFunctionType
AX = mybir.AxisListType

P = 128
B = 8
CTX = 77
CD = 64
H = 16
GH = 8
HD = 64
HC = 8
DEPTH = 6
F = 341
FC = (F + P - 1) // P
FR = F - (FC - 1) * P
E = 8
EH = 512
EC = EH // P
UNITS = 2 * B
LAG = 3
WINDOW = 32
MASKED = -1e30
EPS = 1e-5

A0 = 0
B0 = UNITS
C0 = UNITS * (1 + DEPTH)


def rotary_tables():
    half = np.arange(0, HD, 2, dtype=np.float32)
    inv_freq = 1.0 / 10000.0 ** (half / HD)
    t = np.arange(P, dtype=np.float32)
    freqs = (t[:, None] * inv_freq[None, :]).astype(np.float32)
    freqs = np.concatenate([freqs, freqs], -1)
    base = (half + 0.4 * HD) / (1.4 * HD)
    scale = base[None, :] ** ((t - P // 2) / (WINDOW // 2))[:, None]
    scale = np.concatenate([scale, scale], -1).astype(np.float32)
    sign = np.where(np.arange(HD) < HD // 2, -1.0, 1.0).astype(np.float32)
    cos, sin = np.cos(freqs), np.sin(freqs) * sign
    q = 8.0 * scale
    k = 1.0 / scale
    return np.stack([cos * q, sin * q, cos * k, sin * k], 1).astype(np.float32)


def band_mask():
    i = np.arange(P)[:, None]
    j = np.arange(P)[None, :]
    return np.where((j <= i) & (j >= i - WINDOW), 0.0, MASKED).astype(np.float32)


def constants():
    head_of = (np.arange(CD)[:, None] // HC == np.arange(GH)[None, :]).astype(np.float32)
    return {
        "k_ident": np.eye(P, dtype=np.float32),
        "k_down": np.eye(P, k=1, dtype=np.float32),
        "k_mask": band_mask(),
        "k_rotary": rotary_tables().reshape(P, 4 * HD),
        "k_headof": head_of,
        "k_iota": np.tile(np.arange(E, dtype=np.float32), (P, 1)),
    }


def build(nc, t, out):
    ctx = ExitStack()
    with ctx:
        def sb(name, shape, dt=F32):
            return ctx.enter_context(nc.sbuf_tensor(name, shape, dt))

        def sem(name):
            return ctx.enter_context(nc.semaphore(name))

        ident = sb("ident", [P, P])
        ident16 = sb("ident16", [P, P], BF16)
        down = sb("down", [P, P])
        mask_row = sb("mask_row", [P, P])
        mask16 = sb("mask16", [P, 4, P], BF16)
        rot_base = sb("rot_base", [P, 2, 2, HD])
        rot_tab = sb("rot_tab", [P, DEPTH, 2, 2, HD])
        head_of = sb("head_of", [CD, GH])
        iota = sb("iota", [P, E])
        ones_row = sb("ones_row", [1, P])
        gates = sb("gates", [P, 4])
        tgate = sb("tgate", [P, 4])
        bias_row = sb("bias_row", [P, 2, P])
        resid = sb("resid", [P, B, P])
        local = sb("local", [P, B, P])
        normed = sb("normed", [P, B, P])
        stats = sb("stats", [P, B, 6])
        moments = sb("moments", [P, B, 2])
        rstd = sb("rstd", [P, B])
        ctx_ones = sb("ctx_ones", [CTX, B, CD + 1])
        ctx_twice = sb("ctx_twice", [CTX, B, 2, CD])
        ctx_t = sb("ctx_t", [P, B, CTX])
        wa = sb("wa", [P, 4, H * HD])
        wo_a = wa[:, 3, :].rearrange("p (c o) -> p c o", c=8)
        wq_t = sb("wq_t", [P, 8, P])
        wkv_t = sb("wkv_t", [P, 2, 8, CD])
        w_qk = sb("w_qk", [P, H, CD])
        w_vo = sb("w_vo", [P, 8, P])
        wqkv = sb("wqkv", [P, 3 * H * HD])
        wo_b = sb("wo_b", [P, 8, P])
        w1_b = sb("w1_b", [P, 2 * F])
        w2_b = sb("w2_b", [P, FC, P])
        b1_b = sb("b1_b", [P, 2, FC])
        b2_b = sb("b2_b", [1, P])
        ln_b = sb("ln_b", [P, 2])
        wq_c = sb("wq_c", [P, P])
        wo_c = sb("wo_c", [CD, 2, P])
        wkv_c = sb("wkv_c", [CD, 2, P])
        bqk_c = sb("bqk_c", [CD, 2, 2])
        bq_scaled = sb("bq_scaled", [CD, 2])
        bv_c = sb("bv_c", [CTX, P])
        gate_w = sb("gate_w", [P, E])
        w_up = sb("w_up", [P, 2, 2, EH])
        w_down = sb("w_down", [P, 2, EC, P])
        x_stage = sb("x_stage", [P, P])
        x_t = sb("x_t", [P, P])
        space = sb("space", [P, 4, 2 * GH * HD])
        squares = space[:, 0, :].rearrange("p (h d) -> p h d", d=HD)
        safe_sq = sb("safe_sq", [P, 2 * GH])
        safe_var = sb("safe_var", [P, B])
        minus_half = sb("minus_half", [P, 2 * GH])
        unit_qk, rot_cos, rot_sin = (
            space[:, j, :].rearrange("p (k h d) -> p k h d", k=2, h=GH) for j in (1, 2, 3))
        hidden = space[:, :, :].rearrange("p (f a) (b n) -> p f (a b) n", f=2, b=2)
        sumsq = sb("sumsq", [P, 2 * GH])
        rnorm = sb("rnorm", [P, 2 * GH])
        qk_t = sb("qk_t", [P, 8, P])
        v_ones = sb("v_ones", [P, B, 2, GH, HD + 1])
        ctx_stage = sb("ctx_stage", [P, 2, CTX])
        kc_t = sb("kc_t", [CD, 2, B * CTX])
        kc_heads = sb("kc_heads", [CD, 2, GH, CTX])
        vc_ones = sb("vc_ones", [CTX, B, H, HC + 1])
        row_max = sb("row_max", [P, GH])
        shifted = sb("shifted", [P, GH, P])
        probs = sb("probs", [P, GH, P])
        probs_t = sb("probs_t", [P, GH, P])
        rsum = sb("rsum", [P, GH])
        heads_out = sb("heads_out", [P, GH * HD])
        heads_t = sb("heads_t", [P, 4, P])
        xn_t = sb("xn_t", [P, 2, 4 * P])
        gelu = sb("gelu", [P, FC, 4 * P])
        silu = sb("silu", [P, 2, 4 * P])
        logits = sb("logits", [P, B, E])
        top = sb("top", [P, B, 8])
        top_at = sb("top_at", [P, B, 8], U32)
        top_atf = sb("top_atf", [P, B, 8])
        pair_w = sb("pair_w", [P, 4, B])
        tok_w = sb("tok_w", [P, 3, B, E])
        tok_we = sb("tok_we", [P, 2, B])

        ps = ctx.enter_context(nc.psum_tensor("ps", [P, 8, 512], F32))
        QK_BANK, S_BANK, T_BANK, V_BANK, O_BANK = 0, 2, 4, 6, 7

        LOADS = {"const": 6, "x": 1, "ctx": 3, "wa": 4, "small": 4, "tab": 6, "wc": 8, "wqkv": 1, "wo_b": 1,
                 "ffn_w": 10, "exp0": 3, "exp1": 3}
        loaded = {n: sem("loaded_" + n) for n in LOADS}

        def landed(eng, name, times=1):
            eng.wait_ge(loaded[name], 16 * LOADS[name] * times)

        let_pass = sem("let_pass")

        def wait_alone(eng, semaphore, value):
            eng.wait_ge(semaphore, value)
            eng.sem_inc(let_pass, 1)

        const_ready = sem("const_ready")
        ones_ready = sem("ones_ready")
        tg_ready = sem("tg_ready")
        ln_var, sg_sb = sem("ln_var"), sem("sg_sb")
        prep_ps, prep_act, prep_dve = sem("prep_ps"), sem("prep_act"), sem("prep_dve")
        ln_stats, ln_mom, ln_rstd, ln_out = sem("ln_stats"), sem("ln_mom"), sem("ln_rstd"), sem("ln_out")
        resid_done = sem("resid_done")
        stage_ready = sem("stage_ready")
        xt_ps, xt_sb = sem("xt_ps"), sem("xt_sb")
        k_stage = sem("k_stage")
        qk_ps, v_ps, v_sb = sem("qk_ps"), sem("v_ps"), sem("v_sb")
        sq_sb, ss_sb, rn_sb, un_sb, rot_sb = (sem(n) for n in ("sq_sb", "ss_sb", "rn_sb", "un_sb", "rot_sb"))
        t_ps, t_sb = sem("t_ps"), sem("t_sb")
        s_ps, max_sb, sub_sb, p_sb = (sem(n) for n in ("s_ps", "max_sb", "sub_sb", "p_sb"))
        pt_ps, pt_sb, pv_ps, rs_sb, o_sb = (sem(n) for n in ("pt_ps", "pt_sb", "pv_ps", "rs_sb", "o_sb"))
        ot_ps, ot_sb, y_ps, y_sb = (sem(n) for n in ("ot_ps", "ot_sb", "y_ps", "y_sb"))
        sh_ps, sh_sb, fx_ps, fx_sb, fg_ps, fa_ps, fg_sb, fh_sb, fy_ps, fy_sb = (
            sem(n) for n in ("sh_ps", "sh_sb", "fx_ps", "fx_sb", "fg_ps", "fa_ps", "fg_sb", "fh_sb", "fy_ps", "fy_sb"))
        lg_ps, rt_own, rt_act, tokwe_sb = (sem(n) for n in ("lg_ps", "rt_own", "rt_act", "tokwe_sb"))
        eg_ps, eu_ps, eg_sb, eh_sb, ey_ps, ey_sb = (
            sem(n) for n in ("eg_ps", "eu_ps", "eg_sb", "eh_sb", "ey_ps", "ey_sb"))
        stored = sem("stored")

        def slots(eng, slot):
            def pair(b, lo, hi, nxt):
                for g in range(2):
                    slot(b, g, lambda d, g=g: lo <= g + d <= hi, nxt)
            pair(0, 0, 9, True)
            pair(1, -2, 9, True)
            with eng.Fori(2, B - 1) as b:
                pair(b, -9, 9, True)
            pair(B - 1, -9, 9, False)
            pair(B, -9, -1, False)
            pair(B + 1, -9, -3, False)

        LN_C, LN_D = 2 + DEPTH, 3 + DEPTH

        block = ctx.enter_context(nc.Block())

        @block.sync
        def _(sp):
            def load(dst, src, name, columns=False):
                sp.dma_start(dst, src, allow_slow_non_contiguous=columns).then_inc(loaded[name], 16)

            load(resid[:], t["x"].rearrange("b s d -> s b d"), "x")
            load(ident[:], t["k_ident"], "const")
            load(wa[:, 0, :], t["L0_xattn_Wq"], "wa")
            load(wa[0:CD, 1, :], t["L0_xattn_Wk"], "wa")
            load(wa[0:CD, 2, :], t["L0_xattn_Wv"], "wa")
            load(wo_a, t["L0_xattn_Wo"].rearrange("(c p) o -> p c o", p=P), "wa")
            for k in range(2):
                load(ctx_twice[:, :, k, :], t["ctx_512"].rearrange("b s d -> s b d"), "ctx")
            load(ctx_ones[:, :, 0:CD], t["ctx_512"].rearrange("b s d -> s b d"), "ctx")
            load(down[:], t["k_down"], "const")
            load(mask_row[:], t["k_mask"], "const")
            load(rot_base[:].rearrange("p a b d -> p (a b d)"), t["k_rotary"], "const")
            load(head_of[:], t["k_headof"], "const")
            load(iota[:], t["k_iota"], "const")
            load(gates[:, 0:2], t["g_xattn"].partition_broadcast(P), "small")
            load(gates[:, 2:4], t["g_ffn"].partition_broadcast(P), "small")
            load(bias_row[:, 0, :], t["L0_xattn_bo"].partition_broadcast(P), "small")
            load(bias_row[:, 1, :], t["L1_xattn_bo"].partition_broadcast(P), "small")
            for k, name in enumerate(("L0_ffn_q_scale", "L0_ffn_k_scale")):
                rows = t[name].rearrange("l d -> (l d)").partition_broadcast(P).rearrange("p (l d) -> p l d", l=DEPTH)
                load(rot_tab[:, :, k, 0, :], rows, "tab")
                for a in range(2):
                    half = HD // 2
                    load(rot_tab[:, :, k, 1, half * a:half * a + half],
                         rows[:, :, half * (1 - a):half * (2 - a)], "tab")
            for k, name in enumerate(("L1_xattn_bq", "L1_xattn_bk")):
                load(bqk_c[:, k, :], t[name].rearrange("(g p) -> p g", p=CD), "wc", True)
            load(bv_c[:], t["L1_xattn_bv"].partition_broadcast(CTX), "wc")
            load(wq_c[:], t["L1_xattn_Wq"], "wc")
            load(wo_c[:], t["L1_xattn_Wo"].rearrange("(g p) o -> p g o", p=CD), "wc")
            load(wkv_c[:, 0, :], t["L1_xattn_Wk"], "wc")
            load(wkv_c[:, 1, :], t["L1_xattn_Wv"], "wc")
            load(gate_w[:], t["L1_ffn_gate"], "wc")

            def layer(name, l):
                return t[name][bass.ds(l, 1)]

            def load_qkv(l):
                load(wqkv[:], layer("L0_ffn_Wqkv", l).rearrange("l d n -> d (l n)"), "wqkv")

            def load_out(l):
                load(wo_b[:], layer("L0_ffn_Wo", l).rearrange("l (c p) o -> p (l c) o", p=P), "wo_b")

            def load_ffn(l):
                load(w1_b[:], layer("L0_ffn_W1", l).rearrange("l d n -> d (l n)"), "ffn_w")
                w2 = layer("L0_ffn_W2", l)
                full = (FC - 1) * P
                load(w2_b[:, 0:FC - 1, :], w2[:, 0:full, :].rearrange("l (c p) o -> p (l c) o", p=P), "ffn_w")
                load(w2_b[0:FR, FC - 1, :], w2[:, full:F, :].rearrange("l p o -> p (l o)"), "ffn_w")
                b1 = layer("L0_ffn_b1", l)
                for k in range(2):
                    load(b1_b[:, k, 0:FC - 1], b1[:, k * F:k * F + full].rearrange("l (c p) -> p (l c)", p=P), "ffn_w", True)
                    load(b1_b[0:FR, k, FC - 1:FC], b1[:, k * F + full:(k + 1) * F].rearrange("l p -> p l"), "ffn_w", True)
                load(b2_b[:], layer("L0_ffn_b2", l), "ffn_w")
                load(ln_b[:, 0:1], layer("L0_ffn_ln_g", l).rearrange("l d -> d l"), "ffn_w", True)
                load(ln_b[:, 1:2], layer("L0_ffn_ln_b", l).rearrange("l d -> d l"), "ffn_w", True)

            def load_expert(e, k):
                for j, name in enumerate(("L1_ffn_experts_w1", "L1_ffn_experts_w3")):
                    load(w_up[:, k, j, :], t[name][bass.ds(e, 1)].rearrange("e d n -> d (e n)"), f"exp{k}")
                load(w_down[:, k, :, :],
                     t["L1_ffn_experts_w2"][bass.ds(e, 1)].rearrange("e (c p) o -> p (e c) o", p=P), f"exp{k}")

            load_qkv(0)
            load_out(0)
            load_ffn(0)
            load_expert(0, 0)
            load_expert(1, 1)
            with sp.Fori(1, DEPTH) as l:
                sp.wait_ge(v_ps, UNITS * l)
                load_qkv(l)
                sp.wait_ge(y_ps, B0 + UNITS * l)
                load_out(l)
                sp.wait_ge(fy_ps, 2 * l)
                load_ffn(l)
            with sp.Fori(1, E // 2) as j:
                for k in range(2):
                    sp.wait_ge(ey_ps, 4 * j + 2 * k - 2)
                    load_expert(2 * j + k, k)
            sp.wait_ge(ey_sb, 2 * E)
            sp.dma_start(out.rearrange("b s d -> s b d"), resid[:]).then_inc(stored, 16)
            sp.wait_ge(stored, 16)

        @block.tensor
        def _(pe):
            def prepare():
                landed(pe, "wa")
                landed(pe, "ctx")
                landed(pe, "const")
                for j in range(8):
                    pe.transpose(ps[:, j // 4, (j % 4) * P:(j % 4) * P + P], wa[:, 0, j * P:j * P + P], ident[:])
                for k in range(2):
                    for j in range(8):
                        pe.transpose(ps[:, 2 + k, j * CD:j * CD + CD], wa[0:CD, 1 + k, j * P:j * P + P],
                                     ident[0:CD, 0:CD])
                for b in range(B):
                    tr = pe.transpose(ps[:, 4 + b // 4, (b % 4) * CTX:(b % 4) * CTX + CTX],
                                      ctx_twice[:, b, :, :], ident[0:CTX, 0:CTX])
                tr.then_inc(prep_ps, 1)
                pe.wait_ge(prep_act, 2)
                for h in range(H):
                    r = slice(HD * (h % 2), HD * (h % 2) + HD)
                    pe.matmul(ps[:, 6 + h % 2, (h // 2) * CD:(h // 2) * CD + CD], wq_t[r, h // 2, :],
                              wkv_t[r, 0, h // 2, :], start=True, stop=True)
                for h in range(H):
                    r = slice(HD * (h % 2), HD * (h % 2) + HD)
                    mm = pe.matmul(ps[r, h // 8, (h // 2 % 4) * P:(h // 2 % 4) * P + P], wkv_t[r, 1, h // 2, :],
                                   wo_a[r, h // 2, :], start=True, stop=True)
                mm.then_inc(prep_ps, 1)
                landed(pe, "wc")
                pe.wait_ge(prep_dve, 1)
                for g in range(2):
                    for k in range(2):
                        mm = pe.matmul(ps[0:CD, 2 + 2 * g + k, 0:4 * CTX], wkv_c[:, 0, g * CD:g * CD + CD],
                                       ctx_t[0:CD, 4 * k:4 * k + 4, :], start=True, stop=True)
                mm.then_inc(prep_ps, 1)
                pe.wait_ge(prep_act, 4)
                for b in range(B):
                    mm = pe.matmul(ps[0:CTX, 6 + b // 4, (b % 4) * P:(b % 4) * P + P], ctx_t[0:CD, b, :],
                                   wkv_c[:, 1, :], start=True, stop=True)
                mm.then_inc(prep_ps, 1)

            def attention(kind, n0, b0, l=0):
                keys = P if kind == "B" else CTX
                hd = HC if kind == "C" else HD

                def transpose_x(b):
                    pe.wait_ge(stage_ready, b0 + b + 1)
                    pe.transpose(ps[:, V_BANK, 0:P], x_stage[:], ident[:]).then_inc(xt_ps, 1)

                def slot(b, g, has, nxt):
                    n = n0 + 2 * b + g
                    m = n - B0
                    if has(0):
                        if g == 0:
                            pe.wait_ge(xt_sb, 2 * (b0 + b + 1))
                        if kind == "B":
                            if has(-1):
                                pe.wait_ge(un_sb, m)
                            for k in range(2):
                                c = (k * H + g * GH) * HD
                                mm = pe.matmul(ps[:, QK_BANK + k, :], x_t[:], wqkv[:, c:c + GH * HD],
                                               start=True, stop=True)
                            mm.then_inc(qk_ps, 1)
                            if has(-3):
                                pe.wait_ge(o_sb, n - 2)
                            elif has(-1):
                                pe.wait_ge(v_sb, m)
                            c = (2 * H + g * GH) * HD
                            pe.matmul(ps[:, V_BANK, :], x_t[:], wqkv[:, c:c + GH * HD],
                                      start=True, stop=True).then_inc(v_ps, 1)
                        else:
                            if has(-2):
                                pe.wait_ge(t_sb, n - 1)
                            if kind == "A":
                                for j in range(4):
                                    h = g * GH + 2 * j
                                    mm = pe.matmul(ps[:, QK_BANK + g, j * P:j * P + P], w_qk[:, h:h + 2, :], x_t[:],
                                                   start=True, stop=True)
                            else:
                                mm = pe.matmul(ps[0:CD, QK_BANK + g, 0:P], wq_c[:, g * CD:g * CD + CD], x_t[:],
                                               start=True, stop=True)
                            mm.then_inc(t_ps, 1)
                    if has(-3):
                        wait_alone(pe, o_sb, n - 2)
                        if kind == "C":
                            tr = pe.transpose(ps[0:CD, O_BANK, 0:P], heads_out[:, 0:CD], ident[:])
                        else:
                            for j in range(4):
                                tr = pe.transpose(ps[:, O_BANK, j * P:j * P + P], heads_out[:, j * P:j * P + P],
                                                  ident[:])
                        tr.then_inc(ot_ps, 1)
                    if has(-1) and kind == "B":
                        pe.wait_ge(rot_sb, 3 * m)
                        if has(-3):
                            pe.wait_ge(pt_sb, n - 2)
                        for j in range(8):
                            o = ps[:, T_BANK + j // 4, (j % 4) * P:(j % 4) * P + P]
                            pair = slice(2 * (j % 4), 2 * (j % 4) + 2)
                            pe.matmul(o, rot_cos[:, j // 4, pair, :], ident[:], is_transpose=True,
                                      start=True, stop=False)
                            mm = pe.matmul(o, rot_sin[:, j // 4, pair, :], ident[:], is_transpose=True,
                                           start=False, stop=True)
                        mm.then_inc(t_ps, 1)
                    if has(-3):
                        pe.wait_ge(ot_sb, n - 2)
                        if kind == "B":
                            if has(0):
                                pe.wait_ge(v_sb, m + 1)
                        o = ps[:, V_BANK, 0:P]
                        gy = (g - 3) % 2
                        if kind == "C":
                            mm = pe.matmul(o, heads_t[0:CD, 0, :], wo_c[:, gy, :], start=True, stop=True)
                        else:
                            w = w_vo if kind == "A" else wo_b
                            for j in range(4):
                                mm = pe.matmul(o, heads_t[:, j, :], w[:, 4 * gy + j, :], start=(j == 0), stop=(j == 3))
                        mm.then_inc(y_ps, 1)
                    if g == 1 and nxt:
                        if has(-3):
                            pe.wait_ge(y_sb, n - 2)
                        elif kind == "B":
                            pe.wait_ge(v_sb, m + 1)
                        transpose_x(b + 1)
                    if has(-2):
                        pe.wait_ge(p_sb, n - 1)
                        if has(-1) and kind == "B":
                            pe.wait_ge(t_sb, n)
                        for h in range(GH):
                            tr = pe.transpose(ps[0:keys, T_BANK + h // 4, (h % 4) * P:(h % 4) * P + P],
                                              probs[:, h, 0:keys], ident[:])
                        tr.then_inc(pt_ps, 1)
                    if has(-1):
                        pe.wait_ge(t_sb, n)
                        if kind != "B":
                            pe.wait_ge(k_stage, n if kind == "A" else n - B0 - UNITS * DEPTH + UNITS)
                        if has(-2):
                            pe.wait_ge(sub_sb, n - 1)
                        gs = (g - 1) % 2
                        for k in range(2):
                            if kind == "B":
                                pe.matmul(ps[:, S_BANK + k, :], ident16[:], mask16[:], start=True, stop=False)
                            for j in range(4):
                                h = 2 * j + k
                                r = slice(HD * (h % 2), HD * (h % 2) + HD)
                                o = ps[:, S_BANK + k, j * keys:(j + 1) * keys]
                                if kind == "B":
                                    mm = pe.matmul(o, qk_t[r, h // 2, :], qk_t[r, 4 + h // 2, :],
                                                   start=False, stop=(j == 3))
                                elif kind == "A":
                                    mm = pe.matmul(o, qk_t[r, h // 2, :], ctx_stage[r, gs, :], start=True, stop=True)
                            if kind == "C":
                                mm = pe.matmul(ps[:, S_BANK + k, 0:4 * CTX], qk_t[0:CD, 0, :],
                                               kc_heads[:, gs, 4 * k:4 * k + 4, :], start=True, stop=True)
                        mm.then_inc(s_ps, 1)
                    if has(-2):
                        pe.wait_ge(pt_sb, n - 1)
                        if has(-3):
                            pe.wait_ge(ot_sb, n - 2)
                            pe.wait_ge(y_sb, n - 2)
                        if nxt and g == 1:
                            pe.wait_ge(xt_sb, 2 * (b0 + b + 2))
                        bv = b - 1
                        for at in range(GH):
                            h = at if kind == "C" else 2 * (at % 4) + at // 4
                            if kind == "B":
                                v = v_ones[:, bass.ds(bv, 1), g, h, :]
                            elif kind == "A":
                                v = ctx_ones[:, bass.ds(bv, 1), :]
                            else:
                                v = vc_ones[:, bass.ds(bv, 1), g * GH + h, :]
                            w = hd + 1
                            mm = pe.matmul(ps[:, V_BANK + at // 4, (at % 4) * w:(at % 4) * w + w], probs_t[0:keys, at, :], v,
                                           start=True, stop=True)
                        mm.then_inc(pv_ps, 1)

                transpose_x(0)
                slots(pe, slot)

            def feed_forward(l):
                pe.wait_ge(y_sb, B0 + UNITS * (l + 1))
                for b in range(B):
                    mm = pe.matmul(ps[:, 0, b * CD:b * CD + CD], down[:], local[:, b, CD:P], start=True, stop=True)
                mm.then_inc(sh_ps, 1)
                for hf in range(2):
                    pe.wait_ge(ln_out, B * (2 + l) + 4 * hf + 4)
                    for b in range(4):
                        tr = pe.transpose(ps[:, 1 + hf, b * P:b * P + P], normed[:, 4 * hf + b, :], ident[:])
                    tr.then_inc(fx_ps, 1)
                pe.wait_ge(loaded["ffn_w"], (l + 1) * (16 * LOADS["ffn_w"]))
                for hf in range(2):
                    pe.wait_ge(fx_sb, 2 * l + hf + 1)
                    for c in range(FC):
                        k = FC * hf + c
                        w = P if c < FC - 1 else FR
                        if k >= 2:
                            pe.wait_ge(fg_sb, 2 * FC * l + k - 1)
                            pe.wait_ge(fh_sb, 2 * FC * l + k - 1)
                        pe.matmul(ps[0:w, 3 + k % 2, :], w1_b[:, F + c * P:F + c * P + w], xn_t[:, hf, :],
                                  start=True, stop=True).then_inc(fg_ps, 1)
                        pe.matmul(ps[0:w, 5 + k % 2, :], w1_b[:, c * P:c * P + w], xn_t[:, hf, :],
                                  start=True, stop=True).then_inc(fa_ps, 1)
                for hf in range(2):
                    pe.wait_ge(fh_sb, 2 * FC * l + FC * hf + FC)
                    for b in range(4):
                        o = ps[:, 7 * (1 - hf), b * P:b * P + P]
                        for c in range(FC):
                            w = P if c < FC - 1 else FR
                            pe.matmul(o, hidden[0:w, hf, c, b * P:b * P + P], w2_b[0:w, c, :], start=(c == 0), stop=False)
                        mm = pe.matmul(o, ones_row[:], b2_b[:], start=False, stop=True)
                    mm.then_inc(fy_ps, 1)

            def experts():
                for hf in range(2):
                    pe.wait_ge(ln_out, B * LN_D + 4 * hf + 4)
                    for b in range(4):
                        tr = pe.transpose(ps[:, 6 + hf, b * P:b * P + P], normed[:, 4 * hf + b, :], ident[:])
                    tr.then_inc(fx_ps, 1)
                pe.wait_ge(fx_sb, 2 * DEPTH + 2)
                for b in range(B):
                    mm = pe.matmul(ps[:, 7, b * E:b * E + E], xn_t[:, b // 4, (b % 4) * P:(b % 4) * P + P], gate_w[:],
                                   start=True, stop=True)
                mm.then_inc(lg_ps, 1)

                def up(e, k, hf, first):
                    if hf == 0:
                        pe.wait_ge(loaded[f"exp{k}"], (e - k) * (8 * LOADS["exp0"]) + 16 * LOADS["exp0"])
                    for c in range(EC):
                        q = (2 * e + hf) * EC + c
                        if not (first and c < 2):
                            pe.wait_ge(eg_sb, q - 1)
                            pe.wait_ge(eh_sb, q - 1)
                        pe.matmul(ps[:, c % 2, :], w_up[:, k, 0, c * P:c * P + P], xn_t[:, hf, :],
                                  start=True, stop=True).then_inc(eg_ps, 1)
                        pe.matmul(ps[:, 2 + c % 2, :], w_up[:, k, 1, c * P:c * P + P], xn_t[:, hf, :],
                                  start=True, stop=True).then_inc(eu_ps, 1)

                def down_proj(e, k, hf, first):
                    s = 2 * e + hf
                    pe.wait_ge(eh_sb, (s + 1) * EC)
                    if not first:
                        pe.wait_ge(ey_sb, s - 1)
                    for b in range(4):
                        for c in range(EC):
                            mm = pe.matmul(ps[:, 4 + hf, b * P:b * P + P], hidden[:, hf, c, b * P:b * P + P],
                                           w_down[:, k, c, :], start=(c == 0), stop=(c == EC - 1))
                    mm.then_inc(ey_ps, 1)

                def expert_pair(e, first, last):
                    for k in range(2):
                        for hf in range(2):
                            s = 2 * k + hf
                            if not (last and s == 3):
                                ne = e + (s + 1) // 2
                                up(ne, ((s + 1) // 2) % 2, (s + 1) % 2, False)
                            down_proj(e + k, k, hf, first and s < 2)

                up(0, 0, 0, True)
                expert_pair(0, True, False)
                with pe.Fori(1, E // 2 - 1) as j:
                    expert_pair(2 * j, False, False)
                expert_pair(E - 2, False, True)

            prepare()
            pe.wait_ge(prep_act, 6)
            pe.wait_ge(prep_dve, 3)
            attention("A", A0, 0)
            pe.wait_ge(const_ready, 5)
            with pe.Fori(0, DEPTH) as l:
                pe.wait_ge(loaded["wqkv"], 16 * l + 16)
                pe.wait_ge(loaded["wo_b"], 16 * l + 16)
                attention("B", B0 + UNITS * l, B + B * l, l)
                feed_forward(l)
            attention("C", C0, B + B * DEPTH)
            experts()

        @block.scalar
        def _(act):
            def prepare():
                landed(act, "small")
                act.activation(tgate[:], gates[:], ACT.Tanh).then_inc(tg_ready, 1)
                act.wait_ge(prep_ps, 1)
                act.activation(wq_t[:].rearrange("p (a c) n -> p a (c n)", a=2), ps[:, 0:2, :], ACT.Copy)\
                   .then_inc(prep_act, 1)
                act.activation(wkv_t[:].rearrange("p k c n -> p k (c n)"), ps[:, 2:4, :], ACT.Copy)\
                   .then_inc(prep_act, 1)
                act.wait_ge(prep_ps, 2)
                act.activation(w_qk[:].rearrange("p (j a) n -> p a j n", a=2),
                               ps[:, 6:8, :].rearrange("p a (j n) -> p a j n", n=CD), ACT.Copy,
                               scale=HD ** -0.5).then_inc(prep_act, 1)
                act.activation(w_vo[:].rearrange("p (a c) n -> p a (c n)", a=2), ps[:, 0:2, :], ACT.Copy)\
                   .then_inc(prep_act, 1)
                act.wait_ge(prep_ps, 3)
                landed(act, "wc")
                for g in range(2):
                    act.activation(kc_t[:, g, :].rearrange("p (a c) -> p a c", a=2),
                                   ps[0:CD, 2 + 2 * g:4 + 2 * g, 0:4 * CTX], ACT.Identity,
                                   bias=bqk_c[:, 1, g:g + 1]).then_inc(prep_act, 1)

            def attention(kind, n0, b0):
                keys = P if kind == "B" else CTX

                def copy_x(b):
                    act.wait_ge(xt_ps, b0 + b + 1)
                    if kind == "B":
                        act.activation(x_t[0:CD, :], ps[0:CD, V_BANK, 0:P], ACT.Copy).then_inc(xt_sb, 1)
                        act.activation(x_t[CD:P, 1:P], ps[CD:P, V_BANK, 0:P - 1], ACT.Copy).then_inc(xt_sb, 1)
                    else:
                        act.activation(x_t[0:CD, :], ps[0:CD, V_BANK, 0:P], ACT.Copy).then_inc(xt_sb, 1)
                        act.activation(x_t[CD:P, :], ps[CD:P, V_BANK, 0:P], ACT.Copy).then_inc(xt_sb, 1)

                def slot(b, g, has, nxt):
                    n = n0 + 2 * b + g
                    m = n - B0
                    if has(0) and kind == "B":
                        act.wait_ge(qk_ps, m + 1)
                        if has(-1):
                            act.wait_ge(ss_sb, m)
                        act.activation(squares[:].rearrange("p (a h) d -> p a (h d)", a=2),
                                       ps[:, QK_BANK:QK_BANK + 2, :], ACT.Square).then_inc(sq_sb, 1)
                        act.wait_ge(v_ps, m + 1)
                        act.activation(v_ones[:, bass.ds(b, 1), g, :, 0:HD],
                                       ps[:, V_BANK, :].rearrange("p (a h d) -> p a h d", a=1, h=GH), ACT.Copy)\
                           .then_inc(v_sb, 1)
                    if has(-3):
                        act.wait_ge(ot_ps, n - 2)
                        if has(-4):
                            act.wait_ge(y_ps, n - 3)
                        if kind == "C":
                            act.activation(heads_t[0:CD, 0, :], ps[0:CD, O_BANK, 0:P], ACT.Copy).then_inc(ot_sb, 1)
                        else:
                            act.activation(heads_t[:].rearrange("p c n -> p (c n)"), ps[:, O_BANK, :], ACT.Copy)\
                               .then_inc(ot_sb, 1)
                    if has(-2):
                        act.wait_ge(sub_sb, n - 1)
                        if has(-3):
                            act.wait_ge(pt_ps, n - 2)
                        act.activation(probs[:, :, 0:keys], shifted[:, :, 0:keys], ACT.Exp).then_inc(p_sb, 1)
                    if has(-1):
                        act.wait_ge(t_ps, n)
                        if has(-2):
                            act.wait_ge(s_ps, n - 1)
                        gq = (g - 1) % 2
                        if kind == "B":
                            act.activation(qk_t[:].rearrange("p (a c) n -> p a (c n)", a=2),
                                           ps[:, T_BANK:T_BANK + 2, :], ACT.Copy).then_inc(t_sb, 1)
                        elif kind == "A":
                            act.activation(qk_t[:, 0:4, :].rearrange("p c n -> p (c n)"), ps[:, QK_BANK + gq, :],
                                           ACT.Copy).then_inc(t_sb, 1)
                        else:
                            act.activation(qk_t[0:CD, 0, :], ps[0:CD, QK_BANK + gq, 0:P], ACT.Identity,
                                           bias=bq_scaled[:, gq:gq + 1], scale=HC ** -0.5).then_inc(t_sb, 1)
                    if g == 1 and nxt:
                        copy_x(b + 1)
                    if has(-2):
                        act.wait_ge(pt_ps, n - 1)
                        if has(-3):
                            act.wait_ge(pv_ps, n - 2)
                        act.activation(probs_t[0:keys, :, :].rearrange("p (a c) n -> p a (c n)", a=2),
                                       ps[0:keys, T_BANK:T_BANK + 2, :], ACT.Copy).then_inc(pt_sb, 1)

                copy_x(0)
                slots(act, slot)

            def feed_forward(l):
                for hf in range(2):
                    for c in range(FC):
                        k = FC * hf + c
                        w = P if c < FC - 1 else FR
                        act.wait_ge(fg_ps, 2 * FC * l + k + 1)
                        if k >= FC:
                            act.wait_ge(fh_sb, 2 * FC * l + k - FC + 1)
                        act.activation(gelu[0:w, c, :], ps[0:w, 3 + k % 2, :], ACT.Gelu,
                                       bias=b1_b[0:w, 1, c:c + 1]).then_inc(fg_sb, 1)

            def experts():
                act.wait_ge(rt_own, 4)
                act.activation(pair_w[:, 1, :], pair_w[:, 0, :], ACT.Exp).then_inc(rt_act, 1)

                def pair(e, first):
                    for s in range(4):
                        for c in range(EC):
                            q = (2 * e + s) * EC + c
                            act.wait_ge(eg_ps, q + 1)
                            if not (first and s == 0 and c < 2):
                                act.wait_ge(eh_sb, q - 1)
                            act.activation(silu[:, c % 2, :], ps[:, c % 2, :], ACT.Silu).then_inc(eg_sb, 1)
                pair(0, True)
                with act.Fori(1, E // 2) as j:
                    pair(2 * j, False)

            prepare()
            attention("A", A0, 0)
            with act.Fori(0, DEPTH) as l:
                attention("B", B0 + UNITS * l, B + B * l)
                feed_forward(l)
            attention("C", C0, B + B * DEPTH)
            experts()

        @block.gpsimd
        def _(pool):
            def norm_scale(k):
                wait_alone(pool, ln_mom, B * (k + 1))
                pool.tensor_scalar(safe_var[:], moments[:, :, 1], EPS, None, ALU.add).then_inc(ln_var, 1)
                wait_alone(pool, ln_var, k + 1)
                pool.tensor_tensor(rstd[:], safe_var[:], minus_half[:, 0:B], ALU.pow).then_inc(ln_rstd, 1)

            def stage_keys(kind, n0, k0):
                def slot(b, g, has, nxt):
                    if not has(0):
                        return
                    if has(-2):
                        wait_alone(pool, s_ps, n0 + 2 * b + g - 1)
                    if kind == "A":
                        pool.tensor_copy(ctx_stage[:, g, :], ctx_t[:, bass.ds(b, 1), :].rearrange("p a c -> p (a c)"))\
                            .then_inc(k_stage, 1)
                    else:
                        src = kc_t[:, g, bass.ds(b * CTX, CTX)].unsqueeze(1).to_broadcast([CD, GH, CTX])
                        pool.tensor_tensor(kc_heads[:, g, :, :], src,
                                           head_of[:].unsqueeze(2).to_broadcast([CD, GH, CTX]), ALU.mult)\
                            .then_inc(k_stage, 1)
                slots(pool, slot)

            def local_units(l):
                def slot(b, g, has, nxt):
                    if not has(0):
                        return
                    m = UNITS * l + 2 * b + g
                    wait_alone(pool, ss_sb, m + 1)
                    if has(-1):
                        wait_alone(pool, un_sb, m)
                    pool.tensor_scalar(safe_sq[:], sumsq[:], 1e-24, None, ALU.max).then_inc(sg_sb, 1)
                    wait_alone(pool, sg_sb, m + 1)
                    pool.tensor_tensor(rnorm[:], safe_sq[:], minus_half[:], ALU.pow).then_inc(rn_sb, 1)
                    wait_alone(pool, un_sb, m + 1)
                    if has(-1):
                        wait_alone(pool, t_ps, B0 + m)
                    half = HD // 2

                    def table(s, a, w):
                        tab = rot_tab[:, bass.ds(l, 1), :, s, a:a + w].rearrange("p l k d -> p (l k) d")
                        return tab.unsqueeze(2).to_broadcast([P, 2, GH, w])
                    pool.tensor_tensor(rot_cos[:], unit_qk[:], table(0, 0, HD), ALU.mult).then_inc(rot_sb, 1)
                    for a in range(2):
                        other = half * (1 - a)
                        pool.tensor_tensor(rot_sin[:, :, :, half * a:half * a + half],
                                           unit_qk[:, :, :, other:other + half], table(1, half * a, half),
                                           ALU.mult).then_inc(rot_sb, 1)
                slots(pool, slot)

            pool.memset(v_ones[:, :, :, :, HD:HD + 1], 1.0).then_inc(ones_ready, 1)
            pool.memset(ctx_ones[:, :, CD:CD + 1], 1.0).then_inc(ones_ready, 1)
            pool.memset(vc_ones[:, :, :, HC:HC + 1], 1.0).then_inc(ones_ready, 1)
            pool.memset(minus_half[:], -0.5).then_inc(ones_ready, 1)
            pool.wait_ge(ones_ready, 4)
            norm_scale(0)
            pool.wait_ge(prep_dve, 1)
            stage_keys("A", A0, 0)
            norm_scale(1)
            pool.wait_ge(const_ready, 5)
            with pool.Fori(0, DEPTH) as l:
                local_units(l)
                norm_scale(2 + l)
            norm_scale(LN_C)
            stage_keys("C", C0, UNITS)
            norm_scale(LN_D)

        @block.vector
        def _(dve):
            def layer_norm(k, src, dst, ready):
                ready()
                for b in range(B):
                    dve.bn_stats(stats[:, b, :], src[:, b, :]).then_inc(ln_stats, 1)
                wait_alone(dve, ln_stats, B * (k + 1))
                for b in range(B):
                    dve.bn_aggr(moments[:, b, :], stats[:, b, :]).then_inc(ln_mom, 1)
                dve.wait_ge(ln_mom, B * (k + 1))
                dve.wait_ge(ln_rstd, k + 1)
                for b in range(B):
                    dve.tensor_scalar(dst[:, b, :], src[:, b, :], moments[:, b, 0:1], rstd[:, b:b + 1],
                                      ALU.subtract, ALU.mult).then_inc(ln_out, 1)

            def attention(kind, n0, b0, src):
                keys = P if kind == "B" else CTX
                hd = HC if kind == "C" else HD
                to = local if kind == "B" else resid

                def stage(b):
                    if not (kind == "A" and isinstance(b, int) and b == 0):
                        dve.wait_ge(xt_ps, b0 + b)
                    dve.tensor_copy(x_stage[:], src[:, bass.ds(b, 1), :].rearrange("p a d -> p (a d)"))\
                       .then_inc(stage_ready, 1)

                def slot(b, g, has, nxt):
                    n = n0 + 2 * b + g
                    m = n - B0
                    heads = ps[:, V_BANK:V_BANK + 2, 0:4 * (hd + 1)].rearrange("p a (h d) -> p a h d", h=4)
                    if has(-3):
                        dve.wait_ge(pv_ps, n - 2)
                        dve.reciprocal(rsum[:].rearrange("p (a h d) -> p a h d", a=2, d=1), heads[:, :, :, hd:hd + 1])\
                           .then_inc(rs_sb, 1)
                        dve.wait_ge(rs_sb, n - 2)
                        if has(-4):
                            dve.wait_ge(ot_ps, n - 3)
                        order = "p (a h d) -> p a h d" if kind == "C" else "p (h a d) -> p a h d"
                        dve.tensor_tensor(heads_out[:, 0:GH * hd].rearrange(order, a=2, h=4),
                                          heads[:, :, :, 0:hd],
                                          rsum[:].rearrange("p (a h) -> p a h", a=2).unsqueeze(3)
                                          .to_broadcast([P, 2, 4, hd]), ALU.mult).then_inc(o_sb, 1)
                    if has(-2):
                        dve.wait_ge(s_ps, n - 1)
                        scores = ps[:, S_BANK:S_BANK + 2, 0:4 * keys].rearrange("p a (h k) -> p a h k", h=4)
                        dve.tensor_reduce(row_max[:].rearrange("p (a h) -> p a h", a=2), scores, AX.X, ALU.max)\
                           .then_inc(max_sb, 1)
                        dve.wait_ge(max_sb, n - 1)
                        if has(-3):
                            dve.wait_ge(p_sb, n - 2)
                        dve.tensor_tensor(shifted[:, :, 0:keys].rearrange("p (a h) k -> p a h k", a=2), scores,
                                          row_max[:].rearrange("p (a h) -> p a h", a=2).unsqueeze(3)
                                          .to_broadcast([P, 2, 4, keys]), ALU.subtract).then_inc(sub_sb, 1)
                    if has(0) and kind == "B":
                        dve.wait_ge(sq_sb, m + 1)
                        if has(-1):
                            dve.wait_ge(rn_sb, m)
                        dve.tensor_reduce(sumsq[:], squares[:], AX.X, ALU.add).then_inc(ss_sb, 1)
                    if g == 1 and nxt:
                        stage(b + 1)
                    if has(-3):
                        bo = b + (g - 3) // 2
                        dve.wait_ge(y_ps, n - 2)
                        if has(-4):
                            dve.wait_ge(y_sb, n - 3)
                        y = ps[:, V_BANK, 0:P].rearrange("p (a d) -> p a d", a=1)
                        x = to[:, bass.ds(bo, 1), :]
                        if kind == "B":
                            dve.tensor_tensor(x, y, x, ALU.add).then_inc(y_sb, 1)
                        else:
                            k = 0 if kind == "A" else 1
                            dve.scalar_tensor_tensor(x, y, tgate[:, k:k + 1], x, ALU.mult, ALU.add).then_inc(y_sb, 1)
                    if has(0) and kind == "B":
                        dve.wait_ge(rn_sb, m + 1)
                        if has(-1):
                            dve.wait_ge(rot_sb, 3 * m)
                        dve.tensor_tensor(unit_qk[:], ps[:, QK_BANK:QK_BANK + 2, :]
                                          .rearrange("p a (h d) -> p a h d", h=GH),
                                          rnorm[:].rearrange("p (a h) -> p a h", a=2).unsqueeze(3)
                                          .to_broadcast([P, 2, GH, HD]), ALU.mult).then_inc(un_sb, 1)

                stage(0)
                slots(dve, slot)

            def add_bias(k, done):
                dve.scalar_tensor_tensor(resid[:], bias_row[:, k, :].unsqueeze(1).to_broadcast([P, B, P]),
                                         tgate[:, k:k + 1], resid[:], ALU.mult, ALU.add).then_inc(resid_done, 1)
                dve.wait_ge(resid_done, done)

            def feed_forward(l):
                dve.wait_ge(y_sb, B0 + UNITS * (l + 1))
                dve.tensor_copy(normed[:, :, 0:CD], local[:, :, 0:CD]).then_inc(sh_sb, 1)
                dve.wait_ge(sh_ps, l + 1)
                dve.tensor_copy(normed[:, :, CD:P], ps[:, 0, :].rearrange("p (b d) -> p b d", b=B)).then_inc(sh_sb, 1)
                layer_norm(2 + l, normed, normed, lambda: dve.wait_ge(sh_sb, 2 * l + 2))
                dve.wait_ge(loaded["ffn_w"], (l + 1) * (16 * LOADS["ffn_w"]))
                for hf in range(2):
                    dve.wait_ge(fx_ps, 2 * l + hf + 1)
                    dve.tensor_scalar(xn_t[:, hf, :], ps[:, 1 + hf, :], ln_b[:, 0:1], ln_b[:, 1:2], ALU.mult, ALU.add)\
                       .then_inc(fx_sb, 1)
                for hf in range(2):
                    for c in range(FC):
                        k = FC * hf + c
                        w = P if c < FC - 1 else FR
                        dve.wait_ge(fa_ps, 2 * FC * l + k + 1)
                        dve.wait_ge(fg_sb, 2 * FC * l + k + 1)
                        dve.scalar_tensor_tensor(hidden[0:w, hf, c, :], ps[0:w, 5 + k % 2, :], b1_b[0:w, 0, c:c + 1],
                                                 gelu[0:w, c, :], ALU.add, ALU.mult).then_inc(fh_sb, 1)
                for hf in range(2):
                    dve.wait_ge(fy_ps, 2 * l + hf + 1)
                    x = local[:, 4 * hf:4 * hf + 4, :].rearrange("p b d -> p (b d)")
                    dve.tensor_tensor(x, ps[:, 7 * (1 - hf), :], x, ALU.add).then_inc(fy_sb, 1)
                dve.wait_ge(fy_sb, 2 * l + 2)

            def route():
                done = [0]

                def own(ins):
                    done[0] += 1
                    ins.then_inc(rt_own, 1)
                    return done[0]
                dve.wait_ge(lg_ps, 1)
                n = own(dve.tensor_copy(logits[:].rearrange("p b e -> p (b e)"), ps[:, 7, 0:B * E]))
                dve.wait_ge(rt_own, n)
                for b in range(B):
                    ins = dve.max(top[:, b, :], logits[:, b, :])
                n = own(ins)
                dve.wait_ge(rt_own, n)
                for b in range(B):
                    ins = dve.max_index(top_at[:, b, :], top[:, b, :], logits[:, b, :])
                n = own(ins)
                dve.wait_ge(rt_own, n)
                n = own(dve.tensor_tensor(pair_w[:, 0, :], top[:, :, 1], top[:, :, 0], ALU.subtract))
                n = own(dve.tensor_copy(top_atf[:], top_at[:]))
                dve.wait_ge(rt_act, 1)
                n = own(dve.tensor_scalar(pair_w[:, 2, :], pair_w[:, 1, :], 1.0, None, ALU.add))
                dve.wait_ge(rt_own, n)
                n = own(dve.reciprocal(pair_w[:, 2, :], pair_w[:, 2, :]))
                dve.wait_ge(rt_own, n)
                n = own(dve.tensor_scalar(pair_w[:, 2, :], pair_w[:, 2, :], tgate[:, 3:4], None, ALU.mult))
                dve.wait_ge(rt_own, n)
                n = own(dve.tensor_tensor(pair_w[:, 3, :], pair_w[:, 2, :], pair_w[:, 1, :], ALU.mult))
                dve.wait_ge(rt_own, n)
                for k in range(2):
                    for b in range(B):
                        ins = dve.tensor_scalar(tok_w[:, k, b, :], iota[:], top_atf[:, b, k:k + 1],
                                                pair_w[:, 2 + k, b:b + 1], ALU.is_equal, ALU.mult)
                n = own(ins)
                dve.wait_ge(rt_own, n)
                n = own(dve.tensor_tensor(tok_w[:, 2, :, :], tok_w[:, 0, :, :], tok_w[:, 1, :, :], ALU.add))
                dve.wait_ge(rt_own, n)

            def experts():
                for hf in range(2):
                    dve.wait_ge(fx_ps, 2 * DEPTH + hf + 1)
                    dve.tensor_copy(xn_t[:, hf, :], ps[:, 6 + hf, :]).then_inc(fx_sb, 1)
                route()

                def multiply(e, hf):
                    for c in range(EC):
                        q = (2 * e + hf) * EC + c
                        dve.wait_ge(eu_ps, q + 1)
                        dve.wait_ge(eg_sb, q + 1)
                        dve.tensor_tensor(hidden[:, hf, c, :], ps[:, 2 + c % 2, :], silu[:, c % 2, :], ALU.mult)\
                           .then_inc(eh_sb, 1)

                def weigh(e, k, hf, first):
                    s = 2 * e + hf
                    if hf == 0:
                        dve.tensor_copy(tok_we[:, k, :], tok_w[:, 2, :, bass.ds(e, 1)].rearrange("p b e -> p (b e)"))\
                           .then_inc(tokwe_sb, 1)
                        dve.wait_ge(tokwe_sb, e + 1)
                    dve.wait_ge(ey_ps, s + 1)
                    if not first:
                        dve.wait_ge(ey_sb, s - 1)
                    for b in range(4):
                        x = resid[:, 4 * hf + b, :]
                        ins = dve.scalar_tensor_tensor(x, ps[:, 4 + hf, b * P:b * P + P],
                                                       tok_we[:, k, 4 * hf + b:4 * hf + b + 1], x, ALU.mult, ALU.add)
                    ins.then_inc(ey_sb, 1)

                def expert_pair(e, first, last):
                    for k in range(2):
                        for hf in range(2):
                            s = 2 * k + hf
                            if not (last and s == 3):
                                multiply(e + (s + 1) // 2, (s + 1) % 2)
                            weigh(e + k, k, hf, first and s < 2)

                multiply(0, 0)
                expert_pair(0, True, False)
                with dve.Fori(1, E // 2 - 1) as j:
                    expert_pair(2 * j, False, False)
                expert_pair(E - 2, False, True)

            layer_norm(0, resid, normed, lambda: landed(dve, "x"))
            landed(dve, "const")
            dve.tensor_copy(ident16[:], ident[:]).then_inc(const_ready, 1)
            dve.tensor_copy(mask16[:], mask_row[:].unsqueeze(1).to_broadcast([P, 4, P])).then_inc(const_ready, 1)
            dve.memset(ones_row[:], 1.0).then_inc(const_ready, 1)
            landed(dve, "tab")
            dve.tensor_tensor(rot_tab[:].rearrange("p l a b d -> p l (a b d)"),
                              rot_tab[:].rearrange("p l a b d -> p l (a b d)"),
                              rot_base[:].rearrange("p a b d -> p (a b d)").unsqueeze(1)
                              .to_broadcast([P, DEPTH, 4 * HD]), ALU.mult).then_inc(const_ready, 1)
            dve.wait_ge(prep_ps, 1)
            dve.tensor_copy(ctx_t[:].rearrange("p (a b) c -> p a (b c)", a=2), ps[:, 4:6, 0:4 * CTX])\
               .then_inc(prep_dve, 1)
            landed(dve, "wc")
            dve.tensor_scalar(bq_scaled[:], bqk_c[:, 0, :], HC ** -0.5, None, ALU.mult).then_inc(prep_dve, 1)
            dve.wait_ge(prep_ps, 4)
            dve.wait_ge(ones_ready, 4)
            dve.tensor_tensor(vc_ones[:, :, :, 0:HC].rearrange("p (a b) h d -> p a b h d", a=1)[:, 0],
                              ps[0:CTX, 6:8, :].rearrange("p a (b h d) -> p (a b) h d", b=4, h=H),
                              bv_c[:].rearrange("p (h d) -> p h d", h=H).unsqueeze(1).to_broadcast([CTX, B, H, HC]),
                              ALU.add).then_inc(prep_dve, 1)
            dve.wait_ge(tg_ready, 1)
            dve.wait_ge(ln_out, B)
            attention("A", A0, 0, normed)
            dve.wait_ge(y_sb, UNITS)
            dve.memset(x_t[CD:P, 0:1], 0.0).then_inc(const_ready, 1)
            add_bias(0, 1)
            layer_norm(1, resid, local, lambda: None)
            dve.wait_ge(ln_out, 2 * B)
            with dve.Fori(0, DEPTH) as l:
                attention("B", B0 + UNITS * l, B + B * l, local)
                feed_forward(l)
            dve.scalar_tensor_tensor(resid[:], local[:], tgate[:, 2:3], resid[:], ALU.mult, ALU.add)\
               .then_inc(resid_done, 1)
            layer_norm(LN_C, resid, normed, lambda: dve.wait_ge(resid_done, 2))
            dve.wait_ge(ln_out, B * (LN_C + 1))
            attention("C", C0, B + B * DEPTH, normed)
            dve.wait_ge(y_sb, C0 + UNITS)
            add_bias(1, 3)
            layer_norm(LN_D, resid, normed, lambda: None)
            experts()


_INS = ["x", "ctx_512", "g_xattn", "g_ffn",
        "L0_xattn_Wq", "L0_xattn_Wk", "L0_xattn_Wv", "L0_xattn_Wo", "L0_xattn_bo",
        "L0_ffn_Wqkv", "L0_ffn_q_scale", "L0_ffn_k_scale", "L0_ffn_Wo", "L0_ffn_ln_g", "L0_ffn_ln_b",
        "L0_ffn_W1", "L0_ffn_b1", "L0_ffn_W2", "L0_ffn_b2",
        "L1_xattn_Wq", "L1_xattn_bq", "L1_xattn_Wk", "L1_xattn_bk", "L1_xattn_Wv", "L1_xattn_bv",
        "L1_xattn_Wo", "L1_xattn_bo",
        "L1_ffn_gate", "L1_ffn_experts_w1", "L1_ffn_experts_w2", "L1_ffn_experts_w3"]


def kernel(**inputs):
    import concourse.bacc as bacc
    from concourse.bass_utils import run_bass_kernel_spmd

    nc = bacc.Bacc("TRN2", target_bir_lowering=False, num_devices=1)
    arrays = {f"in_{name}_dram": np.ascontiguousarray(inputs[name]) for name in _INS}
    arrays.update({f"in_{name}_dram": value for name, value in constants().items()})
    t = {name[3:-5]: nc.dram_tensor(name, a.shape, mybir.dt.from_np(a.dtype), kind="ExternalInput").ap()
         for name, a in arrays.items()}
    out = nc.dram_tensor("out_0_dram", (B, P, P), F32, kind="ExternalOutput").ap()
    build(nc, t, out)
    r = run_bass_kernel_spmd(nc, [arrays], core_ids=[0])
    return r.results[0]["out_0_dram"]
```

```python
from contextlib import ExitStack

import numpy as np

import concourse.bass as bass
from concourse import mybir

F32 = mybir.dt.float32
BF16 = mybir.dt.bfloat16
U32 = mybir.dt.uint32
ALU = mybir.AluOpType
ACT = mybir.ActivationFunctionType
AX = mybir.AxisListType

P = 128
B = 8
CTX = 77
CD = 64
H = 16
GH = 8
HD = 64
HC = 8
DEPTH = 6
F = 341
FC = (F + P - 1) // P
FR = F - (FC - 1) * P
E = 8
EH = 512
EC = EH // P
UNITS = 2 * B
LAG = 3
WINDOW = 32
MASKED = -1e30
EPS = 1e-5

CYCLES = UNITS * DEPTH // 4

A0 = 0
B0 = UNITS
C0 = UNITS * (1 + DEPTH)


def rotary_tables():
    half = np.arange(0, HD, 2, dtype=np.float32)
    inv_freq = 1.0 / 10000.0 ** (half / HD)
    t = np.arange(P, dtype=np.float32)
    freqs = (t[:, None] * inv_freq[None, :]).astype(np.float32)
    freqs = np.concatenate([freqs, freqs], -1)
    base = (half + 0.4 * HD) / (1.4 * HD)
    scale = base[None, :] ** ((t - P // 2) / (WINDOW // 2))[:, None]
    scale = np.concatenate([scale, scale], -1).astype(np.float32)
    sign = np.where(np.arange(HD) < HD // 2, -1.0, 1.0).astype(np.float32)
    cos, sin = np.cos(freqs), np.sin(freqs) * sign
    q = 8.0 * scale
    k = 1.0 / scale
    return np.stack([cos * q, sin * q, cos * k, sin * k], 1).astype(np.float32)


def band_mask():
    i = np.arange(P)[:, None]
    j = np.arange(P)[None, :]
    return np.where((j <= i) & (j >= i - WINDOW), 0.0, MASKED).astype(np.float32)


def constants():
    head_of = (np.arange(CD)[:, None] // HC == np.arange(GH)[None, :]).astype(np.float32)
    return {
        "k_ident": np.eye(P, dtype=np.float32),
        "k_down": np.eye(P, k=1, dtype=np.float32),
        "k_mask": band_mask(),
        "k_rotary": rotary_tables().reshape(P, 4 * HD),
        "k_headof": head_of,
        "k_iota": np.tile(np.arange(E, dtype=np.float32), (P, 1)),
    }


def build(nc, t, out):
    ctx = ExitStack()
    with ctx:
        def sb(name, shape, dt=F32):
            return ctx.enter_context(nc.sbuf_tensor(name, shape, dt))

        def sem(name):
            return ctx.enter_context(nc.semaphore(name))

        ident = sb("ident", [P, P])
        ident16 = sb("ident16", [P, P], BF16)
        down = sb("down", [P, P])
        mask_row = sb("mask_row", [P, P])
        mask16 = sb("mask16", [P, 4, P], BF16)
        rot_base = sb("rot_base", [P, 2, 2, HD])
        rot_tab = sb("rot_tab", [P, DEPTH, 2, 2, HD])
        head_of = sb("head_of", [CD, GH])
        iota = sb("iota", [P, E])
        gates = sb("gates", [P, 4])
        tgate = sb("tgate", [P, 4])
        bias_row = sb("bias_row", [P, 2, P])
        resid = sb("resid", [P, B, P])
        local = sb("local", [P, B, P])
        normed = sb("normed", [P, B, P])
        stats = sb("stats", [P, B, 6])
        moments = sb("moments", [P, B, 2])
        rstd = sb("rstd", [P, B])
        ctx_ones = sb("ctx_ones", [CTX, B, CD + 1])
        ctx_twice = sb("ctx_twice", [CTX, B, 2, CD])
        ctx_t = sb("ctx_t", [P, B, CTX])
        wbuf = sb("wbuf", [P, 2, 4 * H * HD])
        wa = wbuf[:, 1, :].rearrange("p (k n) -> p k n", k=4)
        wo_a = wa[:, 3, :].rearrange("p (c o) -> p c o", c=8)
        wq_t = sb("wq_t", [P, 8, P])
        wkv_t = sb("wkv_t", [P, 2, 8, CD])
        w_qk = sb("w_qk", [P, H, CD])
        w_vo = sb("w_vo", [P, 8, P])
        w1_b = sb("w1_b", [P, 2 * F])
        w2_b = sb("w2_b", [P, FC, P])
        b1_b = sb("b1_b", [P, 2, FC])
        ln_b = sb("ln_b", [P, 2])
        wq_c = sb("wq_c", [P, P])
        wo_c = sb("wo_c", [CD, 2, P])
        wkv_c = sb("wkv_c", [CD, 2, P])
        bqk_c = sb("bqk_c", [CD, 2, 2])
        bq_scaled = sb("bq_scaled", [CD, 2])
        bv_c = sb("bv_c", [CTX, P])
        gate_w = sb("gate_w", [P, E])
        w_up = sb("w_up", [P, 2, 2, EH])
        w_down = sb("w_down", [P, 2, EC, P])
        x_stage = sb("x_stage", [P, P])
        x_t = sb("x_t", [P, P])
        space = sb("space", [P, 4, 2 * GH * HD])
        squares = space[:, 0, :].rearrange("p (h d) -> p h d", d=HD)
        safe_sq = sb("safe_sq", [P, 2 * GH])
        safe_var = sb("safe_var", [P, B])
        minus_half = sb("minus_half", [P, 2 * GH])
        raw_qk, rot_cos, rot_sin = (
            space[:, j, :].rearrange("p (k h d) -> p k h d", k=2, h=GH) for j in (1, 2, 3))
        hidden = space[:, :, :].rearrange("p (f a) (b n) -> p f (a b) n", f=2, b=2)
        sumsq = sb("sumsq", [P, 2 * GH])
        rnorm = sb("rnorm", [P, 2 * GH])
        qk_t = sb("qk_t", [P, 8, P])
        v_ones = sb("v_ones", [P, B, 2, GH, HD + 1])
        ctx_stage = sb("ctx_stage", [P, 2, CTX])
        kc_t = sb("kc_t", [CD, 2, B * CTX])
        kc_heads = sb("kc_heads", [CD, 2, GH, CTX])
        vc_ones = sb("vc_ones", [CTX, B, H, HC + 1])
        row_max = sb("row_max", [P, GH])
        shifted = sb("shifted", [P, GH, P])
        probs = sb("probs", [P, GH, P])
        probs_t = sb("probs_t", [P, GH, P])
        rsum = sb("rsum", [P, GH])
        heads_out = sb("heads_out", [P, GH * HD])
        heads_t = sb("heads_t", [P, 4, P])
        xn_t = sb("xn_t", [P, 2, 4 * P])
        pair_n = sb("pair_n", [P, 2, P])
        pair_stats = sb("pair_stats", [P, 2, 6])
        pair_mom = sb("pair_mom", [P, 2, 2])
        pair_var = sb("pair_var", [P, 2])
        pair_rstd = sb("pair_rstd", [P, 2])
        pair_t = sb("pair_t", [P, 2 * P])
        gelu = sb("gelu", [P, FC, 2 * P])
        table_call = sb("table_call", [P, 1])
        pair_hid = sb("pair_hid", [P, FC, 2 * P])
        silu = sb("silu", [P, 2, 4 * P])
        turned = silu[:].rearrange("p k (h d) -> p k h d", h=GH)
        logits = sb("logits", [P, B, E])
        top = sb("top", [P, B, 8])
        top_at = sb("top_at", [P, B, 8], U32)
        top_atf = sb("top_atf", [P, B, 8])
        pair_w = sb("pair_w", [P, 4, B])
        tok_w = sb("tok_w", [P, 3, B, E])
        tok_we = sb("tok_we", [P, 2, B])

        ps = ctx.enter_context(nc.psum_tensor("ps", [P, 8, 512], F32))
        QK_BANK, S_BANK, T_BANK, V_BANK, O_BANK = 0, 2, 4, 6, 7

        LOADS = {"const": 6, "x": 1, "ctx": 3, "wa": 4, "small": 4, "tab": 6, "wc": 8, "wqkv": 1, "wo_b": 1,
                 "ffn_in": 7, "ffn_out": 3, "exp0": 3, "exp1": 3}
        loaded = {n: sem("loaded_" + n) for n in LOADS}

        def landed(eng, name, times=1):
            eng.wait_ge(loaded[name], 16 * LOADS[name] * times)

        let_pass = sem("let_pass")

        def wait_alone(eng, semaphore, value):
            eng.wait_ge(semaphore, value)
            eng.sem_inc(let_pass, 1)

        const_ready = sem("const_ready")
        ones_ready = sem("ones_ready")
        tg_ready = sem("tg_ready")
        ln_var, sg_sb = sem("ln_var"), sem("sg_sb")
        prep_ps, prep_act, prep_dve = sem("prep_ps"), sem("prep_act"), sem("prep_dve")
        ln_stats, ln_mom, ln_rstd, ln_out = sem("ln_stats"), sem("ln_mom"), sem("ln_rstd"), sem("ln_out")
        resid_done = sem("resid_done")
        stage_ready = sem("stage_ready")
        xt_ps, xt_sb = sem("xt_ps"), sem("xt_sb")
        k_stage = sem("k_stage")
        qk_ps, v_ps, v_sb = sem("qk_ps"), sem("v_ps"), sem("v_sb")
        raw_sb, sq_sb, ss_sb, rn_sb, un_sb, rot_sb, ra_sb = (
            sem(n) for n in ("raw_sb", "sq_sb", "ss_sb", "rn_sb", "un_sb", "rot_sb", "ra_sb"))
        t_ps, t_sb = sem("t_ps"), sem("t_sb")
        s_ps, max_sb, sub_sb, p_sb = (sem(n) for n in ("s_ps", "max_sb", "sub_sb", "p_sb"))
        pt_ps, pt_sb, pv_ps, rs_sb, o_sb = (sem(n) for n in ("pt_ps", "pt_sb", "pv_ps", "rs_sb", "o_sb"))
        ot_ps, ot_sb, y_ps, y_sb = (sem(n) for n in ("ot_ps", "ot_sb", "y_ps", "y_sb"))
        sh_ps, sh_sb, fs_sb, fm_sb, fv_sb, fr_sb, fn_sb, fx_ps, fx_sb, fg_ps, fc_sb, fa_ps, fg_sb, fh_sb, fy_ps, fy_sb = (
            sem(n) for n in ("sh_ps", "sh_sb", "fs_sb", "fm_sb", "fv_sb", "fr_sb", "fn_sb", "fx_ps", "fx_sb",
                             "fg_ps", "fc_sb", "fa_ps", "fg_sb", "fh_sb", "fy_ps", "fy_sb"))
        ex_ps, ex_sb = sem("ex_ps"), sem("ex_sb")
        lg_ps, rt_own, rt_act, tokwe_sb = (sem(n) for n in ("lg_ps", "rt_own", "rt_act", "tokwe_sb"))
        eg_ps, eu_ps, eg_sb, eh_sb, ey_ps, ey_sb = (
            sem(n) for n in ("eg_ps", "eu_ps", "eg_sb", "eh_sb", "ey_ps", "ey_sb"))
        table_back = sem("table_back")
        stored = sem("stored")

        def slots(eng, slot):
            def pair(b, lo, hi, nxt):
                for g in range(2):
                    slot(b, g, lambda d, g=g: lo <= g + d <= hi, nxt)
            pair(0, 0, 9, True)
            pair(1, -2, 9, True)
            with eng.Fori(2, B - 1) as b:
                pair(b, -9, 9, True)
            pair(B - 1, -9, 9, False)
            pair(B, -9, -1, False)
            pair(B + 1, -9, -3, False)

        def local_slots(eng, slot):
            def cycle(c, lo, hi):
                for s in range(4):
                    slot(c, s, lambda d, s=s: 4 * lo <= s + d < 4 * hi, lambda d: lo <= d < hi,
                         s + 1 < 4 * hi)
            for c in range(3):
                cycle(c, -c, 9)
            with eng.Fori(3, CYCLES - 1) as c:
                cycle(c, -9, 9)
            for c in range(CYCLES - 1, CYCLES + 3):
                cycle(c, -9, CYCLES - c)

        def in_layer(c):
            return 2 * (c % 4), c // 4

        LN_C, LN_D = 2, 3

        block = ctx.enter_context(nc.Block())

        @block.sync
        def _(sp):
            def load(dst, src, name, columns=False):
                sp.dma_start(dst, src, allow_slow_non_contiguous=columns).then_inc(loaded[name], 16)

            load(resid[:], t["x"].rearrange("b s d -> s b d"), "x")
            load(ident[:], t["k_ident"], "const")
            load(wa[:, 0, :], t["L0_xattn_Wq"], "wa")
            load(wa[0:CD, 1, :], t["L0_xattn_Wk"], "wa")
            load(wa[0:CD, 2, :], t["L0_xattn_Wv"], "wa")
            load(wo_a, t["L0_xattn_Wo"].rearrange("(c p) o -> p c o", p=P), "wa")
            for k in range(2):
                load(ctx_twice[:, :, k, :], t["ctx_512"].rearrange("b s d -> s b d"), "ctx")
            load(ctx_ones[:, :, 0:CD], t["ctx_512"].rearrange("b s d -> s b d"), "ctx")
            load(down[:], t["k_down"], "const")
            load(mask_row[:], t["k_mask"], "const")
            load(rot_base[:].rearrange("p a b d -> p (a b d)"), t["k_rotary"], "const")
            load(head_of[:], t["k_headof"], "const")
            load(iota[:], t["k_iota"], "const")
            load(gates[:, 0:2], t["g_xattn"].partition_broadcast(P), "small")
            load(gates[:, 2:4], t["g_ffn"].partition_broadcast(P), "small")
            load(bias_row[:, 0, :], t["L0_xattn_bo"].partition_broadcast(P), "small")
            load(bias_row[:, 1, :], t["L1_xattn_bo"].partition_broadcast(P), "small")
            for k, name in enumerate(("L0_ffn_q_scale", "L0_ffn_k_scale")):
                rows = t[name].rearrange("l d -> (l d)").partition_broadcast(P).rearrange("p (l d) -> p l d", l=DEPTH)
                load(rot_tab[:, :, k, 0, :], rows, "tab")
                for a in range(2):
                    half = HD // 2
                    load(rot_tab[:, :, k, 1, half * a:half * a + half],
                         rows[:, :, half * (1 - a):half * (2 - a)], "tab")
            for k, name in enumerate(("L1_xattn_bq", "L1_xattn_bk")):
                load(bqk_c[:, k, :], t[name].rearrange("(g p) -> p g", p=CD), "wc", True)
            load(bv_c[:], t["L1_xattn_bv"].partition_broadcast(CTX), "wc")
            load(wq_c[:], t["L1_xattn_Wq"], "wc")
            load(wo_c[:], t["L1_xattn_Wo"].rearrange("(g p) o -> p g o", p=CD), "wc")
            load(wkv_c[:, 0, :], t["L1_xattn_Wk"], "wc")
            load(wkv_c[:, 1, :], t["L1_xattn_Wv"], "wc")
            load(gate_w[:], t["L1_ffn_gate"], "wc")

            def layer(name, l):
                return t[name][bass.ds(l, 1)]

            def load_qkv(l):
                load(wbuf[:, l % 2, 0:3 * H * HD] if isinstance(l, int) else
                     wbuf[:, bass.ds(l % 2, 1), 0:3 * H * HD].rearrange("p a n -> p (a n)"),
                     layer("L0_ffn_Wqkv", l).rearrange("l d n -> d (l n)"), "wqkv")

            def load_out(l):
                dst = wbuf[:, bass.ds(l % 2, 1), 3 * H * HD:4 * H * HD].rearrange("p a (c o) -> p (a c) o", c=8)
                load(dst, layer("L0_ffn_Wo", l).rearrange("l (c p) o -> p (l c) o", p=P), "wo_b")

            def load_ffn_in(l):
                load(w1_b[:], layer("L0_ffn_W1", l).rearrange("l d n -> d (l n)"), "ffn_in")
                full = (FC - 1) * P
                b1 = layer("L0_ffn_b1", l)
                for k in range(2):
                    load(b1_b[:, k, 0:FC - 1], b1[:, k * F:k * F + full].rearrange("l (c p) -> p (l c)", p=P),
                         "ffn_in", True)
                    load(b1_b[0:FR, k, FC - 1:FC], b1[:, k * F + full:(k + 1) * F].rearrange("l p -> p l"),
                         "ffn_in", True)
                load(ln_b[:, 0:1], layer("L0_ffn_ln_g", l).rearrange("l d -> d l"), "ffn_in", True)
                load(ln_b[:, 1:2], layer("L0_ffn_ln_b", l).rearrange("l d -> d l"), "ffn_in", True)

            def load_ffn_out(l):
                w2 = layer("L0_ffn_W2", l)
                full = (FC - 1) * P
                load(w2_b[:, 0:FC - 1, :], w2[:, 0:full, :].rearrange("l (c p) o -> p (l c) o", p=P), "ffn_out")
                load(w2_b[0:FR, FC - 1, :], w2[:, full:F, :].rearrange("l p o -> p (l o)"), "ffn_out")
                load(w2_b[FR:FR + 1, FC - 1, :], layer("L0_ffn_b2", l), "ffn_out")

            def load_expert(e, k):
                for j, name in enumerate(("L1_ffn_experts_w1", "L1_ffn_experts_w3")):
                    load(w_up[:, k, j, :], t[name][bass.ds(e, 1)].rearrange("e d n -> d (e n)"), f"exp{k}")
                load(w_down[:, k, :, :],
                     t["L1_ffn_experts_w2"][bass.ds(e, 1)].rearrange("e (c p) o -> p (e c) o", p=P), f"exp{k}")

            load_qkv(0)
            load_out(0)
            load_ffn_in(0)
            load_ffn_out(0)
            load_expert(0, 0)
            load_expert(1, 1)
            sp.wait_ge(prep_ps, 2)
            sp.wait_ge(loaded["wqkv"], 16)
            load_qkv(1)
            sp.wait_ge(loaded["wo_b"], 16)
            load_out(1)
            with sp.Fori(1, DEPTH - 1) as l:
                wait_alone(sp, fh_sb, FC * 4 * l)
                load_ffn_in(l)
                wait_alone(sp, fy_ps, 4 * l)
                load_ffn_out(l)
                wait_alone(sp, v_ps, UNITS * l)
                wait_alone(sp, loaded["wqkv"], 16 * (l + 1))
                load_qkv(l + 1)
                wait_alone(sp, loaded["wo_b"], 16 * (l + 1))
                wait_alone(sp, y_ps, B0 + UNITS * l)
                load_out(l + 1)
            sp.wait_ge(fh_sb, FC * 4 * (DEPTH - 1))
            load_ffn_in(DEPTH - 1)
            sp.wait_ge(fy_ps, 4 * (DEPTH - 1))
            load_ffn_out(DEPTH - 1)
            with sp.Fori(1, E // 2) as j:
                for k in range(2):
                    sp.wait_ge(ey_ps, 4 * j + 2 * k - 2)
                    load_expert(2 * j + k, k)
            sp.wait_ge(ey_sb, 2 * E)
            sp.dma_start(out.rearrange("b s d -> s b d"), resid[:]).then_inc(stored, 16)
            sp.wait_ge(stored, 16)

        @block.tensor
        def _(pe):
            def prepare():
                landed(pe, "wa")
                landed(pe, "ctx")
                landed(pe, "const")
                for j in range(8):
                    pe.transpose(ps[:, j // 4, (j % 4) * P:(j % 4) * P + P], wa[:, 0, j * P:j * P + P], ident[:])
                for k in range(2):
                    for j in range(8):
                        pe.transpose(ps[:, 2 + k, j * CD:j * CD + CD], wa[0:CD, 1 + k, j * P:j * P + P],
                                     ident[0:CD, 0:CD])
                for b in range(B):
                    tr = pe.transpose(ps[:, 4 + b // 4, (b % 4) * CTX:(b % 4) * CTX + CTX],
                                      ctx_twice[:, b, :, :], ident[0:CTX, 0:CTX])
                tr.then_inc(prep_ps, 1)
                pe.wait_ge(prep_act, 2)
                for h in range(H):
                    r = slice(HD * (h % 2), HD * (h % 2) + HD)
                    pe.matmul(ps[:, 6 + h % 2, (h // 2) * CD:(h // 2) * CD + CD], wq_t[r, h // 2, :],
                              wkv_t[r, 0, h // 2, :], start=True, stop=True)
                for h in range(H):
                    r = slice(HD * (h % 2), HD * (h % 2) + HD)
                    mm = pe.matmul(ps[r, h // 8, (h // 2 % 4) * P:(h // 2 % 4) * P + P], wkv_t[r, 1, h // 2, :],
                                   wo_a[r, h // 2, :], start=True, stop=True)
                mm.then_inc(prep_ps, 1)
                landed(pe, "wc")
                pe.wait_ge(prep_dve, 1)
                for g in range(2):
                    for k in range(2):
                        mm = pe.matmul(ps[0:CD, 2 + 2 * g + k, 0:4 * CTX], wkv_c[:, 0, g * CD:g * CD + CD],
                                       ctx_t[0:CD, 4 * k:4 * k + 4, :], start=True, stop=True)
                mm.then_inc(prep_ps, 1)
                pe.wait_ge(prep_act, 4)
                for b in range(B):
                    mm = pe.matmul(ps[0:CTX, 6 + b // 4, (b % 4) * P:(b % 4) * P + P], ctx_t[0:CD, b, :],
                                   wkv_c[:, 1, :], start=True, stop=True)
                mm.then_inc(prep_ps, 1)

            def transpose_x(count):
                pe.wait_ge(stage_ready, count)
                pe.transpose(ps[:, T_BANK, 0:P], x_stage[:], ident[:]).then_inc(xt_ps, 1)

            def transpose_heads(n, wide):
                wait_alone(pe, o_sb, n + 1)
                if not wide:
                    tr = pe.transpose(ps[0:CD, O_BANK, 0:P], heads_out[:, 0:CD], ident[:])
                else:
                    for j in range(4):
                        tr = pe.transpose(ps[:, O_BANK, j * P:j * P + P], heads_out[:, j * P:j * P + P], ident[:])
                tr.then_inc(ot_ps, 1)

            def transpose_probs(keys):
                for h in range(GH):
                    tr = pe.transpose(ps[0:keys, T_BANK + h // 4, (h % 4) * P:(h % 4) * P + P],
                                      probs[:, h, 0:keys], ident[:])
                tr.then_inc(pt_ps, 1)

            def weigh_values(keys, width, value):
                for at in range(GH):
                    mm = pe.matmul(ps[:, V_BANK + at // 4, (at % 4) * width:(at % 4) * width + width],
                                   probs_t[0:keys, at, :], value(at), start=True, stop=True)
                mm.then_inc(pv_ps, 1)

            def cross_attention(kind, n0, b0):
                hd = HC if kind == "C" else HD

                def slot(b, g, has, nxt):
                    n = n0 + 2 * b + g
                    if has(0):
                        if g == 0:
                            pe.wait_ge(xt_sb, 2 * (b0 + b + 1))
                        if has(-2):
                            pe.wait_ge(t_sb, n - 1)
                        if has(-4):
                            pe.wait_ge(y_sb, n - 3)
                        if kind == "A":
                            for j in range(4):
                                h = g * GH + 2 * j
                                mm = pe.matmul(ps[:, QK_BANK + g, j * P:j * P + P], w_qk[:, h:h + 2, :], x_t[:],
                                               start=True, stop=True)
                        else:
                            mm = pe.matmul(ps[0:CD, QK_BANK + g, 0:P], wq_c[:, g * CD:g * CD + CD], x_t[:],
                                           start=True, stop=True)
                        mm.then_inc(t_ps, 1)
                    if has(-2):
                        pe.wait_ge(p_sb, n - 1)
                        if has(-3):
                            pe.wait_ge(pt_sb, n - 2)
                        transpose_probs(CTX)
                    if has(-3):
                        transpose_heads(n - 3, kind == "A")
                    if has(-1):
                        pe.wait_ge(t_sb, n)
                        pe.wait_ge(k_stage, n if kind == "A" else n - C0 + UNITS)
                        if has(-2):
                            pe.wait_ge(sub_sb, n - 1)
                        gs = (g - 1) % 2
                        for j in range(4):
                            for k in range(2):
                                r = slice(HD * k, HD * k + HD)
                                if kind == "A":
                                    mm = pe.matmul(ps[:, S_BANK + k, j * CTX:(j + 1) * CTX], qk_t[r, j, :],
                                                   ctx_stage[r, gs, :], start=True, stop=True)
                        if kind == "C":
                            for k in range(2):
                                mm = pe.matmul(ps[:, S_BANK + k, 0:4 * CTX], qk_t[0:CD, 0, :],
                                               kc_heads[:, gs, 4 * k:4 * k + 4, :], start=True, stop=True)
                        mm.then_inc(s_ps, 1)
                    if has(-3):
                        pe.wait_ge(ot_sb, n - 2)
                        o = ps[:, QK_BANK + 1 - g, 0:P]
                        gy = (g - 3) % 2
                        if kind == "C":
                            mm = pe.matmul(o, heads_t[0:CD, 0, :], wo_c[:, gy, :], start=True, stop=True)
                        else:
                            for j in range(4):
                                mm = pe.matmul(o, heads_t[:, j, :], w_vo[:, 4 * gy + j, :], start=(j == 0), stop=(j == 3))
                        mm.then_inc(y_ps, 1)
                    if g == 1 and nxt:
                        if has(-2):
                            pe.wait_ge(pt_sb, n - 1)
                        transpose_x(b0 + b + 2)
                    if has(-2):
                        pe.wait_ge(pt_sb, n - 1)
                        if has(-3):
                            pe.wait_ge(ot_sb, n - 2)
                        bv = bass.ds(b - 1, 1)
                        if kind == "A":
                            weigh_values(CTX, HD + 1, lambda at: ctx_ones[:, bv, :])
                        else:
                            weigh_values(CTX, GH * (HC + 1), lambda at: vc_ones[:, bv, g * GH:(g + 1) * GH, :]
                                         .rearrange("p a h d -> p a (h d)"))

                transpose_x(b0 + 1)
                slots(pe, slot)

            def local_layers():
                def slot(c, s, has, ff, nxt):
                    n = B0 + 4 * c + s
                    m = 4 * c + s
                    g = s % 2
                    b_now, l_now = in_layer(c)
                    b_last, l_last = in_layer(c - 1) if has(-4) else (0, 0)
                    x_count = B + 2 * c + s // 2 + 1
                    if has(0):
                        if s == 0:
                            pe.wait_ge(loaded["wqkv"], 16 * l_now + 16)
                        if g == 0:
                            pe.wait_ge(xt_sb, 2 * x_count)
                        if has(-1):
                            pe.wait_ge(raw_sb, m)
                            if has(-2):
                                pe.wait_ge(t_sb, n - 1)
                        side = bass.ds(l_now % 2, 1)
                        for k in range(2):
                            at = (k * H + g * GH) * HD
                            mm = pe.matmul(ps[:, QK_BANK + k, :], x_t[:], wbuf[:, side, at:at + GH * HD],
                                           start=True, stop=True)
                        mm.then_inc(qk_ps, 1)
                    if has(-2) and (ff(-2) or (s == 0 and ff(-3))):
                        pe.wait_ge(sub_sb, n - 1)
                    feed_forward(c, s, ff)
                    if has(0):
                        if has(-3):
                            pe.wait_ge(o_sb, n - 2)
                        elif has(-1):
                            pe.wait_ge(v_sb, m)
                        at = (2 * H + g * GH) * HD
                        pe.matmul(ps[:, V_BANK, :], x_t[:], wbuf[:, side, at:at + GH * HD],
                                  start=True, stop=True).then_inc(v_ps, 1)
                    if has(-3):
                        transpose_heads(n - 3, True)
                    if has(-1):
                        pe.wait_ge(un_sb, m)
                        if has(0):
                            pe.wait_ge(raw_sb, m + 1)
                        for j in range(8):
                            pair = slice(2 * (j % 4), 2 * (j % 4) + 2)
                            tr = pe.transpose(ps[:, QK_BANK + j // 4, (j % 4) * P:(j % 4) * P + P],
                                              turned[:, j // 4, pair, :], ident[:])
                        tr.then_inc(t_ps, 1)
                    if has(-2):
                        pe.wait_ge(p_sb, n - 1)
                        if has(-3):
                            pe.wait_ge(pt_sb, n - 2)
                        transpose_probs(P)
                    if has(-3):
                        layer_y = l_last if s < 3 else l_now
                        if s == 3 and has(0):
                            pe.wait_ge(loaded["wo_b"], 16 * layer_y + 16)
                        pe.wait_ge(ot_sb, n - 2)
                        if has(0):
                            pe.wait_ge(v_sb, m + 1)
                        gy = (g - 3) % 2
                        for j in range(4):
                            at = (3 * H + 8 * gy + 2 * j) * HD
                            mm = pe.matmul(ps[:, V_BANK, 0:P], heads_t[:, j, :],
                                           wbuf[:, bass.ds(layer_y % 2, 1), at:at + P], start=(j == 0), stop=(j == 3))
                        mm.then_inc(y_ps, 1)
                    if has(-1):
                        pe.wait_ge(t_sb, n)
                        if has(-2):
                            pe.wait_ge(sub_sb, n - 1)
                        if s == 0:
                            if ff(-3):
                                pe.wait_ge(fy_sb, c - 2)
                            if ff(-2):
                                pe.wait_ge(sh_sb, 2 * (c - 1))
                        elif ff(-2):
                            done, each = ((fx_sb, 1), (fc_sb, 2), (fh_sb, FC))[s - 1]
                            pe.wait_ge(done, each * (c - 1))
                        for k in range(2):
                            pe.matmul(ps[:, S_BANK + k, :], ident16[:], mask16[:], start=True, stop=False)
                        for j in range(4):
                            for k in range(2):
                                r = slice(HD * k, HD * k + HD)
                                mm = pe.matmul(ps[:, S_BANK + k, j * P:(j + 1) * P], qk_t[r, j, :], qk_t[r, 4 + j, :],
                                               start=False, stop=(j == 3))
                        mm.then_inc(s_ps, 1)
                    if g == 1 and nxt:
                        if has(-2):
                            pe.wait_ge(pt_sb, n - 1)
                        transpose_x(x_count + 1)
                    if has(-2):
                        pe.wait_ge(pt_sb, n - 1)
                        if has(0):
                            pe.wait_ge(v_sb, m + 1)
                        if has(-3):
                            pe.wait_ge(ot_sb, n - 2)
                            pe.wait_ge(y_sb, n - 2)
                        bv = b_now if s >= 2 else b_last + 1
                        weigh_values(P, HD + 1,
                                     lambda at: v_ones[:, bass.ds(bv, 1), g, 2 * (at % 4) + at // 4, :])

                def feed_forward(c, s, ff):
                    if s == 0 and ff(-3):
                        _, l_out = in_layer(c - 3)
                        pe.wait_ge(loaded["ffn_out"], (l_out + 1) * (16 * LOADS["ffn_out"]))
                        pe.wait_ge(fh_sb, FC * (c - 2))
                        for b in range(2):
                            o = ps[:, S_BANK + 1, b * P:b * P + P]
                            for k in range(FC):
                                w = P if k < FC - 1 else FR + 1
                                mm = pe.matmul(o, pair_hid[0:w, k, b * P:b * P + P], w2_b[0:w, k, :],
                                               start=(k == 0), stop=(k == FC - 1))
                        mm.then_inc(fy_ps, 1)
                    if not ff(-2):
                        return
                    b_in, l_in = in_layer(c - 2)
                    if s == 0:
                        pe.wait_ge(y_sb, B0 + 4 * (c - 1))
                        for b in range(2):
                            mm = pe.matmul(ps[:, S_BANK, b * CD:b * CD + CD], down[:],
                                           local[:, bass.ds(b_in + b, 1), CD:P], start=True, stop=True)
                        mm.then_inc(sh_ps, 1)
                    if s == 1:
                        pe.wait_ge(fn_sb, 2 * (c - 1))
                        for b in range(2):
                            tr = pe.transpose(ps[:, S_BANK, b * P:b * P + P], pair_n[:, b, :], ident[:])
                        tr.then_inc(fx_ps, 1)
                    if s >= 2:
                        off, ready = ((F, fg_ps), (0, fa_ps))[s - 2]
                        if s == 2:
                            pe.wait_ge(fx_sb, c - 1)
                        else:
                            pe.wait_ge(fc_sb, 2 * (c - 1))
                        for k in range(FC):
                            w = P if k < FC - 1 else FR
                            mm = pe.matmul(ps[0:w, S_BANK + k // 2, (k % 2) * 2 * P:(k % 2 + 1) * 2 * P],
                                           w1_b[:, off + k * P:off + k * P + w], pair_t[:], start=True, stop=True)
                        mm.then_inc(ready, 1)

                transpose_x(B + 1)
                local_slots(pe, slot)

            def experts():
                for hf in range(2):
                    pe.wait_ge(ln_out, B * LN_D + 4 * hf + 4)
                    for b in range(4):
                        tr = pe.transpose(ps[:, 6 + hf, b * P:b * P + P], normed[:, 4 * hf + b, :], ident[:])
                    tr.then_inc(ex_ps, 1)
                pe.wait_ge(ex_sb, 2)
                for b in range(B):
                    mm = pe.matmul(ps[:, 7, b * E:b * E + E], xn_t[:, b // 4, (b % 4) * P:(b % 4) * P + P], gate_w[:],
                                   start=True, stop=True)
                mm.then_inc(lg_ps, 1)

                def up(e, k, hf, first):
                    if hf == 0:
                        pe.wait_ge(loaded[f"exp{k}"], (e - k) * (8 * LOADS["exp0"]) + 16 * LOADS["exp0"])
                    for c in range(EC):
                        q = (2 * e + hf) * EC + c
                        if not (first and c < 2):
                            pe.wait_ge(eg_sb, q - 1)
                            pe.wait_ge(eh_sb, q - 1)
                        pe.matmul(ps[:, c % 2, :], w_up[:, k, 0, c * P:c * P + P], xn_t[:, hf, :],
                                  start=True, stop=True).then_inc(eg_ps, 1)
                        pe.matmul(ps[:, 2 + c % 2, :], w_up[:, k, 1, c * P:c * P + P], xn_t[:, hf, :],
                                  start=True, stop=True).then_inc(eu_ps, 1)

                def down_proj(e, k, hf, first):
                    s = 2 * e + hf
                    pe.wait_ge(eh_sb, (s + 1) * EC)
                    if not first:
                        pe.wait_ge(ey_sb, s - 1)
                    for b in range(4):
                        for c in range(EC):
                            mm = pe.matmul(ps[:, 4 + hf, b * P:b * P + P], hidden[:, hf, c, b * P:b * P + P],
                                           w_down[:, k, c, :], start=(c == 0), stop=(c == EC - 1))
                    mm.then_inc(ey_ps, 1)

                def expert_pair(e, first, last):
                    for k in range(2):
                        for hf in range(2):
                            s = 2 * k + hf
                            if not (last and s == 3):
                                ne = e + (s + 1) // 2
                                up(ne, ((s + 1) // 2) % 2, (s + 1) % 2, False)
                            down_proj(e + k, k, hf, first and s < 2)

                up(0, 0, 0, True)
                expert_pair(0, True, False)
                with pe.Fori(1, E // 2 - 1) as j:
                    expert_pair(2 * j, False, False)
                expert_pair(E - 2, False, True)

            prepare()
            pe.wait_ge(prep_act, 6)
            pe.wait_ge(prep_dve, 3)
            cross_attention("A", A0, 0)
            pe.wait_ge(const_ready, 5)
            local_layers()
            cross_attention("C", C0, B + B * DEPTH)
            experts()

        @block.scalar
        def _(act):
            def prepare():
                landed(act, "small")
                act.activation(tgate[:], gates[:], ACT.Tanh).then_inc(tg_ready, 1)
                act.wait_ge(prep_ps, 1)
                act.activation(wq_t[:].rearrange("p (a c) n -> p a (c n)", a=2), ps[:, 0:2, :], ACT.Copy)\
                   .then_inc(prep_act, 1)
                act.activation(wkv_t[:].rearrange("p k c n -> p k (c n)"), ps[:, 2:4, :], ACT.Copy)\
                   .then_inc(prep_act, 1)
                act.wait_ge(prep_ps, 2)
                act.activation(w_qk[:].rearrange("p (j a) n -> p a j n", a=2),
                               ps[:, 6:8, :].rearrange("p a (j n) -> p a j n", n=CD), ACT.Copy,
                               scale=HD ** -0.5).then_inc(prep_act, 1)
                act.activation(w_vo[:].rearrange("p (a c) n -> p a (c n)", a=2), ps[:, 0:2, :], ACT.Copy)\
                   .then_inc(prep_act, 1)
                act.wait_ge(prep_ps, 3)
                landed(act, "wc")
                for g in range(2):
                    act.activation(kc_t[:, g, :].rearrange("p (a c) -> p a c", a=2),
                                   ps[0:CD, 2 + 2 * g:4 + 2 * g, 0:4 * CTX], ACT.Identity,
                                   bias=bqk_c[:, 1, g:g + 1]).then_inc(prep_act, 1)

            def copy_x(count, shift):
                act.wait_ge(xt_ps, count)
                act.activation(x_t[0:CD, :], ps[0:CD, T_BANK, 0:P], ACT.Copy).then_inc(xt_sb, 1)
                act.activation(x_t[CD:P, shift:P], ps[CD:P, T_BANK, 0:P - shift], ACT.Copy).then_inc(xt_sb, 1)

            def copy_heads(n, has, wide):
                act.wait_ge(ot_ps, n + 1)
                if has(-4):
                    act.wait_ge(y_ps, n)
                if wide:
                    act.activation(heads_t[:].rearrange("p c n -> p (c n)"), ps[:, O_BANK, :], ACT.Copy)\
                       .then_inc(ot_sb, 1)
                else:
                    act.activation(heads_t[0:CD, 0, :], ps[0:CD, O_BANK, 0:P], ACT.Copy).then_inc(ot_sb, 1)

            def exponent(n, has, keys):
                act.wait_ge(sub_sb, n + 1)
                if has(-3):
                    act.wait_ge(pt_ps, n)
                act.activation(probs[:, :, 0:keys], shifted[:, :, 0:keys], ACT.Exp).then_inc(p_sb, 1)

            def copy_probs(n, has, keys):
                act.wait_ge(pt_ps, n + 1)
                if has(-3):
                    act.wait_ge(pv_ps, n)
                act.activation(probs_t[0:keys, :, :].rearrange("p (a c) n -> p a (c n)", a=2),
                               ps[0:keys, T_BANK:T_BANK + 2, :], ACT.Copy).then_inc(pt_sb, 1)

            def cross_attention(kind, n0, b0):
                def slot(b, g, has, nxt):
                    n = n0 + 2 * b + g
                    if has(-1):
                        act.wait_ge(t_ps, n)
                        if has(-2):
                            act.wait_ge(s_ps, n - 1)
                        gq = (g - 1) % 2
                        if kind == "A":
                            act.activation(qk_t[:, 0:4, :].rearrange("p c n -> p (c n)"), ps[:, QK_BANK + gq, :],
                                           ACT.Copy).then_inc(t_sb, 1)
                        else:
                            act.activation(qk_t[0:CD, 0, :], ps[0:CD, QK_BANK + gq, 0:P], ACT.Identity,
                                           bias=bq_scaled[:, gq:gq + 1], scale=HC ** -0.5).then_inc(t_sb, 1)
                    if has(-2):
                        exponent(n - 2, has, CTX)
                    if has(-3):
                        copy_heads(n - 3, has, kind == "A")
                    if has(-2):
                        copy_probs(n - 2, has, CTX)
                    if g == 1 and nxt:
                        copy_x(b0 + b + 2, 0)

                copy_x(b0 + 1, 0)
                slots(act, slot)

            def local_layers():
                def slot(c, s, has, ff, nxt):
                    n = B0 + 4 * c + s
                    m = 4 * c + s
                    if has(-2):
                        exponent(n - 2, has, P)
                    if has(0):
                        act.wait_ge(qk_ps, m + 1)
                        if has(-1):
                            act.wait_ge(rot_sb, 3 * m)
                            act.wait_ge(sq_sb, m)
                        act.activation(raw_qk[:].rearrange("p a h d -> p a (h d)"),
                                       ps[:, QK_BANK:QK_BANK + 2, :], ACT.Copy).then_inc(raw_sb, 1)
                        act.wait_ge(v_ps, m + 1)
                        act.activation(v_ones[:, bass.ds(in_layer(c)[0] + s // 2, 1), s % 2, :, 0:HD],
                                       ps[:, V_BANK, :].rearrange("p (a h d) -> p a h d", a=1, h=GH), ACT.Copy)\
                           .then_inc(v_sb, 1)
                    if has(-3):
                        copy_heads(n - 3, has, True)
                    if has(0):
                        if has(-1):
                            act.wait_ge(ss_sb, m)
                        act.wait_ge(raw_sb, m + 1)
                        act.activation(squares[:], raw_qk[:].rearrange("p a h d -> p (a h) d"),
                                       ACT.Square).then_inc(sq_sb, 1)
                    if has(-1):
                        act.wait_ge(t_ps, n)
                        if has(-2):
                            act.wait_ge(s_ps, n - 1)
                        act.activation(qk_t[:].rearrange("p (a c) n -> p a (c n)", a=2),
                                       ps[:, QK_BANK:QK_BANK + 2, :], ACT.Copy).then_inc(t_sb, 1)
                    if has(-2):
                        copy_probs(n - 2, has, P)
                    if s % 2 == 1 and nxt:
                        copy_x(B + 2 * c + s // 2 + 2, 1)
                    if s == 2 and ff(-2):
                        for k in range(FC):
                            w = P if k < FC - 1 else FR
                            act.wait_ge(fc_sb, 2 * (c - 1) - (1 if k < FC - 1 else 0))
                            act.activation(gelu[0:w, k, :], gelu[0:w, k, :], ACT.Gelu, bias=b1_b[0:w, 1, k:k + 1])\
                               .then_inc(fg_sb, 1)
                        if ff(-3):
                            act.wait_ge(table_back, c - 2)
                        act.activation(table_call[:], tgate[:, 0:1], ACT.Exp).then_inc(table_back, 1)

                copy_x(B + 1, 1)
                local_slots(act, slot)

            def experts():
                act.wait_ge(rt_own, 4)
                act.activation(pair_w[:, 1, :], pair_w[:, 0, :], ACT.Exp).then_inc(rt_act, 1)

                def pair(e, first):
                    for s in range(4):
                        for c in range(EC):
                            q = (2 * e + s) * EC + c
                            act.wait_ge(eg_ps, q + 1)
                            if not (first and s == 0 and c < 2):
                                act.wait_ge(eh_sb, q - 1)
                            act.activation(silu[:, c % 2, :], ps[:, c % 2, :], ACT.Silu).then_inc(eg_sb, 1)
                pair(0, True)
                with act.Fori(1, E // 2) as j:
                    pair(2 * j, False)

            prepare()
            cross_attention("A", A0, 0)
            local_layers()
            cross_attention("C", C0, B + B * DEPTH)
            experts()

        @block.gpsimd
        def _(pool):
            def norm_scale(k):
                wait_alone(pool, ln_mom, B * (k + 1))
                pool.tensor_scalar(safe_var[:], moments[:, :, 1], EPS, None, ALU.add).then_inc(ln_var, 1)
                wait_alone(pool, ln_var, k + 1)
                pool.tensor_tensor(rstd[:], safe_var[:], minus_half[:, 0:B], ALU.pow).then_inc(ln_rstd, 1)

            def stage_keys(kind, n0, k0):
                def slot(b, g, has, nxt):
                    if not has(0):
                        return
                    if has(-2):
                        wait_alone(pool, s_ps, n0 + 2 * b + g - 1)
                    if kind == "A":
                        pool.tensor_copy(ctx_stage[:, g, :], ctx_t[:, bass.ds(b, 1), :].rearrange("p a c -> p (a c)"))\
                            .then_inc(k_stage, 1)
                    else:
                        src = kc_t[:, g, bass.ds(b * CTX, CTX)].unsqueeze(1).to_broadcast([CD, GH, CTX])
                        pool.tensor_tensor(kc_heads[:, g, :, :], src,
                                           head_of[:].unsqueeze(2).to_broadcast([CD, GH, CTX]), ALU.mult)\
                            .then_inc(k_stage, 1)
                slots(pool, slot)

            def local_units():
                def slot(c, s, has, ff, nxt):
                    m = 4 * c + s
                    half = HD // 2
                    layer = bass.ds(in_layer(c)[1], 1)

                    def table(k, a, w):
                        tab = rot_tab[:, layer, :, k, a:a + w].rearrange("p l k d -> p (l k) d")
                        return tab.unsqueeze(2).to_broadcast([P, 2, GH, w])
                    if has(0):
                        wait_alone(pool, raw_sb, m + 1)
                        if has(-1):
                            wait_alone(pool, ra_sb, m)
                        pool.tensor_tensor(rot_cos[:], raw_qk[:], table(0, 0, HD), ALU.mult).then_inc(rot_sb, 1)
                        for a in range(2):
                            other = half * (1 - a)
                            pool.tensor_tensor(rot_sin[:, :, :, half * a:half * a + half],
                                               raw_qk[:, :, :, other:other + half], table(1, half * a, half),
                                               ALU.mult).then_inc(rot_sb, 1)
                    if s == 0 and ff(-2):
                        wait_alone(pool, fm_sb, 2 * (c - 1))
                        pool.tensor_scalar(pair_var[:], pair_mom[:, :, 1], EPS, None, ALU.add).then_inc(fv_sb, 1)
                        wait_alone(pool, fv_sb, c - 1)
                        pool.tensor_tensor(pair_rstd[:], pair_var[:], minus_half[:, 0:2], ALU.pow).then_inc(fr_sb, 1)
                    if has(0):
                        wait_alone(pool, ss_sb, m + 1)
                        if has(-1):
                            wait_alone(pool, un_sb, m)
                        pool.tensor_scalar(safe_sq[:], sumsq[:], 1e-24, None, ALU.max).then_inc(sg_sb, 1)
                        wait_alone(pool, sg_sb, m + 1)
                        pool.tensor_tensor(rnorm[:], safe_sq[:], minus_half[:], ALU.pow).then_inc(rn_sb, 1)
                local_slots(pool, slot)

            pool.memset(v_ones[:, :, :, :, HD:HD + 1], 1.0).then_inc(ones_ready, 1)
            pool.memset(ctx_ones[:, :, CD:CD + 1], 1.0).then_inc(ones_ready, 1)
            pool.memset(vc_ones[:, :, :, HC:HC + 1], 1.0).then_inc(ones_ready, 1)
            pool.memset(minus_half[:], -0.5).then_inc(ones_ready, 1)
            pool.wait_ge(ones_ready, 4)
            norm_scale(0)
            pool.wait_ge(prep_dve, 1)
            stage_keys("A", A0, 0)
            norm_scale(1)
            pool.wait_ge(const_ready, 5)
            local_units()
            norm_scale(LN_C)
            stage_keys("C", C0, UNITS)
            norm_scale(LN_D)

        @block.vector
        def _(dve):
            def layer_norm(k, src, dst, ready):
                ready()
                for b in range(B):
                    dve.bn_stats(stats[:, b, :], src[:, b, :]).then_inc(ln_stats, 1)
                wait_alone(dve, ln_stats, B * (k + 1))
                for b in range(B):
                    dve.bn_aggr(moments[:, b, :], stats[:, b, :]).then_inc(ln_mom, 1)
                dve.wait_ge(ln_mom, B * (k + 1))
                dve.wait_ge(ln_rstd, k + 1)
                for b in range(B):
                    dve.tensor_scalar(dst[:, b, :], src[:, b, :], moments[:, b, 0:1], rstd[:, b:b + 1],
                                      ALU.subtract, ALU.mult).then_inc(ln_out, 1)

            def stage(src, b, used):
                if not (isinstance(used, int) and used == 0):
                    dve.wait_ge(xt_ps, used)
                dve.tensor_copy(x_stage[:], src[:, bass.ds(b, 1), :].rearrange("p a d -> p (a d)"))\
                   .then_inc(stage_ready, 1)

            def divide_heads(n, has, hd):
                if hd == HD:
                    heads = [ps[:, V_BANK:V_BANK + 2, 0:4 * (hd + 1)].rearrange("p a (h d) -> p a h d", h=4)]
                else:
                    row = GH * (hd + 1)
                    heads = []
                    for a in range(2):
                        first = 4 * a * (hd + 1)
                        step = row + hd + 1
                        heads.append(ps[:, V_BANK + a:V_BANK + a + 1, first:first + 4 * step]
                                     .rearrange("p a (h d) -> p a h d", h=4)[:, :, :, 0:hd + 1])
                size = 2 // len(heads)
                dve.wait_ge(pv_ps, n + 1)
                for a, part in enumerate(heads):
                    ins = dve.reciprocal(rsum[:, a * 4:(a + size) * 4].rearrange("p (a h d) -> p a h d", a=size, d=1),
                                         part[:, :, :, hd:hd + 1])
                ins.then_inc(rs_sb, 1)
                dve.wait_ge(rs_sb, n + 1)
                if has(-4):
                    dve.wait_ge(ot_ps, n)
                order = "p (a h d) -> p a h d" if hd == HC else "p (h a d) -> p a h d"
                for a, part in enumerate(heads):
                    ins = dve.tensor_tensor(heads_out[:, a * 4 * hd:(a + size) * 4 * hd].rearrange(order, a=size, h=4),
                                            part[:, :, :, 0:hd],
                                            rsum[:, a * 4:(a + size) * 4].rearrange("p (a h) -> p a h", a=size)
                                            .unsqueeze(3).to_broadcast([P, size, 4, hd]), ALU.mult)
                ins.then_inc(o_sb, 1)

            def subtract_max(n, has, keys):
                dve.wait_ge(s_ps, n + 1)
                scores = ps[:, S_BANK:S_BANK + 2, 0:4 * keys].rearrange("p a (h k) -> p a h k", h=4)
                dve.tensor_reduce(row_max[:].rearrange("p (a h) -> p a h", a=2), scores, AX.X, ALU.max)\
                   .then_inc(max_sb, 1)
                dve.wait_ge(max_sb, n + 1)
                if has(-3):
                    dve.wait_ge(p_sb, n)
                dve.tensor_tensor(shifted[:, :, 0:keys].rearrange("p (a h) k -> p a h k", a=2), scores,
                                  row_max[:].rearrange("p (a h) -> p a h", a=2).unsqueeze(3)
                                  .to_broadcast([P, 2, 4, keys]), ALU.subtract).then_inc(sub_sb, 1)

            def cross_attention(kind, n0, b0, src):
                hd = HC if kind == "C" else HD

                def slot(b, g, has, nxt):
                    n = n0 + 2 * b + g
                    if has(-3):
                        divide_heads(n - 3, has, hd)
                    if g == 1 and nxt:
                        stage(src, b + 1, b0 + b + 1)
                    if has(-1):
                        subtract_max(n - 1, lambda d: has(d + 1), CTX)
                    if has(-3):
                        dve.wait_ge(y_ps, n - 2)
                        if has(-4):
                            dve.wait_ge(y_sb, n - 3)
                        k = 0 if kind == "A" else 1
                        x = resid[:, bass.ds(b + (g - 3) // 2, 1), :]
                        dve.scalar_tensor_tensor(x, ps[:, QK_BANK + 1 - g, 0:P].rearrange("p (a d) -> p a d", a=1),
                                                 tgate[:, k:k + 1], x, ALU.mult, ALU.add).then_inc(y_sb, 1)

                stage(src, 0, b0)
                slots(dve, slot)

            def local_layers():
                def slot(c, s, has, ff, nxt):
                    n = B0 + 4 * c + s
                    m = 4 * c + s
                    b_now, _ = in_layer(c)
                    b_last, _ = in_layer(c - 1) if has(-4) else (0, 0)
                    if has(-3):
                        divide_heads(n - 3, has, HD)
                    if has(-1):
                        dve.wait_ge(rn_sb, m)
                        dve.wait_ge(ra_sb, m)
                        dve.tensor_tensor(turned[:], turned[:], rnorm[:].rearrange("p (a h) -> p a h", a=2)
                                          .unsqueeze(3).to_broadcast([P, 2, GH, HD]), ALU.mult).then_inc(un_sb, 1)
                    feed_forward(c, s, ff)
                    if has(0):
                        dve.wait_ge(sq_sb, m + 1)
                        if has(-1):
                            dve.wait_ge(rn_sb, m)
                        dve.tensor_reduce(sumsq[:], squares[:], AX.X, ALU.add).then_inc(ss_sb, 1)
                    if has(-3):
                        dve.wait_ge(y_ps, n - 2)
                        if has(-4):
                            dve.wait_ge(y_sb, n - 3)
                        x = local[:, bass.ds(b_now if s == 3 else b_last + (s + 1) // 2, 1), :]
                        dve.tensor_tensor(x, ps[:, V_BANK, 0:P].rearrange("p (a d) -> p a d", a=1), x, ALU.add)\
                           .then_inc(y_sb, 1)
                    if s == 1 and nxt:
                        stage(local, b_now + 1, B + 2 * c + 1)
                    if s == 3 and nxt:
                        if ff(-3):
                            dve.wait_ge(fy_sb, c - 2)
                        stage(local, in_layer(c + 1)[0], B + 2 * c + 2)
                    if has(0):
                        dve.wait_ge(rot_sb, 3 * (m + 1))
                        if has(-1):
                            dve.wait_ge(t_ps, B0 + m)
                        dve.tensor_tensor(turned[:], rot_cos[:], rot_sin[:], ALU.add).then_inc(ra_sb, 1)
                    if has(-1):
                        subtract_max(n - 1, lambda d: has(d + 1), P)
                    if s == 0 and ff(-2):
                        dve.wait_ge(fr_sb, c - 1)
                        for b in range(2):
                            dve.tensor_scalar(pair_n[:, b, :], pair_n[:, b, :], pair_mom[:, b, 0:1],
                                              pair_rstd[:, b:b + 1], ALU.subtract, ALU.mult).then_inc(fn_sb, 1)

                def feed_forward(c, s, ff):
                    if s == 0 and ff(-3):
                        dve.wait_ge(fy_ps, c - 2)
                        x = local[:, bass.ds(in_layer(c - 3)[0], 2), :]
                        dve.tensor_tensor(x, ps[:, S_BANK + 1, 0:2 * P].rearrange("p (b d) -> p b d", b=2), x, ALU.add)\
                           .then_inc(fy_sb, 1)
                    if not ff(-2):
                        return
                    b_in, l_in = in_layer(c - 2)
                    if s == 0:
                        x = local[:, bass.ds(b_in, 2), 0:CD]
                        dve.wait_ge(y_sb, B0 + 4 * (c - 1))
                        dve.tensor_copy(pair_n[:, :, 0:CD], x).then_inc(sh_sb, 1)
                        dve.wait_ge(sh_ps, c - 1)
                        dve.tensor_copy(pair_n[:, :, CD:P], ps[:, S_BANK, 0:2 * CD].rearrange("p (b d) -> p b d", b=2))\
                           .then_inc(sh_sb, 1)
                        dve.wait_ge(sh_sb, 2 * (c - 1))
                        for b in range(2):
                            dve.bn_stats(pair_stats[:, b, :], pair_n[:, b, :]).then_inc(fs_sb, 1)
                        wait_alone(dve, fs_sb, 2 * (c - 1))
                        for b in range(2):
                            dve.bn_aggr(pair_mom[:, b, :], pair_stats[:, b, :]).then_inc(fm_sb, 1)
                    if s == 1:
                        dve.wait_ge(loaded["ffn_in"], (l_in + 1) * (16 * LOADS["ffn_in"]))
                        dve.wait_ge(fx_ps, c - 1)
                        dve.tensor_scalar(pair_t[:], ps[:, S_BANK, 0:2 * P], ln_b[:, 0:1], ln_b[:, 1:2],
                                          ALU.mult, ALU.add).then_inc(fx_sb, 1)
                    if s == 2:
                        dve.wait_ge(fg_ps, c - 1)
                        if ff(-3):
                            dve.wait_ge(fh_sb, FC * (c - 2))
                        dve.tensor_copy(gelu[:, 0:2, :].rearrange("p k n -> p (k n)"), ps[:, S_BANK, :])\
                           .then_inc(fc_sb, 1)
                        dve.tensor_copy(gelu[0:FR, 2, :], ps[0:FR, S_BANK + 1, 0:2 * P]).then_inc(fc_sb, 1)
                    if s == 3:
                        dve.wait_ge(fa_ps, c - 1)
                        dve.wait_ge(fg_sb, FC * (c - 1))
                        for k in range(FC):
                            w = P if k < FC - 1 else FR
                            dve.scalar_tensor_tensor(pair_hid[0:w, k, :],
                                                     ps[0:w, S_BANK + k // 2, (k % 2) * 2 * P:(k % 2 + 1) * 2 * P],
                                                     b1_b[0:w, 0, k:k + 1], gelu[0:w, k, :], ALU.add, ALU.mult)\
                               .then_inc(fh_sb, 1)

                stage(local, 0, B)
                local_slots(dve, slot)

            def add_bias(k, done):
                dve.scalar_tensor_tensor(resid[:], bias_row[:, k, :].unsqueeze(1).to_broadcast([P, B, P]),
                                         tgate[:, k:k + 1], resid[:], ALU.mult, ALU.add).then_inc(resid_done, 1)
                dve.wait_ge(resid_done, done)

            def route():
                done = [0]

                def own(ins):
                    done[0] += 1
                    ins.then_inc(rt_own, 1)
                    return done[0]
                dve.wait_ge(lg_ps, 1)
                n = own(dve.tensor_copy(logits[:].rearrange("p b e -> p (b e)"), ps[:, 7, 0:B * E]))
                dve.wait_ge(rt_own, n)
                for b in range(B):
                    ins = dve.max(top[:, b, :], logits[:, b, :])
                n = own(ins)
                dve.wait_ge(rt_own, n)
                for b in range(B):
                    ins = dve.max_index(top_at[:, b, :], top[:, b, :], logits[:, b, :])
                n = own(ins)
                dve.wait_ge(rt_own, n)
                n = own(dve.tensor_tensor(pair_w[:, 0, :], top[:, :, 1], top[:, :, 0], ALU.subtract))
                n = own(dve.tensor_copy(top_atf[:], top_at[:]))
                dve.wait_ge(rt_act, 1)
                n = own(dve.tensor_scalar(pair_w[:, 2, :], pair_w[:, 1, :], 1.0, None, ALU.add))
                dve.wait_ge(rt_own, n)
                n = own(dve.reciprocal(pair_w[:, 2, :], pair_w[:, 2, :]))
                dve.wait_ge(rt_own, n)
                n = own(dve.tensor_scalar(pair_w[:, 2, :], pair_w[:, 2, :], tgate[:, 3:4], None, ALU.mult))
                dve.wait_ge(rt_own, n)
                n = own(dve.tensor_tensor(pair_w[:, 3, :], pair_w[:, 2, :], pair_w[:, 1, :], ALU.mult))
                dve.wait_ge(rt_own, n)
                for k in range(2):
                    for b in range(B):
                        ins = dve.tensor_scalar(tok_w[:, k, b, :], iota[:], top_atf[:, b, k:k + 1],
                                                pair_w[:, 2 + k, b:b + 1], ALU.is_equal, ALU.mult)
                n = own(ins)
                dve.wait_ge(rt_own, n)
                n = own(dve.tensor_tensor(tok_w[:, 2, :, :], tok_w[:, 0, :, :], tok_w[:, 1, :, :], ALU.add))
                dve.wait_ge(rt_own, n)

            def experts():
                for hf in range(2):
                    dve.wait_ge(ex_ps, hf + 1)
                    dve.tensor_copy(xn_t[:, hf, :], ps[:, 6 + hf, :]).then_inc(ex_sb, 1)
                route()

                def multiply(e, hf):
                    for c in range(EC):
                        q = (2 * e + hf) * EC + c
                        dve.wait_ge(eu_ps, q + 1)
                        dve.wait_ge(eg_sb, q + 1)
                        dve.tensor_tensor(hidden[:, hf, c, :], ps[:, 2 + c % 2, :], silu[:, c % 2, :], ALU.mult)\
                           .then_inc(eh_sb, 1)

                def weigh(e, k, hf, first):
                    s = 2 * e + hf
                    if hf == 0:
                        dve.tensor_copy(tok_we[:, k, :], tok_w[:, 2, :, bass.ds(e, 1)].rearrange("p b e -> p (b e)"))\
                           .then_inc(tokwe_sb, 1)
                        dve.wait_ge(tokwe_sb, e + 1)
                    dve.wait_ge(ey_ps, s + 1)
                    if not first:
                        dve.wait_ge(ey_sb, s - 1)
                    for b in range(4):
                        x = resid[:, 4 * hf + b, :]
                        ins = dve.scalar_tensor_tensor(x, ps[:, 4 + hf, b * P:b * P + P],
                                                       tok_we[:, k, 4 * hf + b:4 * hf + b + 1], x, ALU.mult, ALU.add)
                    ins.then_inc(ey_sb, 1)

                def expert_pair(e, first, last):
                    for k in range(2):
                        for hf in range(2):
                            s = 2 * k + hf
                            if not (last and s == 3):
                                multiply(e + (s + 1) // 2, (s + 1) % 2)
                            weigh(e + k, k, hf, first and s < 2)

                multiply(0, 0)
                expert_pair(0, True, False)
                with dve.Fori(1, E // 2 - 1) as j:
                    expert_pair(2 * j, False, False)
                expert_pair(E - 2, False, True)

            layer_norm(0, resid, normed, lambda: landed(dve, "x"))
            landed(dve, "const")
            dve.tensor_copy(ident16[:], ident[:]).then_inc(const_ready, 1)
            dve.tensor_copy(mask16[:], mask_row[:].unsqueeze(1).to_broadcast([P, 4, P])).then_inc(const_ready, 1)
            dve.memset(pair_hid[:, FC - 1, :], 1.0).then_inc(const_ready, 1)
            landed(dve, "tab")
            dve.tensor_tensor(rot_tab[:].rearrange("p l a b d -> p l (a b d)"),
                              rot_tab[:].rearrange("p l a b d -> p l (a b d)"),
                              rot_base[:].rearrange("p a b d -> p (a b d)").unsqueeze(1)
                              .to_broadcast([P, DEPTH, 4 * HD]), ALU.mult).then_inc(const_ready, 1)
            dve.wait_ge(prep_ps, 1)
            dve.tensor_copy(ctx_t[:].rearrange("p (a b) c -> p a (b c)", a=2), ps[:, 4:6, 0:4 * CTX])\
               .then_inc(prep_dve, 1)
            landed(dve, "wc")
            dve.tensor_scalar(bq_scaled[:], bqk_c[:, 0, :], HC ** -0.5, None, ALU.mult).then_inc(prep_dve, 1)
            dve.wait_ge(prep_ps, 4)
            dve.wait_ge(ones_ready, 4)
            dve.tensor_tensor(vc_ones[:, :, :, 0:HC].rearrange("p (a b) h d -> p a b h d", a=1)[:, 0],
                              ps[0:CTX, 6:8, :].rearrange("p a (b h d) -> p (a b) h d", b=4, h=H),
                              bv_c[:].rearrange("p (h d) -> p h d", h=H).unsqueeze(1).to_broadcast([CTX, B, H, HC]),
                              ALU.add).then_inc(prep_dve, 1)
            dve.wait_ge(tg_ready, 1)
            dve.wait_ge(ln_out, B)
            cross_attention("A", A0, 0, normed)
            dve.wait_ge(y_sb, UNITS)
            dve.memset(x_t[CD:P, 0:1], 0.0).then_inc(const_ready, 1)
            add_bias(0, 1)
            layer_norm(1, resid, local, lambda: None)
            dve.wait_ge(ln_out, 2 * B)
            local_layers()
            dve.wait_ge(fy_sb, CYCLES)
            dve.scalar_tensor_tensor(resid[:], local[:], tgate[:, 2:3], resid[:], ALU.mult, ALU.add)\
               .then_inc(resid_done, 1)
            layer_norm(LN_C, resid, normed, lambda: dve.wait_ge(resid_done, 2))
            dve.wait_ge(ln_out, B * (LN_C + 1))
            cross_attention("C", C0, B + B * DEPTH, normed)
            dve.wait_ge(y_sb, C0 + UNITS)
            add_bias(1, 3)
            layer_norm(LN_D, resid, normed, lambda: None)
            experts()


_INS = ["x", "ctx_512", "g_xattn", "g_ffn",
        "L0_xattn_Wq", "L0_xattn_Wk", "L0_xattn_Wv", "L0_xattn_Wo", "L0_xattn_bo",
        "L0_ffn_Wqkv", "L0_ffn_q_scale", "L0_ffn_k_scale", "L0_ffn_Wo", "L0_ffn_ln_g", "L0_ffn_ln_b",
        "L0_ffn_W1", "L0_ffn_b1", "L0_ffn_W2", "L0_ffn_b2",
        "L1_xattn_Wq", "L1_xattn_bq", "L1_xattn_Wk", "L1_xattn_bk", "L1_xattn_Wv", "L1_xattn_bv",
        "L1_xattn_Wo", "L1_xattn_bo",
        "L1_ffn_gate", "L1_ffn_experts_w1", "L1_ffn_experts_w2", "L1_ffn_experts_w3"]


def kernel(**inputs):
    import concourse.bacc as bacc
    from concourse.bass_utils import run_bass_kernel_spmd

    nc = bacc.Bacc("TRN2", target_bir_lowering=False, num_devices=1)
    arrays = {f"in_{name}_dram": np.ascontiguousarray(inputs[name]) for name in _INS}
    arrays.update({f"in_{name}_dram": value for name, value in constants().items()})
    t = {name[3:-5]: nc.dram_tensor(name, a.shape, mybir.dt.from_np(a.dtype), kind="ExternalInput").ap()
         for name, a in arrays.items()}
    out = nc.dram_tensor("out_0_dram", (B, P, P), F32, kind="ExternalOutput").ap()
    build(nc, t, out)
    r = run_bass_kernel_spmd(nc, [arrays], core_ids=[0])
    return r.results[0]["out_0_dram"]
```

```python
from contextlib import ExitStack

import numpy as np

import concourse.bass as bass
from concourse import mybir

F32 = mybir.dt.float32
F32R = mybir.dt.float32r
BF16 = mybir.dt.bfloat16
U32 = mybir.dt.uint32
ALU = mybir.AluOpType
ACT = mybir.ActivationFunctionType
AX = mybir.AxisListType

P = 128
B = 8
CTX = 77
CD = 64
H = 16
GH = 8
HD = 64
HC = 8
DEPTH = 6
F = 341
FC = (F + P - 1) // P
FR = F - (FC - 1) * P
E = 8
EH = 512
EC = EH // P
UNITS = 2 * B
WINDOW = 32
MASKED = -1e30
EPS = 1e-5
QKV = 3 * H * HD

CYCLES = UNITS * DEPTH // 4

A0 = 0
B0 = UNITS
C0 = UNITS * (1 + DEPTH)


def rotary_tables():
    half = np.arange(0, HD, 2, dtype=np.float32)
    inv_freq = 1.0 / 10000.0 ** (half / HD)
    t = np.arange(P, dtype=np.float32)
    freqs = (t[:, None] * inv_freq[None, :]).astype(np.float32)
    freqs = np.concatenate([freqs, freqs], -1)
    base = (half + 0.4 * HD) / (1.4 * HD)
    scale = base[None, :] ** ((t - P // 2) / (WINDOW // 2))[:, None]
    scale = np.concatenate([scale, scale], -1).astype(np.float32)
    sign = np.where(np.arange(HD) < HD // 2, -1.0, 1.0).astype(np.float32)
    cos, sin = np.cos(freqs), np.sin(freqs) * sign
    q = 8.0 * scale
    k = 1.0 / scale
    return np.stack([cos * q, sin * q, cos * k, sin * k], 1).astype(np.float32)


def band_mask():
    i = np.arange(P)[:, None]
    j = np.arange(P)[None, :]
    return np.where((j <= i) & (j >= i - WINDOW), 0.0, MASKED).astype(np.float32)


def constants():
    head_of = (np.arange(CD)[:, None] // HC == np.arange(GH)[None, :]).astype(np.float32)
    return {
        "k_ident": np.eye(P, dtype=np.float32),
        "k_down": np.eye(P, k=1, dtype=np.float32),
        "k_mask": band_mask(),
        "k_rotary": rotary_tables().reshape(P, 4 * HD),
        "k_headof": head_of,
        "k_iota": np.tile(np.arange(E, dtype=np.float32), (P, 1)),
    }


def build(nc, t, out):
    ctx = ExitStack()
    with ctx:
        def sb(name, shape, dt=F32):
            return ctx.enter_context(nc.sbuf_tensor(name, shape, dt))

        def sem(name):
            return ctx.enter_context(nc.semaphore(name))

        ident = sb("ident", [P, P])
        ident16 = sb("ident16", [P, P], BF16)
        down = sb("down", [P, P])
        mask_row = sb("mask_row", [P, P])
        mask16 = sb("mask16", [P, 4, P], BF16)
        rot_base = sb("rot_base", [P, 2, 2, HD])
        rot_tab = sb("rot_tab", [P, DEPTH, 2, 2, HD])
        head_of = sb("head_of", [CD, GH])
        iota = sb("iota", [P, E])
        gates = sb("gates", [P, 4])
        tgate = sb("tgate", [P, 4])
        bias_row = sb("bias_row", [P, 2, P])
        resid = sb("resid", [P, B, P])
        local = sb("local", [P, B, P])
        normed = sb("normed", [P, B, P])
        stats = sb("stats", [P, B, 6])
        moments = sb("moments", [P, B, 2])
        rstd = sb("rstd", [P, B])
        ctx_ones = sb("ctx_ones", [CTX, B, CD + 1])
        ctx_twice = sb("ctx_twice", [CTX, B, 2, CD])
        ctx_t = sb("ctx_t", [P, B, CTX])
        raw = sb("raw", [P, QKV])
        wo_b = sb("wo_b", [P, 2, H * HD])
        wa = raw[:].rearrange("p (k n) -> p k n", k=3)
        wo_a = wo_b[:, 1, :].rearrange("p (c o) -> p c o", c=8)
        w_up = raw[:, 0:4 * EH].rearrange("p (k j n) -> p k j n", k=2, j=2)
        w_down = raw[:, 4 * EH:6 * EH].rearrange("p (k c n) -> p k c n", k=2, c=EC)
        w_high = sb("w_high", [P, QKV], F32R)
        w_low = sb("w_low", [P, QKV], F32R)
        up_high, up_low = (w[:, 0:4 * EH].rearrange("p (k j n) -> p k j n", k=2, j=2) for w in (w_high, w_low))
        xn_high, xn_low = (w[:, 4 * EH:6 * EH].rearrange("p (f n) -> p f n", f=2) for w in (w_high, w_low))
        wq_t = sb("wq_t", [P, 8, P])
        wkv_t = sb("wkv_t", [P, 2, 8, CD])
        w_qk = sb("w_qk", [P, H, CD])
        w_vo = sb("w_vo", [P, 8, P])
        w1_b = sb("w1_b", [P, 2 * F])
        w2_b = sb("w2_b", [P, FC, P])
        b1_b = sb("b1_b", [P, 2, FC])
        ln_b = sb("ln_b", [P, 2])
        wq_c = sb("wq_c", [P, P])
        wo_c = sb("wo_c", [CD, 2, P])
        wkv_c = sb("wkv_c", [CD, 2, P])
        bqk_c = sb("bqk_c", [CD, 2, 2])
        bq_scaled = sb("bq_scaled", [CD, 2])
        bv_c = sb("bv_c", [CTX, P])
        gate_w = sb("gate_w", [P, E])
        x_stage = sb("x_stage", [P, P])
        x_stages = sb("x_stages", [P, 2, P], F32R)
        x_t = sb("x_t", [P, P])
        x_parts = sb("x_parts", [P, 2, P], F32R)
        space = sb("space", [P, 4, 2 * GH * HD])
        squares = space[:, 0, :].rearrange("p (h d) -> p h d", d=HD)
        safe_sq = sb("safe_sq", [P, 2 * GH])
        safe_var = sb("safe_var", [P, B])
        minus_half = sb("minus_half", [P, 2 * GH])
        raw_qk, rot_cos, rot_sin = (
            space[:, j, :].rearrange("p (k h d) -> p k h d", k=2, h=GH) for j in (1, 2, 3))
        hidden = space[:, :, :].rearrange("p (f a) (b n) -> p f (a b) n", f=2, b=2)
        sumsq = sb("sumsq", [P, 2 * GH])
        rnorm = sb("rnorm", [P, 2 * GH])
        qk_t = sb("qk_t", [P, 8, P])
        v_ones = sb("v_ones", [P, B, 2, GH, HD + 1])
        ctx_stage = sb("ctx_stage", [P, 2, CTX])
        kc_t = sb("kc_t", [CD, 2, B * CTX])
        kc_heads = sb("kc_heads", [CD, 2, GH, CTX])
        vc_ones = sb("vc_ones", [CTX, B, H, HC + 1])
        row_max = sb("row_max", [P, GH])
        shifted = sb("shifted", [P, GH, P])
        x_router = shifted
        probs = sb("probs", [P, GH, P])
        probs_t = sb("probs_t", [P, GH, P])
        rsum = sb("rsum", [P, GH])
        heads_out = sb("heads_out", [P, GH * HD])
        heads_t = sb("heads_t", [P, 4, P])
        pair_n = sb("pair_n", [P, 2, P])
        pair_stats = sb("pair_stats", [P, 2, 6])
        pair_mom = sb("pair_mom", [P, 2, 2])
        pair_var = sb("pair_var", [P, 2])
        pair_rstd = sb("pair_rstd", [P, 2])
        pair_t = sb("pair_t", [P, 2 * P])
        gelu = sb("gelu", [P, FC, 2 * P])
        table_call = sb("table_call", [P, 1])
        pair_hid = sb("pair_hid", [P, FC, 2 * P])
        silu = sb("silu", [P, 2, 4 * P])
        turned = silu[:].rearrange("p k (h d) -> p k h d", h=GH)
        logits = sb("logits", [P, B, E])
        top = sb("top", [P, B, 8])
        top_at = sb("top_at", [P, B, 8], U32)
        top_atf = sb("top_atf", [P, B, 8])
        pair_w = sb("pair_w", [P, 4, B])
        tok_w = sb("tok_w", [P, 3, B, E])
        tok_we = sb("tok_we", [P, 2, B])

        ps = ctx.enter_context(nc.psum_tensor("ps", [P, 8, 512], F32))
        QK_BANK, S_BANK, T_BANK, V_BANK, O_BANK = 0, 2, 4, 6, 7

        LOADS = {"ident": 1, "const": 5, "x": 1, "ctx": 3, "wa": 4, "small": 4, "tab": 6, "wc": 8, "wqkv": 1, "wo_b": 1,
                 "ffn_in": 7, "ffn_out": 3, "up0": 2, "up1": 2, "down0": 1, "down1": 1}
        loaded = {n: sem("loaded_" + n) for n in LOADS}

        def landed(eng, name, times=1):
            eng.wait_ge(loaded[name], 16 * LOADS[name] * times)

        let_pass = sem("let_pass")

        def wait_alone(eng, semaphore, value):
            eng.wait_ge(semaphore, value)
            eng.sem_inc(let_pass, 1)

        const_ready = sem("const_ready")
        ones_ready = sem("ones_ready")
        tg_ready = sem("tg_ready")
        ln_var, sg_sb = sem("ln_var"), sem("sg_sb")
        prep_ps, prep_act, prep_dve = sem("prep_ps"), sem("prep_act"), sem("prep_dve")
        ln_stats, ln_mom, ln_rstd, ln_out = sem("ln_stats"), sem("ln_mom"), sem("ln_rstd"), sem("ln_out")
        resid_done = sem("resid_done")
        stage_ready = sem("stage_ready")
        stage_high = sem("stage_high")
        high_sb, low_sb, e_split = sem("high_sb"), sem("low_sb"), sem("e_split")
        xt_ps, xt_sb = sem("xt_ps"), sem("xt_sb")
        k_stage = sem("k_stage")
        qk_ps, v_ps, v_sb = sem("qk_ps"), sem("v_ps"), sem("v_sb")
        raw_sb, sq_sb, ss_sb, rn_sb, un_sb, rot_sb, ra_sb = (
            sem(n) for n in ("raw_sb", "sq_sb", "ss_sb", "rn_sb", "un_sb", "rot_sb", "ra_sb"))
        t_ps, t_sb = sem("t_ps"), sem("t_sb")
        s_ps, max_sb, sub_sb, p_sb = (sem(n) for n in ("s_ps", "max_sb", "sub_sb", "p_sb"))
        pt_ps, pt_sb, pv_ps, rs_sb, o_sb = (sem(n) for n in ("pt_ps", "pt_sb", "pv_ps", "rs_sb", "o_sb"))
        ot_ps, ot_sb, y_ps, y_sb = (sem(n) for n in ("ot_ps", "ot_sb", "y_ps", "y_sb"))
        sh_ps, sh_sb, fs_sb, fm_sb, fv_sb, fr_sb, fn_sb, fx_ps, fx_sb, fg_ps, fc_sb, fa_ps, fg_sb, fh_sb, fy_ps, fy_sb = (
            sem(n) for n in ("sh_ps", "sh_sb", "fs_sb", "fm_sb", "fv_sb", "fr_sb", "fn_sb", "fx_ps", "fx_sb",
                             "fg_ps", "fc_sb", "fa_ps", "fg_sb", "fh_sb", "fy_ps", "fy_sb"))
        ex_ps, ex_sb = sem("ex_ps"), sem("ex_sb")
        xr_sb = sem("xr_sb")
        lg_ps, rt_own, rt_act, tokwe_sb = (sem(n) for n in ("lg_ps", "rt_own", "rt_act", "tokwe_sb"))
        eg_ps, eu_ps, eg_sb, eh_sb, ey_ps, ey_sb = (
            sem(n) for n in ("eg_ps", "eu_ps", "eg_sb", "eh_sb", "ey_ps", "ey_sb"))
        table_back = sem("table_back")
        stored = sem("stored")

        def slots(eng, slot):
            def pair(b, lo, hi, nxt):
                for g in range(2):
                    slot(b, g, lambda d, g=g: lo <= g + d <= hi, nxt)
            pair(0, 0, 9, True)
            pair(1, -2, 9, True)
            with eng.Fori(2, B - 1) as b:
                pair(b, -9, 9, True)
            pair(B - 1, -9, 9, False)
            pair(B, -9, -1, False)
            pair(B + 1, -9, -3, False)

        def local_slots(eng, slot):
            def cycle(c, lo, hi, more):
                for s in range(4):
                    slot(c, s, lambda d, s=s: 4 * lo <= s + d < 4 * hi, lambda d: lo <= d < hi,
                         s + 1 < 4 * hi, more)
            for c in range(3):
                cycle(c, -c, 9, 0)
            with eng.Fori(1, DEPTH) as l:
                for k in range(4):
                    cycle(4 * l - 1 + k, -9, 9, (1, 2, 0, 0)[k])
            for c in range(CYCLES - 1, CYCLES + 3):
                cycle(c, -9, CYCLES - c, 0)

        def weight_groups(w):
            return w[:].rearrange("p (k g n) -> p g k n", k=3, g=2)

        def in_layer(c):
            return 2 * (c % 4), c // 4

        LN_C, LN_D = 2, 3

        block = ctx.enter_context(nc.Block())

        @block.sync
        def _(sp):
            def load(dst, src, name, columns=False):
                sp.dma_start(dst, src, allow_slow_non_contiguous=columns).then_inc(loaded[name], 16)

            load(resid[:], t["x"].rearrange("b s d -> s b d"), "x")
            load(ident[:], t["k_ident"], "ident")
            load(wa[:, 0, :], t["L0_xattn_Wq"], "wa")
            load(wa[0:CD, 1, :], t["L0_xattn_Wk"], "wa")
            load(wa[0:CD, 2, :], t["L0_xattn_Wv"], "wa")
            load(wo_a, t["L0_xattn_Wo"].rearrange("(c p) o -> p c o", p=P), "wa")
            for k in range(2):
                load(ctx_twice[:, :, k, :], t["ctx_512"].rearrange("b s d -> s b d"), "ctx")
            load(ctx_ones[:, :, 0:CD], t["ctx_512"].rearrange("b s d -> s b d"), "ctx")
            load(down[:], t["k_down"], "const")
            load(mask_row[:], t["k_mask"], "const")
            load(rot_base[:].rearrange("p a b d -> p (a b d)"), t["k_rotary"], "const")
            load(head_of[:], t["k_headof"], "const")
            load(iota[:], t["k_iota"], "const")
            load(gates[:, 0:2], t["g_xattn"].partition_broadcast(P), "small")
            load(gates[:, 2:4], t["g_ffn"].partition_broadcast(P), "small")
            load(bias_row[:, 0, :], t["L0_xattn_bo"].partition_broadcast(P), "small")
            load(bias_row[:, 1, :], t["L1_xattn_bo"].partition_broadcast(P), "small")
            for k, name in enumerate(("L0_ffn_q_scale", "L0_ffn_k_scale")):
                rows = t[name].rearrange("l d -> (l d)").partition_broadcast(P).rearrange("p (l d) -> p l d", l=DEPTH)
                load(rot_tab[:, :, k, 0, :], rows, "tab")
                for a in range(2):
                    half = HD // 2
                    load(rot_tab[:, :, k, 1, half * a:half * a + half],
                         rows[:, :, half * (1 - a):half * (2 - a)], "tab")
            for k, name in enumerate(("L1_xattn_bq", "L1_xattn_bk")):
                load(bqk_c[:, k, :], t[name].rearrange("(g p) -> p g", p=CD), "wc", True)
            load(bv_c[:], t["L1_xattn_bv"].partition_broadcast(CTX), "wc")
            load(wq_c[:], t["L1_xattn_Wq"], "wc")
            load(wo_c[:], t["L1_xattn_Wo"].rearrange("(g p) o -> p g o", p=CD), "wc")
            load(wkv_c[:, 0, :], t["L1_xattn_Wk"], "wc")
            load(wkv_c[:, 1, :], t["L1_xattn_Wv"], "wc")
            load(gate_w[:], t["L1_ffn_gate"], "wc")

            def layer(name, l):
                return t[name][bass.ds(l, 1)]

            def load_qkv(l):
                load(raw[:], layer("L0_ffn_Wqkv", l).rearrange("l d n -> d (l n)"), "wqkv")

            def load_out(l):
                dst = wo_b[:, bass.ds(l % 2, 1), :].rearrange("p a (c o) -> p (a c) o", c=8)
                load(dst, layer("L0_ffn_Wo", l).rearrange("l (c p) o -> p (l c) o", p=P), "wo_b")

            def load_ffn_in(l):
                load(w1_b[:], layer("L0_ffn_W1", l).rearrange("l d n -> d (l n)"), "ffn_in")
                full = (FC - 1) * P
                b1 = layer("L0_ffn_b1", l)
                for k in range(2):
                    load(b1_b[:, k, 0:FC - 1], b1[:, k * F:k * F + full].rearrange("l (c p) -> p (l c)", p=P),
                         "ffn_in", True)
                    load(b1_b[0:FR, k, FC - 1:FC], b1[:, k * F + full:(k + 1) * F].rearrange("l p -> p l"),
                         "ffn_in", True)
                load(ln_b[:, 0:1], layer("L0_ffn_ln_g", l).rearrange("l d -> d l"), "ffn_in", True)
                load(ln_b[:, 1:2], layer("L0_ffn_ln_b", l).rearrange("l d -> d l"), "ffn_in", True)

            def load_ffn_out(l):
                w2 = layer("L0_ffn_W2", l)
                full = (FC - 1) * P
                load(w2_b[:, 0:FC - 1, :], w2[:, 0:full, :].rearrange("l (c p) o -> p (l c) o", p=P), "ffn_out")
                load(w2_b[0:FR, FC - 1, :], w2[:, full:F, :].rearrange("l p o -> p (l o)"), "ffn_out")
                load(w2_b[FR:FR + 1, FC - 1, :], layer("L0_ffn_b2", l), "ffn_out")

            def load_up(e, k):
                for j, name in enumerate(("L1_ffn_experts_w1", "L1_ffn_experts_w3")):
                    load(w_up[:, k, j, :], t[name][bass.ds(e, 1)].rearrange("e d n -> d (e n)"), f"up{k}")

            def load_down(e, k):
                load(w_down[:, k, :, :],
                     t["L1_ffn_experts_w2"][bass.ds(e, 1)].rearrange("e (c p) o -> p (e c) o", p=P), f"down{k}")

            load_out(0)
            load_ffn_in(0)
            load_ffn_out(0)
            sp.wait_ge(prep_ps, 2)
            load_qkv(0)
            sp.wait_ge(loaded["wo_b"], 16)
            load_out(1)
            sp.wait_ge(low_sb, 2)
            load_qkv(1)
            with sp.Fori(1, DEPTH - 1) as l:
                wait_alone(sp, fh_sb, FC * 4 * l)
                load_ffn_in(l)
                wait_alone(sp, fy_ps, 4 * l)
                load_ffn_out(l)
                wait_alone(sp, low_sb, 2 * l + 2)
                load_qkv(l + 1)
                wait_alone(sp, loaded["wo_b"], 16 * (l + 1))
                wait_alone(sp, y_ps, B0 + UNITS * l)
                load_out(l + 1)
            sp.wait_ge(fh_sb, FC * 4 * (DEPTH - 1))
            load_ffn_in(DEPTH - 1)
            sp.wait_ge(fy_ps, 4 * (DEPTH - 1))
            load_ffn_out(DEPTH - 1)
            sp.wait_ge(low_sb, 2 * DEPTH)
            for k in range(2):
                load_up(k, k)
                load_down(k, k)
            with sp.Fori(1, E // 2) as j:
                for k in range(2):
                    sp.wait_ge(eu_ps, (4 * j + 2 * k - 2) * EC)
                    load_up(2 * j + k, k)
                    sp.wait_ge(ey_ps, 4 * j + 2 * k - 2)
                    load_down(2 * j + k, k)
            sp.wait_ge(ey_sb, 2 * E)
            sp.dma_start(out.rearrange("b s d -> s b d"), resid[:]).then_inc(stored, 16)
            sp.wait_ge(stored, 16)

        @block.tensor
        def _(pe):
            def prepare():
                landed(pe, "wa")
                landed(pe, "ctx")
                landed(pe, "ident")
                for j in range(8):
                    pe.transpose(ps[:, j // 4, (j % 4) * P:(j % 4) * P + P], wa[:, 0, j * P:j * P + P], ident[:])
                for k in range(2):
                    for j in range(8):
                        pe.transpose(ps[:, 2 + k, j * CD:j * CD + CD], wa[0:CD, 1 + k, j * P:j * P + P],
                                     ident[0:CD, 0:CD])
                for b in range(B):
                    tr = pe.transpose(ps[:, 4 + b // 4, (b % 4) * CTX:(b % 4) * CTX + CTX],
                                      ctx_twice[:, b, :, :], ident[0:CTX, 0:CTX])
                tr.then_inc(prep_ps, 1)
                pe.wait_ge(prep_act, 2)
                for h in range(H):
                    r = slice(HD * (h % 2), HD * (h % 2) + HD)
                    pe.matmul(ps[:, 6 + h % 2, (h // 2) * CD:(h // 2) * CD + CD], wq_t[r, h // 2, :],
                              wkv_t[r, 0, h // 2, :], start=True, stop=True)
                for h in range(H):
                    r = slice(HD * (h % 2), HD * (h % 2) + HD)
                    mm = pe.matmul(ps[r, h // 8, (h // 2 % 4) * P:(h // 2 % 4) * P + P], wkv_t[r, 1, h // 2, :],
                                   wo_a[r, h // 2, :], start=True, stop=True)
                mm.then_inc(prep_ps, 1)

            def second_keys():
                landed(pe, "wc")
                for g in range(2):
                    for k in range(2):
                        mm = pe.matmul(ps[0:CD, 2 + 2 * g + k, 0:4 * CTX], wkv_c[:, 0, g * CD:g * CD + CD],
                                       ctx_t[0:CD, 4 * k:4 * k + 4, :], start=True, stop=True)
                mm.then_inc(prep_ps, 1)

            def second_values():
                for b in range(B):
                    mm = pe.matmul(ps[0:CTX, 6 + b // 4, (b % 4) * P:(b % 4) * P + P], ctx_t[0:CD, b, :],
                                   wkv_c[:, 1, :], start=True, stop=True)
                mm.then_inc(prep_ps, 1)

            def transpose_x(count, parts):
                pe.wait_ge(stage_ready, count)
                for k in range(parts):
                    src = x_stage[:] if parts == 1 else x_stages[:, k, :].bitcast(F32)
                    tr = pe.transpose(ps[:, T_BANK, k * P:k * P + P], src, ident[:])
                tr.then_inc(xt_ps, 1)

            def product(o, left, left_low, right, right_low):
                pe.matmul(o, left, right_low, start=True, stop=False)
                pe.matmul(o, left_low, right, start=False, stop=False)
                return pe.matmul(o, left, right, start=False, stop=True)

            def transpose_heads(n, wide):
                wait_alone(pe, o_sb, n + 1)
                if not wide:
                    tr = pe.transpose(ps[0:CD, O_BANK, 0:P], heads_out[:, 0:CD], ident[:])
                else:
                    for j in range(4):
                        tr = pe.transpose(ps[:, O_BANK, j * P:j * P + P], heads_out[:, j * P:j * P + P], ident[:])
                tr.then_inc(ot_ps, 1)

            def transpose_probs(keys):
                for h in range(GH):
                    tr = pe.transpose(ps[0:keys, T_BANK + h // 4, (h % 4) * P:(h % 4) * P + P],
                                      probs[:, h, 0:keys], ident[:])
                tr.then_inc(pt_ps, 1)

            def weigh_values(keys, width, value):
                for at in range(GH):
                    mm = pe.matmul(ps[:, V_BANK + at // 4, (at % 4) * width:(at % 4) * width + width],
                                   probs_t[0:keys, at, :], value(at), start=True, stop=True)
                mm.then_inc(pv_ps, 1)

            def cross_attention(kind, n0, b0):
                hd = HC if kind == "C" else HD

                def slot(b, g, has, nxt):
                    n = n0 + 2 * b + g
                    if has(0):
                        if g == 0:
                            pe.wait_ge(xt_sb, 2 * (b0 + b + 1))
                        if has(-2):
                            pe.wait_ge(t_sb, n - 1)
                        if has(-4):
                            pe.wait_ge(y_sb, n - 3)
                        if kind == "A":
                            for j in range(4):
                                h = g * GH + 2 * j
                                mm = pe.matmul(ps[:, QK_BANK + g, j * P:j * P + P], w_qk[:, h:h + 2, :], x_t[:],
                                               start=True, stop=True)
                        else:
                            mm = pe.matmul(ps[0:CD, QK_BANK + g, 0:P], wq_c[:, g * CD:g * CD + CD], x_t[:],
                                           start=True, stop=True)
                        mm.then_inc(t_ps, 1)
                    if has(-2):
                        pe.wait_ge(p_sb, n - 1)
                        if has(-3):
                            pe.wait_ge(pt_sb, n - 2)
                        transpose_probs(CTX)
                    if kind == "A" and isinstance(b, int) and b == B + 1 and g == 0:
                        second_keys()
                    if has(-3):
                        transpose_heads(n - 3, kind == "A")
                    if has(-1):
                        pe.wait_ge(t_sb, n)
                        pe.wait_ge(k_stage, n if kind == "A" else n - C0 + UNITS)
                        if has(-2):
                            pe.wait_ge(sub_sb, n - 1)
                        gs = (g - 1) % 2
                        if kind == "A":
                            for j in range(4):
                                for k in range(2):
                                    r = slice(HD * k, HD * k + HD)
                                    mm = pe.matmul(ps[:, S_BANK + k, j * CTX:(j + 1) * CTX], qk_t[r, j, :],
                                                   ctx_stage[r, gs, :], start=True, stop=True)
                        else:
                            for k in range(2):
                                mm = pe.matmul(ps[:, S_BANK + k, 0:4 * CTX], qk_t[0:CD, 0, :],
                                               kc_heads[:, gs, 4 * k:4 * k + 4, :], start=True, stop=True)
                        mm.then_inc(s_ps, 1)
                    if has(-3):
                        pe.wait_ge(ot_sb, n - 2)
                        o = ps[:, QK_BANK + 1 - g, 0:P]
                        gy = (g - 3) % 2
                        if kind == "C":
                            mm = pe.matmul(o, heads_t[0:CD, 0, :], wo_c[:, gy, :], start=True, stop=True)
                        else:
                            for j in range(4):
                                mm = pe.matmul(o, heads_t[:, j, :], w_vo[:, 4 * gy + j, :], start=(j == 0), stop=(j == 3))
                        mm.then_inc(y_ps, 1)
                    if g == 1 and nxt:
                        if has(-2):
                            pe.wait_ge(pt_sb, n - 1)
                        transpose_x(b0 + b + 2, 1)
                    if has(-2):
                        pe.wait_ge(pt_sb, n - 1)
                        if has(-3):
                            pe.wait_ge(ot_sb, n - 2)
                        bv = bass.ds(b - 1, 1)
                        if kind == "A":
                            weigh_values(CTX, HD + 1, lambda at: ctx_ones[:, bv, :])
                        else:
                            weigh_values(CTX, GH * (HC + 1), lambda at: vc_ones[:, bv, g * GH:(g + 1) * GH, :]
                                         .rearrange("p a h d -> p a (h d)"))

                transpose_x(b0 + 1, 1)
                slots(pe, slot)

            def local_layers():
                def slot(c, s, has, ff, nxt, more):
                    n = B0 + 4 * c + s
                    m = 4 * c + s
                    g = s % 2
                    b_now, l_now = in_layer(c)
                    b_last, l_last = in_layer(c - 1) if has(-4) else (0, 0)
                    x_count = B + 2 * c + s // 2 + 1
                    if has(0):
                        if s < 2:
                            pe.wait_ge(low_sb, 2 * l_now + s + 1)
                        if g == 0:
                            pe.wait_ge(xt_sb, 2 * x_count)
                        if has(-1):
                            pe.wait_ge(raw_sb, m)
                            if has(-2):
                                pe.wait_ge(t_sb, n - 1)
                        for k in range(2):
                            at = (k * H + g * GH) * HD
                            mm = product(ps[:, QK_BANK + k, :], x_parts[:, 0, :], x_parts[:, 1, :],
                                         w_high[:, at:at + GH * HD], w_low[:, at:at + GH * HD])
                        mm.then_inc(qk_ps, 1)
                    if has(-2) and (ff(-2) or (s == 0 and ff(-3))):
                        pe.wait_ge(sub_sb, n - 1)
                    feed_forward(c, s, ff)
                    if has(0):
                        if has(-3):
                            pe.wait_ge(o_sb, n - 2)
                        elif has(-1):
                            pe.wait_ge(v_sb, m)
                        at = (2 * H + g * GH) * HD
                        product(ps[:, V_BANK, :], x_parts[:, 0, :], x_parts[:, 1, :],
                                w_high[:, at:at + GH * HD], w_low[:, at:at + GH * HD]).then_inc(v_ps, 1)
                    if has(-3):
                        transpose_heads(n - 3, True)
                    if has(-1):
                        pe.wait_ge(un_sb, m)
                        if has(0):
                            pe.wait_ge(raw_sb, m + 1)
                        for j in range(8):
                            pair = slice(2 * (j % 4), 2 * (j % 4) + 2)
                            tr = pe.transpose(ps[:, QK_BANK + j // 4, (j % 4) * P:(j % 4) * P + P],
                                              turned[:, j // 4, pair, :], ident[:])
                        tr.then_inc(t_ps, 1)
                    if has(-2):
                        pe.wait_ge(p_sb, n - 1)
                        if has(-3):
                            pe.wait_ge(pt_sb, n - 2)
                        transpose_probs(P)
                    if has(-3):
                        layer_y = l_last if s < 3 else l_now
                        if s == 3 and has(0):
                            pe.wait_ge(loaded["wo_b"], 16 * layer_y + 16)
                        pe.wait_ge(ot_sb, n - 2)
                        if has(0):
                            pe.wait_ge(v_sb, m + 1)
                        gy = (g - 3) % 2
                        for j in range(4):
                            at = (8 * gy + 2 * j) * HD
                            mm = pe.matmul(ps[:, V_BANK, 0:P], heads_t[:, j, :],
                                           wo_b[:, bass.ds(layer_y % 2, 1), at:at + P], start=(j == 0), stop=(j == 3))
                        mm.then_inc(y_ps, 1)
                    if has(-1):
                        pe.wait_ge(t_sb, n)
                        if has(-2):
                            pe.wait_ge(sub_sb, n - 1)
                        if s == 0:
                            if ff(-3):
                                pe.wait_ge(fy_sb, c - 2)
                            if ff(-2):
                                pe.wait_ge(sh_sb, 2 * (c - 1))
                        elif ff(-2):
                            done, each = ((fx_sb, 1), (fc_sb, 2), (fh_sb, FC))[s - 1]
                            pe.wait_ge(done, each * (c - 1))
                        for k in range(2):
                            pe.matmul(ps[:, S_BANK + k, :], ident16[:], mask16[:], start=True, stop=False)
                        for j in range(4):
                            for k in range(2):
                                r = slice(HD * k, HD * k + HD)
                                mm = pe.matmul(ps[:, S_BANK + k, j * P:(j + 1) * P], qk_t[r, j, :], qk_t[r, 4 + j, :],
                                               start=False, stop=(j == 3))
                        mm.then_inc(s_ps, 1)
                    if g == 1 and nxt:
                        if has(-2):
                            pe.wait_ge(pt_sb, n - 1)
                        transpose_x(x_count + 1, 2)
                    if has(-2):
                        pe.wait_ge(pt_sb, n - 1)
                        if has(0):
                            pe.wait_ge(v_sb, m + 1)
                        if has(-3):
                            pe.wait_ge(ot_sb, n - 2)
                            pe.wait_ge(y_sb, n - 2)
                        bv = b_now if s >= 2 else b_last + 1
                        weigh_values(P, HD + 1,
                                     lambda at: v_ones[:, bass.ds(bv, 1), g, 2 * (at % 4) + at // 4, :])

                def feed_forward(c, s, ff):
                    if s == 0 and ff(-3):
                        _, l_out = in_layer(c - 3)
                        pe.wait_ge(loaded["ffn_out"], (l_out + 1) * (16 * LOADS["ffn_out"]))
                        pe.wait_ge(fh_sb, FC * (c - 2))
                        for b in range(2):
                            o = ps[:, S_BANK + 1, b * P:b * P + P]
                            for k in range(FC):
                                w = P if k < FC - 1 else FR + 1
                                mm = pe.matmul(o, pair_hid[0:w, k, b * P:b * P + P], w2_b[0:w, k, :],
                                               start=(k == 0), stop=(k == FC - 1))
                        mm.then_inc(fy_ps, 1)
                    if not ff(-2):
                        return
                    b_in, l_in = in_layer(c - 2)
                    if s == 0:
                        pe.wait_ge(y_sb, B0 + 4 * (c - 1))
                        for b in range(2):
                            mm = pe.matmul(ps[:, S_BANK, b * CD:b * CD + CD], down[:],
                                           local[:, bass.ds(b_in + b, 1), CD:P], start=True, stop=True)
                        mm.then_inc(sh_ps, 1)
                    if s == 1:
                        pe.wait_ge(fn_sb, 2 * (c - 1))
                        for b in range(2):
                            tr = pe.transpose(ps[:, S_BANK, b * P:b * P + P], pair_n[:, b, :], ident[:])
                        tr.then_inc(fx_ps, 1)
                    if s >= 2:
                        off, ready = ((F, fg_ps), (0, fa_ps))[s - 2]
                        if s == 2:
                            pe.wait_ge(fx_sb, c - 1)
                        else:
                            pe.wait_ge(fc_sb, 2 * (c - 1))
                        for k in range(FC):
                            w = P if k < FC - 1 else FR
                            mm = pe.matmul(ps[0:w, S_BANK + k // 2, (k % 2) * 2 * P:(k % 2 + 1) * 2 * P],
                                           w1_b[:, off + k * P:off + k * P + w], pair_t[:], start=True, stop=True)
                        mm.then_inc(ready, 1)

                transpose_x(B + 1, 2)
                local_slots(pe, slot)

            def experts():
                def transpose_half(hf):
                    pe.wait_ge(ln_out, 4 * (2 * LN_D + hf + 1))
                    for b in range(4):
                        tr = pe.transpose(ps[:, 6 + hf, b * P:b * P + P], normed[:, 4 * hf + b, :], ident[:])
                    tr.then_inc(ex_ps, 1)

                def router_logits():
                    pe.wait_ge(xr_sb, 2)
                    for b in range(B):
                        mm = pe.matmul(ps[:, 7, b * E:b * E + E], x_router[:, b, :], gate_w[:],
                                       start=True, stop=True)
                    mm.then_inc(lg_ps, 1)

                def up(e, k, hf, first):
                    if hf == 0:
                        pe.wait_ge(e_split, 2 * e + 2)
                    if isinstance(e, int) and e == 0:
                        pe.wait_ge(ex_sb, 2 * hf + 2)
                    for c in range(EC):
                        q = (2 * e + hf) * EC + c
                        if not (first and c < 2):
                            pe.wait_ge(eg_sb, q - 1)
                            pe.wait_ge(eh_sb, q - 1)
                        for j, done in enumerate((eg_ps, eu_ps)):
                            product(ps[:, 2 * j + c % 2, :], up_high[:, k, j, c * P:c * P + P],
                                    up_low[:, k, j, c * P:c * P + P], xn_high[:, hf, :], xn_low[:, hf, :])\
                                .then_inc(done, 1)

                def down_proj(e, k, hf, first):
                    s = 2 * e + hf
                    if hf == 0:
                        pe.wait_ge(loaded[f"down{k}"], (e - k) * 8 + 16)
                    pe.wait_ge(eh_sb, (s + 1) * EC)
                    if not first:
                        pe.wait_ge(ey_sb, s - 1)
                    for b in range(4):
                        for c in range(EC):
                            mm = pe.matmul(ps[:, 4 + hf, b * P:b * P + P], hidden[:, hf, c, b * P:b * P + P],
                                           w_down[:, k, c, :], start=(c == 0), stop=(c == EC - 1))
                    mm.then_inc(ey_ps, 1)

                def expert_pair(e, first, last):
                    for k in range(2):
                        for hf in range(2):
                            s = 2 * k + hf
                            if not (last and s == 3):
                                ne = e + (s + 1) // 2
                                up(ne, ((s + 1) // 2) % 2, (s + 1) % 2, False)
                            down_proj(e + k, k, hf, first and s < 2)

                transpose_half(0)
                up(0, 0, 0, True)
                transpose_half(1)
                router_logits()
                expert_pair(0, True, False)
                with pe.Fori(1, E // 2 - 1) as j:
                    expert_pair(2 * j, False, False)
                expert_pair(E - 2, False, True)

            prepare()
            pe.wait_ge(prep_act, 4)
            pe.wait_ge(prep_dve, 1)
            cross_attention("A", A0, 0)
            second_values()
            pe.wait_ge(prep_act, 6)
            pe.wait_ge(prep_dve, 3)
            pe.wait_ge(const_ready, 5)
            local_layers()
            cross_attention("C", C0, B + B * DEPTH)
            experts()

        @block.scalar
        def _(act):
            def prepare():
                landed(act, "small")
                act.activation(tgate[:], gates[:], ACT.Tanh).then_inc(tg_ready, 1)
                act.wait_ge(prep_ps, 1)
                act.activation(wq_t.rearrange("p (a c) n -> p a (c n)", a=2), ps[:, 0:2, :], ACT.Copy)\
                   .then_inc(prep_act, 1)
                act.activation(wkv_t.rearrange("p k c n -> p k (c n)"), ps[:, 2:4, :], ACT.Copy)\
                   .then_inc(prep_act, 1)
                act.wait_ge(prep_ps, 2)
                act.activation(w_qk.rearrange("p (j a) n -> p a j n", a=2),
                               ps[:, 6:8, :].rearrange("p a (j n) -> p a j n", n=CD), ACT.Copy,
                               scale=HD ** -0.5).then_inc(prep_act, 1)
                act.activation(w_vo[:].rearrange("p (a c) n -> p a (c n)", a=2), ps[:, 0:2, :], ACT.Copy)\
                   .then_inc(prep_act, 1)

            def prepare_second():
                act.wait_ge(prep_ps, 3)
                landed(act, "wc")
                for g in range(2):
                    act.activation(kc_t[:, g, :].rearrange("p (a c) -> p a c", a=2),
                                   ps[0:CD, 2 + 2 * g:4 + 2 * g, 0:4 * CTX], ACT.Identity,
                                   bias=bqk_c[:, 1, g:g + 1]).then_inc(prep_act, 1)

            def upper_weights(l, g):
                act.wait_ge(loaded["wqkv"], 16 * l + 16)
                act.activation(weight_groups(w_high)[:, g], weight_groups(raw)[:, g], ACT.Copy).then_inc(high_sb, 1)

            def copy_x(count, shift):
                act.wait_ge(xt_ps, count)
                parts = 1 + shift
                seen = ps[:, T_BANK, 0:parts * P].rearrange("p (k n) -> p k n", k=parts)
                dst = x_parts[:] if shift else x_t[:].unsqueeze(1)
                act.activation(dst[0:CD], seen[0:CD], ACT.Copy).then_inc(xt_sb, 1)
                act.activation(dst[CD:P, :, shift:P], seen[CD:P, :, 0:P - shift], ACT.Copy).then_inc(xt_sb, 1)

            def copy_heads(n, has, wide):
                act.wait_ge(ot_ps, n + 1)
                if has(-4):
                    act.wait_ge(y_ps, n)
                if wide:
                    act.activation(heads_t[:].rearrange("p c n -> p (c n)"), ps[:, O_BANK, :], ACT.Copy)\
                       .then_inc(ot_sb, 1)
                else:
                    act.activation(heads_t[0:CD, 0, :], ps[0:CD, O_BANK, 0:P], ACT.Copy).then_inc(ot_sb, 1)

            def exponent(n, has, keys):
                act.wait_ge(sub_sb, n + 1)
                if has(-3):
                    act.wait_ge(pt_ps, n)
                act.activation(probs[:, :, 0:keys], shifted[:, :, 0:keys], ACT.Exp).then_inc(p_sb, 1)

            def copy_probs(n, has, keys):
                act.wait_ge(pt_ps, n + 1)
                if has(-3):
                    act.wait_ge(pv_ps, n)
                act.activation(probs_t[0:keys, :, :].rearrange("p (a c) n -> p a (c n)", a=2),
                               ps[0:keys, T_BANK:T_BANK + 2, :], ACT.Copy).then_inc(pt_sb, 1)

            def cross_attention(kind, n0, b0):
                def slot(b, g, has, nxt):
                    n = n0 + 2 * b + g
                    if has(-1):
                        act.wait_ge(t_ps, n)
                        if has(-2):
                            act.wait_ge(s_ps, n - 1)
                        gq = (g - 1) % 2
                        if kind == "A":
                            act.activation(qk_t[:, 0:4, :].rearrange("p c n -> p (c n)"), ps[:, QK_BANK + gq, :],
                                           ACT.Copy).then_inc(t_sb, 1)
                        else:
                            act.activation(qk_t[0:CD, 0, :], ps[0:CD, QK_BANK + gq, 0:P], ACT.Identity,
                                           bias=bq_scaled[:, gq:gq + 1], scale=HC ** -0.5).then_inc(t_sb, 1)
                    if has(-2):
                        exponent(n - 2, has, CTX)
                    if has(-3):
                        copy_heads(n - 3, has, kind == "A")
                    if has(-2):
                        copy_probs(n - 2, has, CTX)
                    if g == 1 and nxt:
                        copy_x(b0 + b + 2, 0)
                    if kind == "A" and isinstance(b, int) and b == B - 1:
                        upper_weights(0, g)

                copy_x(b0 + 1, 0)
                slots(act, slot)

            def local_layers():
                def slot(c, s, has, ff, nxt, more):
                    n = B0 + 4 * c + s
                    m = 4 * c + s
                    if has(0):
                        act.wait_ge(qk_ps, m + 1)
                        if has(-1):
                            act.wait_ge(rot_sb, 3 * m)
                            act.wait_ge(sq_sb, m)
                        act.activation(raw_qk[:].rearrange("p a h d -> p a (h d)"),
                                       ps[:, QK_BANK:QK_BANK + 2, :], ACT.Copy).then_inc(raw_sb, 1)
                    if has(-2):
                        exponent(n - 2, has, P)
                    if has(0):
                        act.wait_ge(v_ps, m + 1)
                        act.activation(v_ones[:, bass.ds(in_layer(c)[0] + s // 2, 1), s % 2, :, 0:HD],
                                       ps[:, V_BANK, :].rearrange("p (a h d) -> p a h d", a=1, h=GH), ACT.Copy)\
                           .then_inc(v_sb, 1)
                    if has(-3):
                        copy_heads(n - 3, has, True)
                    if has(0):
                        if has(-1):
                            act.wait_ge(ss_sb, m)
                        act.wait_ge(raw_sb, m + 1)
                        act.activation(squares[:], raw_qk[:].rearrange("p a h d -> p (a h) d"),
                                       ACT.Square).then_inc(sq_sb, 1)
                    if has(-1):
                        act.wait_ge(t_ps, n)
                        if has(-2):
                            act.wait_ge(s_ps, n - 1)
                        act.activation(qk_t[:].rearrange("p (a c) n -> p a (c n)", a=2),
                                       ps[:, QK_BANK:QK_BANK + 2, :], ACT.Copy).then_inc(t_sb, 1)
                    if has(-2):
                        copy_probs(n - 2, has, P)
                    if s % 2 == 1 and nxt:
                        copy_x(B + 2 * c + s // 2 + 2, 1)
                    if more == 1 and s >= 2:
                        act.wait_ge(v_ps, m + 1)
                        upper_weights(in_layer(c)[1] + 1, s - 2)
                    if s == 2 and ff(-2):
                        for k in range(FC):
                            w = P if k < FC - 1 else FR
                            act.wait_ge(fc_sb, 2 * (c - 1) - (1 if k < FC - 1 else 0))
                            act.activation(gelu[0:w, k, :], gelu[0:w, k, :], ACT.Gelu, bias=b1_b[0:w, 1, k:k + 1])\
                               .then_inc(fg_sb, 1)
                        if ff(-3):
                            act.wait_ge(table_back, c - 2)
                        act.activation(table_call[:], tgate[:, 0:1], ACT.Exp).then_inc(table_back, 1)

                copy_x(B + 1, 1)
                local_slots(act, slot)

            def experts():
                def copy_half(hf):
                    act.wait_ge(ex_ps, hf + 1)
                    act.activation(x_router[:, 4 * hf:4 * hf + 4, :].rearrange("p b n -> p (b n)"),
                                   ps[:, 6 + hf, :], ACT.Copy).then_inc(xr_sb, 1)

                def gates_of(s0, first):
                    for c in range(EC):
                        q = s0 * EC + c
                        act.wait_ge(eg_ps, q + 1)
                        if not (first and c < 2):
                            act.wait_ge(eh_sb, q - 1)
                        act.activation(silu[:, c % 2, :], ps[:, c % 2, :], ACT.Silu).then_inc(eg_sb, 1)

                copy_half(0)
                gates_of(0, True)
                copy_half(1)
                act.wait_ge(rt_own, 4)
                act.activation(pair_w[:, 1, :], pair_w[:, 0, :], ACT.Exp).then_inc(rt_act, 1)
                for s in range(1, 4):
                    gates_of(s, False)
                with act.Fori(1, E // 2) as j:
                    for s in range(4):
                        gates_of(4 * j + s, False)

            prepare()
            cross_attention("A", A0, 0)
            prepare_second()
            local_layers()
            cross_attention("C", C0, B + B * DEPTH)
            experts()

        @block.gpsimd
        def _(pool):
            def norm_scale(i):
                half = slice(4 * (i % 2), 4 * (i % 2) + 4)
                wait_alone(pool, ln_mom, 4 * (i + 1))
                pool.tensor_scalar(safe_var[:, half], moments[:, half, 1], EPS, None, ALU.add).then_inc(ln_var, 1)
                wait_alone(pool, ln_var, i + 1)
                pool.tensor_tensor(rstd[:, half], safe_var[:, half], minus_half[:, 0:4], ALU.pow).then_inc(ln_rstd, 1)

            def stage_keys(kind, n0, after):
                def slot(b, g, has, nxt):
                    if not has(0):
                        if isinstance(b, int) and b == B and g == 0:
                            norm_scale(2 * after)
                        return
                    if has(-2):
                        wait_alone(pool, s_ps, n0 + 2 * b + g - 1)
                    if kind == "A":
                        pool.tensor_copy(ctx_stage[:, g, :], ctx_t[:, bass.ds(b, 1), :].rearrange("p a c -> p (a c)"))\
                            .then_inc(k_stage, 1)
                    else:
                        src = kc_t[:, g, bass.ds(b * CTX, CTX)].unsqueeze(1).to_broadcast([CD, GH, CTX])
                        pool.tensor_tensor(kc_heads[:, g, :, :], src,
                                           head_of[:].unsqueeze(2).to_broadcast([CD, GH, CTX]), ALU.mult)\
                            .then_inc(k_stage, 1)
                        if isinstance(b, int) and b == 0 and g == 1:
                            norm_scale(2 * LN_C + 1)
                slots(pool, slot)

            def local_units():
                def slot(c, s, has, ff, nxt, more):
                    m = 4 * c + s
                    half = HD // 2
                    layer = bass.ds(in_layer(c)[1], 1)

                    def table(k, a, w):
                        tab = rot_tab[:, layer, :, k, a:a + w].rearrange("p l k d -> p (l k) d")
                        return tab.unsqueeze(2).to_broadcast([P, 2, GH, w])
                    if has(0):
                        wait_alone(pool, raw_sb, m + 1)
                        if has(-1):
                            wait_alone(pool, ra_sb, m)
                        pool.tensor_tensor(rot_cos[:], raw_qk[:], table(0, 0, HD), ALU.mult).then_inc(rot_sb, 1)
                        for a in range(2):
                            other = half * (1 - a)
                            pool.tensor_tensor(rot_sin[:, :, :, half * a:half * a + half],
                                               raw_qk[:, :, :, other:other + half], table(1, half * a, half),
                                               ALU.mult).then_inc(rot_sb, 1)
                    if s == 0 and ff(-2):
                        wait_alone(pool, fm_sb, 2 * (c - 1))
                        pool.tensor_scalar(pair_var[:], pair_mom[:, :, 1], EPS, None, ALU.add).then_inc(fv_sb, 1)
                        wait_alone(pool, fv_sb, c - 1)
                        pool.tensor_tensor(pair_rstd[:], pair_var[:], minus_half[:, 0:2], ALU.pow).then_inc(fr_sb, 1)
                    if has(0):
                        wait_alone(pool, ss_sb, m + 1)
                        if has(-1):
                            wait_alone(pool, un_sb, m)
                        pool.tensor_scalar(safe_sq[:], sumsq[:], 1e-24, None, ALU.max).then_inc(sg_sb, 1)
                        wait_alone(pool, sg_sb, m + 1)
                        pool.tensor_tensor(rnorm[:], safe_sq[:], minus_half[:], ALU.pow).then_inc(rn_sb, 1)
                    if isinstance(c, int) and c == CYCLES + 1 and s == 1:
                        norm_scale(2 * LN_C)
                local_slots(pool, slot)

            pool.memset(v_ones[:, :, :, :, HD:HD + 1], 1.0).then_inc(ones_ready, 1)
            pool.memset(ctx_ones[:, :, CD:CD + 1], 1.0).then_inc(ones_ready, 1)
            pool.memset(vc_ones[:, :, :, HC:HC + 1], 1.0).then_inc(ones_ready, 1)
            pool.memset(minus_half[:], -0.5).then_inc(ones_ready, 1)
            pool.wait_ge(ones_ready, 4)
            norm_scale(0)
            norm_scale(1)
            pool.wait_ge(prep_dve, 1)
            stage_keys("A", A0, 1)
            norm_scale(3)
            pool.wait_ge(const_ready, 5)
            local_units()
            stage_keys("C", C0, LN_D)
            norm_scale(2 * LN_D + 1)

        @block.vector
        def _(dve):
            def measure(i, src):
                ready = 4 * (i + 1)
                for b in range(4 * (i % 2), 4 * (i % 2) + 4):
                    dve.bn_stats(stats[:, b, :], src[:, b, :]).then_inc(ln_stats, 1)
                wait_alone(dve, ln_stats, ready)
                for b in range(4 * (i % 2), 4 * (i % 2) + 4):
                    dve.bn_aggr(moments[:, b, :], stats[:, b, :]).then_inc(ln_mom, 1)

            def normalise(i, src, dst):
                dve.wait_ge(ln_mom, 4 * (i + 1))
                dve.wait_ge(ln_rstd, i + 1)
                for b in range(4 * (i % 2), 4 * (i % 2) + 4):
                    dve.tensor_scalar(dst[:, b, :], src[:, b, :], moments[:, b, 0:1], rstd[:, b:b + 1],
                                      ALU.subtract, ALU.mult).then_inc(ln_out, 1)

            def split(high, low, whole, done, before):
                dve.tensor_copy(high, whole).then_inc(done, 1)
                dve.wait_ge(done, before + 1)
                dve.tensor_tensor(low, whole, high.bitcast(F32), ALU.subtract).then_inc(done, 1)

            def lower_weights(l, g):
                high, low, whole = (weight_groups(w)[:, g] for w in (w_high, w_low, raw))
                dve.wait_ge(high_sb, 2 * l + g + 1)
                dve.tensor_tensor(low, whole, high.bitcast(F32), ALU.subtract).then_inc(low_sb, 1)

            def split_expert(e, k):
                dve.wait_ge(loaded[f"up{k}"], (e - k) * 16 + 32)
                split(up_high[:, k], up_low[:, k], w_up[:, k], e_split, 2 * e)

            def stage_parts(b, used):
                x = local[:, bass.ds(b, 1), :]
                dve.wait_ge(xt_ps, used)
                dve.tensor_copy(x_stages[:, 0:1, :], x).then_inc(stage_high, 1)
                dve.wait_ge(stage_high, used - B + 1)
                dve.tensor_tensor(x_stages[:, 1:2, :], x, x_stages[:, 0:1, :].bitcast(F32), ALU.subtract)\
                    .then_inc(stage_ready, 1)

            def stage(src, b, used):
                if not (isinstance(used, int) and used == 0):
                    dve.wait_ge(xt_ps, used)
                dve.tensor_copy(x_stage[:], src[:, bass.ds(b, 1), :].rearrange("p a d -> p (a d)"))\
                   .then_inc(stage_ready, 1)

            def divide_heads(n, has, hd):
                if hd == HD:
                    heads = [ps[:, V_BANK:V_BANK + 2, 0:4 * (hd + 1)].rearrange("p a (h d) -> p a h d", h=4)]
                else:
                    row = GH * (hd + 1)
                    heads = []
                    for a in range(2):
                        first = 4 * a * (hd + 1)
                        step = row + hd + 1
                        heads.append(ps[:, V_BANK + a:V_BANK + a + 1, first:first + 4 * step]
                                     .rearrange("p a (h d) -> p a h d", h=4)[:, :, :, 0:hd + 1])
                size = 2 // len(heads)
                dve.wait_ge(pv_ps, n + 1)
                for a, part in enumerate(heads):
                    ins = dve.reciprocal(rsum[:, a * 4:(a + size) * 4].rearrange("p (a h d) -> p a h d", a=size, d=1),
                                         part[:, :, :, hd:hd + 1])
                ins.then_inc(rs_sb, 1)
                dve.wait_ge(rs_sb, n + 1)
                if has(-4):
                    dve.wait_ge(ot_ps, n)
                order = "p (a h d) -> p a h d" if hd == HC else "p (h a d) -> p a h d"
                for a, part in enumerate(heads):
                    ins = dve.tensor_tensor(heads_out[:, a * 4 * hd:(a + size) * 4 * hd].rearrange(order, a=size, h=4),
                                            part[:, :, :, 0:hd],
                                            rsum[:, a * 4:(a + size) * 4].rearrange("p (a h) -> p a h", a=size)
                                            .unsqueeze(3).to_broadcast([P, size, 4, hd]), ALU.mult)
                ins.then_inc(o_sb, 1)

            def subtract_max(n, has, keys):
                dve.wait_ge(s_ps, n + 1)
                scores = ps[:, S_BANK:S_BANK + 2, 0:4 * keys].rearrange("p a (h k) -> p a h k", h=4)
                dve.tensor_reduce(row_max[:].rearrange("p (a h) -> p a h", a=2), scores, AX.X, ALU.max)\
                   .then_inc(max_sb, 1)
                dve.wait_ge(max_sb, n + 1)
                if has(-3):
                    dve.wait_ge(p_sb, n)
                dve.tensor_tensor(shifted[:, :, 0:keys].rearrange("p (a h) k -> p a h k", a=2), scores,
                                  row_max[:].rearrange("p (a h) -> p a h", a=2).unsqueeze(3)
                                  .to_broadcast([P, 2, 4, keys]), ALU.subtract).then_inc(sub_sb, 1)

            def half_of(x, i):
                return x[:, 4 * (i % 2):4 * (i % 2) + 4, :]

            def add_bias(i):
                k, done = (0, i - 1) if i < 2 * LN_C else (1, i - 1)
                dve.scalar_tensor_tensor(half_of(resid, i), bias_row[:, k, :].unsqueeze(1).to_broadcast([P, 4, P]),
                                         tgate[:, k:k + 1], half_of(resid, i), ALU.mult, ALU.add)\
                   .then_inc(resid_done, 1)
                dve.wait_ge(resid_done, done)

            def add_local(i):
                dve.scalar_tensor_tensor(half_of(resid, i), half_of(local, i), tgate[:, 2:3], half_of(resid, i),
                                         ALU.mult, ALU.add).then_inc(resid_done, 1)
                dve.wait_ge(resid_done, i - 1)

            def cross_attention(kind, n0, b0, src, after, second_begin, second_end):
                after_dst = local if kind == "A" else normed
                hd = HC if kind == "C" else HD

                def slot(b, g, has, nxt):
                    n = n0 + 2 * b + g
                    if has(-3):
                        divide_heads(n - 3, has, hd)
                    if g == 1 and nxt:
                        stage(src, b + 1, b0 + b + 1)
                    if has(-1):
                        subtract_max(n - 1, lambda d: has(d + 1), CTX)
                    if has(-3):
                        dve.wait_ge(y_ps, n - 2)
                        if has(-4):
                            dve.wait_ge(y_sb, n - 3)
                        k = 0 if kind == "A" else 1
                        x = resid[:, bass.ds(b + (g - 3) // 2, 1), :]
                        dve.scalar_tensor_tensor(x, ps[:, QK_BANK + 1 - g, 0:P].rearrange("p (a d) -> p a d", a=1),
                                                 tgate[:, k:k + 1], x, ALU.mult, ALU.add).then_inc(y_sb, 1)
                    if isinstance(b, int) and b == 1 and g == 1:
                        second_end()
                    if not isinstance(b, int) or b < B:
                        return
                    if kind == "A" and g == 0:
                        lower_weights(0, b - B)
                    if b == B and g == 1:
                        dve.wait_ge(y_sb, n0 + UNITS // 2)
                        add_bias(2 * after)
                        measure(2 * after, resid)
                    if b == B + 1 and g == 0:
                        normalise(2 * after, resid, after_dst)

                stage(src, 0, b0)
                if kind == "C":
                    split_expert(0, 0)
                second_begin()
                slots(dve, slot)

            def local_layers(second_begin, second_end):
                def slot(c, s, has, ff, nxt, more):
                    n = B0 + 4 * c + s
                    m = 4 * c + s
                    b_now, _ = in_layer(c)
                    b_last, _ = in_layer(c - 1) if has(-4) else (0, 0)
                    if has(-3):
                        divide_heads(n - 3, has, HD)
                    if has(-1):
                        dve.wait_ge(rn_sb, m)
                        dve.wait_ge(ra_sb, m)
                        dve.tensor_tensor(turned[:], turned[:], rnorm[:].rearrange("p (a h) -> p a h", a=2)
                                          .unsqueeze(3).to_broadcast([P, 2, GH, HD]), ALU.mult).then_inc(un_sb, 1)
                    feed_forward(c, s, ff)
                    if more == 1 and s == 3:
                        lower_weights(in_layer(c)[1] + 1, 0)
                    if more == 2 and s == 0:
                        lower_weights(in_layer(c)[1], 1)
                    if has(0):
                        dve.wait_ge(sq_sb, m + 1)
                        if has(-1):
                            dve.wait_ge(rn_sb, m)
                        dve.tensor_reduce(sumsq[:], squares[:], AX.X, ALU.add).then_inc(ss_sb, 1)
                    if has(-3):
                        dve.wait_ge(y_ps, n - 2)
                        if has(-4):
                            dve.wait_ge(y_sb, n - 3)
                        x = local[:, bass.ds(b_now if s == 3 else b_last + (s + 1) // 2, 1), :]
                        dve.tensor_tensor(x, ps[:, V_BANK, 0:P].rearrange("p (a d) -> p a d", a=1), x, ALU.add)\
                           .then_inc(y_sb, 1)
                    if s == 1 and nxt:
                        stage_parts(b_now + 1, B + 2 * c + 1)
                    if s == 3 and nxt:
                        if ff(-3):
                            dve.wait_ge(fy_sb, c - 2)
                        stage_parts(in_layer(c + 1)[0], B + 2 * c + 2)
                    if has(0):
                        dve.wait_ge(rot_sb, 3 * (m + 1))
                        if has(-1):
                            dve.wait_ge(t_ps, B0 + m)
                        dve.tensor_tensor(turned[:], rot_cos[:], rot_sin[:], ALU.add).then_inc(ra_sb, 1)
                    if has(-1):
                        subtract_max(n - 1, lambda d: has(d + 1), P)
                    if s == 0 and ff(-2):
                        dve.wait_ge(fr_sb, c - 1)
                        for b in range(2):
                            dve.tensor_scalar(pair_n[:, b, :], pair_n[:, b, :], pair_mom[:, b, 0:1],
                                              pair_rstd[:, b:b + 1], ALU.subtract, ALU.mult).then_inc(fn_sb, 1)
                    if isinstance(c, int) and c == 0 and s == 1:
                        second_end()
                    if isinstance(c, int) and c == CYCLES + 1 and s == 1:
                        dve.wait_ge(fy_sb, CYCLES - 2)
                        add_local(2 * LN_C)
                        measure(2 * LN_C, resid)
                    if isinstance(c, int) and c == CYCLES + 1 and s == 2:
                        normalise(2 * LN_C, resid, normed)

                def feed_forward(c, s, ff):
                    if s == 0 and ff(-3):
                        dve.wait_ge(fy_ps, c - 2)
                        x = local[:, bass.ds(in_layer(c - 3)[0], 2), :]
                        dve.tensor_tensor(x, ps[:, S_BANK + 1, 0:2 * P].rearrange("p (b d) -> p b d", b=2), x, ALU.add)\
                           .then_inc(fy_sb, 1)
                    if not ff(-2):
                        return
                    b_in, l_in = in_layer(c - 2)
                    if s == 0:
                        x = local[:, bass.ds(b_in, 2), 0:CD]
                        dve.wait_ge(y_sb, B0 + 4 * (c - 1))
                        dve.tensor_copy(pair_n[:, :, 0:CD], x).then_inc(sh_sb, 1)
                        dve.wait_ge(sh_ps, c - 1)
                        dve.tensor_copy(pair_n[:, :, CD:P], ps[:, S_BANK, 0:2 * CD].rearrange("p (b d) -> p b d", b=2))\
                           .then_inc(sh_sb, 1)
                        dve.wait_ge(sh_sb, 2 * (c - 1))
                        for b in range(2):
                            dve.bn_stats(pair_stats[:, b, :], pair_n[:, b, :]).then_inc(fs_sb, 1)
                        wait_alone(dve, fs_sb, 2 * (c - 1))
                        for b in range(2):
                            dve.bn_aggr(pair_mom[:, b, :], pair_stats[:, b, :]).then_inc(fm_sb, 1)
                    if s == 1:
                        dve.wait_ge(loaded["ffn_in"], (l_in + 1) * (16 * LOADS["ffn_in"]))
                        dve.wait_ge(fx_ps, c - 1)
                        dve.tensor_scalar(pair_t[:], ps[:, S_BANK, 0:2 * P], ln_b[:, 0:1], ln_b[:, 1:2],
                                          ALU.mult, ALU.add).then_inc(fx_sb, 1)
                    if s == 2:
                        dve.wait_ge(fg_ps, c - 1)
                        if ff(-3):
                            dve.wait_ge(fh_sb, FC * (c - 2))
                        dve.tensor_copy(gelu[:, 0:2, :].rearrange("p k n -> p (k n)"), ps[:, S_BANK, :])\
                           .then_inc(fc_sb, 1)
                        dve.tensor_copy(gelu[0:FR, 2, :], ps[0:FR, S_BANK + 1, 0:2 * P]).then_inc(fc_sb, 1)
                    if s == 3:
                        dve.wait_ge(fa_ps, c - 1)
                        dve.wait_ge(fg_sb, FC * (c - 1))
                        for k in range(FC):
                            w = P if k < FC - 1 else FR
                            dve.scalar_tensor_tensor(pair_hid[0:w, k, :],
                                                     ps[0:w, S_BANK + k // 2, (k % 2) * 2 * P:(k % 2 + 1) * 2 * P],
                                                     b1_b[0:w, 0, k:k + 1], gelu[0:w, k, :], ALU.add, ALU.mult)\
                               .then_inc(fh_sb, 1)

                stage_parts(0, B)
                second_begin()
                local_slots(dve, slot)

            route_steps = [0]

            def own(ins):
                route_steps[0] += 1
                ins.then_inc(rt_own, 1)
                return route_steps[0]

            def route():
                dve.wait_ge(lg_ps, 1)
                n = own(dve.tensor_copy(logits[:].rearrange("p b e -> p (b e)"), ps[:, 7, 0:B * E]))
                dve.wait_ge(rt_own, n)
                for b in range(B):
                    ins = dve.max(top[:, b, :], logits[:, b, :])
                n = own(ins)
                dve.wait_ge(rt_own, n)
                for b in range(B):
                    ins = dve.max_index(top_at[:, b, :], top[:, b, :], logits[:, b, :])
                n = own(ins)
                dve.wait_ge(rt_own, n)
                n = own(dve.tensor_tensor(pair_w[:, 0, :], top[:, :, 1], top[:, :, 0], ALU.subtract))
                n = own(dve.tensor_copy(top_atf[:], top_at[:]))
                dve.wait_ge(rt_act, 1)
                n = own(dve.tensor_scalar(pair_w[:, 2, :], pair_w[:, 1, :], 1.0, None, ALU.add))
                dve.wait_ge(rt_own, n)
                n = own(dve.reciprocal(pair_w[:, 2, :], pair_w[:, 2, :]))
                dve.wait_ge(rt_own, n)
                n = own(dve.tensor_scalar(pair_w[:, 2, :], pair_w[:, 2, :], tgate[:, 3:4], None, ALU.mult))
                dve.wait_ge(rt_own, n)
                n = own(dve.tensor_tensor(pair_w[:, 3, :], pair_w[:, 2, :], pair_w[:, 1, :], ALU.mult))

            def place_weights():
                dve.wait_ge(rt_own, route_steps[0])
                for k in range(2):
                    for b in range(B):
                        ins = dve.tensor_scalar(tok_w[:, k, b, :], iota[:], top_atf[:, b, k:k + 1],
                                                pair_w[:, 2 + k, b:b + 1], ALU.is_equal, ALU.mult)
                n = own(ins)
                dve.wait_ge(rt_own, n)
                n = own(dve.tensor_tensor(tok_w[:, 2, :, :], tok_w[:, 0, :, :], tok_w[:, 1, :, :], ALU.add))
                dve.wait_ge(rt_own, n)

            def experts(second_begin, second_end):
                def two_parts(hf):
                    dve.wait_ge(xr_sb, hf + 1)
                    whole = x_router[:, 4 * hf:4 * hf + 4, :].rearrange("p b n -> p (b n)")
                    split(xn_high[:, hf, :], xn_low[:, hf, :], whole, ex_sb, 2 * hf)

                def multiply(e, hf, chunks=range(EC)):
                    for c in chunks:
                        q = (2 * e + hf) * EC + c
                        dve.wait_ge(eu_ps, q + 1)
                        dve.wait_ge(eg_sb, q + 1)
                        dve.tensor_tensor(hidden[:, hf, c, :], ps[:, 2 + c % 2, :], silu[:, c % 2, :], ALU.mult)\
                           .then_inc(eh_sb, 1)

                def weigh(e, k, hf, first):
                    s = 2 * e + hf
                    if hf == 0:
                        dve.tensor_copy(tok_we[:, k, :], tok_w[:, 2, :, bass.ds(e, 1)].rearrange("p b e -> p (b e)"))\
                           .then_inc(tokwe_sb, 1)
                        dve.wait_ge(tokwe_sb, e + 1)
                    dve.wait_ge(ey_ps, s + 1)
                    if not first:
                        dve.wait_ge(ey_sb, s - 1)
                    for b in range(4):
                        x = resid[:, 4 * hf + b, :]
                        ins = dve.scalar_tensor_tensor(x, ps[:, 4 + hf, b * P:b * P + P],
                                                       tok_we[:, k, 4 * hf + b:4 * hf + b + 1], x, ALU.mult, ALU.add)
                    ins.then_inc(ey_sb, 1)

                def expert_pair(e, first, last):
                    for k in range(2):
                        for hf in range(2):
                            s = 2 * k + hf
                            if not (last and s == 3):
                                multiply(e + (s + 1) // 2, (s + 1) % 2)
                            if hf == 0 and not (last and k == 1):
                                split_expert(e + k + 1, 1 - k)
                            if first and s == 0:
                                place_weights()
                            weigh(e + k, k, hf, first and s < 2)

                two_parts(0)
                second_begin()
                multiply(0, 0, range(2))
                second_end()
                multiply(0, 0, range(2, EC))
                two_parts(1)
                route()
                expert_pair(0, True, False)
                with dve.Fori(1, E // 2 - 1) as j:
                    expert_pair(2 * j, False, False)
                expert_pair(E - 2, False, True)

            def prepare_second():
                landed(dve, "wc")
                dve.tensor_scalar(bq_scaled[:], bqk_c[:, 0, :], HC ** -0.5, None, ALU.mult).then_inc(prep_dve, 1)
                dve.wait_ge(prep_ps, 4)
                dve.wait_ge(ones_ready, 4)
                dve.tensor_tensor(vc_ones[:, :, :, 0:HC].rearrange("p (a b) h d -> p a b h d", a=1)[:, 0],
                                  ps[0:CTX, 6:8, :].rearrange("p a (b h d) -> p (a b) h d", b=4, h=H),
                                  bv_c[:].rearrange("p (h d) -> p h d", h=H).unsqueeze(1).to_broadcast([CTX, B, H, HC]),
                                  ALU.add).then_inc(prep_dve, 1)

            landed(dve, "x")
            for i in range(2):
                measure(i, resid)
            for i in range(2):
                normalise(i, resid, normed)
            landed(dve, "const")
            landed(dve, "ident")
            dve.tensor_copy(ident16[:], ident[:]).then_inc(const_ready, 1)
            dve.tensor_copy(mask16[:], mask_row[:].unsqueeze(1).to_broadcast([P, 4, P])).then_inc(const_ready, 1)
            dve.memset(pair_hid[:, FC - 1, :], 1.0).then_inc(const_ready, 1)
            landed(dve, "tab")
            dve.tensor_tensor(rot_tab[:].rearrange("p l a b d -> p l (a b d)"),
                              rot_tab[:].rearrange("p l a b d -> p l (a b d)"),
                              rot_base[:].rearrange("p a b d -> p (a b d)").unsqueeze(1)
                              .to_broadcast([P, DEPTH, 4 * HD]), ALU.mult).then_inc(const_ready, 1)
            dve.wait_ge(prep_ps, 1)
            dve.tensor_copy(ctx_t[:].rearrange("p (a b) c -> p a (b c)", a=2), ps[:, 4:6, 0:4 * CTX])\
               .then_inc(prep_dve, 1)
            dve.wait_ge(tg_ready, 1)
            dve.wait_ge(ln_out, B)
            cross_attention("A", A0, 0, normed, 1, lambda: None, lambda: None)
            dve.tensor_scalar(x_parts[CD:P, :, 0:1], ident[CD:P, 0:2].unsqueeze(2), 0.0, None, ALU.mult)\
               .then_inc(const_ready, 1)

            def local_begin():
                dve.wait_ge(y_sb, UNITS)
                add_bias(3)
                measure(3, resid)
                prepare_second()

            def local_end():
                normalise(3, resid, local)
                dve.wait_ge(ln_out, 4 * 4)
            dve.wait_ge(ln_out, 4 * 3)
            local_layers(local_begin, local_end)

            def cross_begin():
                dve.wait_ge(fy_sb, CYCLES)
                add_local(2 * LN_C + 1)
                measure(2 * LN_C + 1, resid)

            def cross_end():
                normalise(2 * LN_C + 1, resid, normed)
                dve.wait_ge(ln_out, 4 * (2 * LN_C + 2))
            dve.wait_ge(ln_out, 4 * (2 * LN_C + 1))
            cross_attention("C", C0, B + B * DEPTH, normed, LN_D, cross_begin, cross_end)

            def experts_begin():
                dve.wait_ge(y_sb, C0 + UNITS)
                add_bias(2 * LN_D + 1)
                measure(2 * LN_D + 1, resid)
            experts(experts_begin, lambda: normalise(2 * LN_D + 1, resid, normed))


_INS = ["x", "ctx_512", "g_xattn", "g_ffn",
        "L0_xattn_Wq", "L0_xattn_Wk", "L0_xattn_Wv", "L0_xattn_Wo", "L0_xattn_bo",
        "L0_ffn_Wqkv", "L0_ffn_q_scale", "L0_ffn_k_scale", "L0_ffn_Wo", "L0_ffn_ln_g", "L0_ffn_ln_b",
        "L0_ffn_W1", "L0_ffn_b1", "L0_ffn_W2", "L0_ffn_b2",
        "L1_xattn_Wq", "L1_xattn_bq", "L1_xattn_Wk", "L1_xattn_bk", "L1_xattn_Wv", "L1_xattn_bv",
        "L1_xattn_Wo", "L1_xattn_bo",
        "L1_ffn_gate", "L1_ffn_experts_w1", "L1_ffn_experts_w2", "L1_ffn_experts_w3"]


def kernel(**inputs):
    import concourse.bacc as bacc
    from concourse.bass_utils import run_bass_kernel_spmd

    nc = bacc.Bacc("TRN2", target_bir_lowering=False, num_devices=1)
    arrays = {f"in_{name}_dram": np.ascontiguousarray(inputs[name]) for name in _INS}
    arrays.update({f"in_{name}_dram": value for name, value in constants().items()})
    t = {name[3:-5]: nc.dram_tensor(name, a.shape, mybir.dt.from_np(a.dtype), kind="ExternalInput").ap()
         for name, a in arrays.items()}
    out = nc.dram_tensor("out_0_dram", (B, P, P), F32, kind="ExternalOutput").ap()
    build(nc, t, out)
    r = run_bass_kernel_spmd(nc, [arrays], core_ids=[0])
    return r.results[0]["out_0_dram"]
```
